# Optimizing a Trainium2 kernel written in Bass

```python
import numpy as np
import jax
import jax.numpy as jnp

def _softmax(x, axis=-1):
    return jax.nn.softmax(x, axis=axis)

def _gelu(x):
    return jax.nn.gelu(x, approximate=True)

def _silu(x):
    return jax.nn.silu(x)

def _sigmoid(x):
    return jax.nn.sigmoid(x)

def _layernorm(x, axis=-1, eps=1e-05):
    m = jnp.mean(x, axis=axis, keepdims=True)
    v = jnp.var(x, axis=axis, keepdims=True)
    return (x - m) / jnp.sqrt(v + eps)

def _scatter_add(tgt, idx, src, axis=0):
    return tgt.at[idx].add(src)

def _segment_sum(src, seg, n):
    return jax.ops.segment_sum(src, seg, n)
kernel_name = 'mk_lm_tower_d2_tok_ids1024_r4_42d55e'

def setup_inputs(seed: int=0):
    np.random.seed(seed)
    _w = jnp.asarray

    def _rec_inputs():
        import jax
        import jax.numpy as jnp
        _rk = jax.random.key(seed)
        x = jax.random.randint(jax.random.fold_in(_rk, 1), (16, 128), 0, 12564, jnp.int32)
        return x
    x = _rec_inputs()

    def _L0_tok_setup():
        import jax, jax.numpy as jnp
        import numpy as np
        B, T, D, INNER, N, V, L, P = (4, 1024, 256, 512, 64, 50257, 4, 5000)
        DECAY, INP = (0.95, 0.05)

        def _silu(x):
            return x * jax.nn.sigmoid(x)

        def _layer(x, W_in_l, cw, cb, WB, WC, Dv, Wo, g, b):
            xp = x @ W_in_l.T
            x_in, x_gate = jnp.split(xp, 2, axis=-1)
            xc = jnp.transpose(x_in, (0, 2, 1))
            xc = jnp.pad(xc, ((0, 0), (0, 0), (3, 0)))
            xc = jax.lax.conv_general_dilated(xc, cw, window_strides=(1,), padding='VALID', dimension_numbers=('NCH', 'OIH', 'NCH'), feature_group_count=INNER)
            xc = xc + cb[None, :, None]
            u = _silu(jnp.transpose(xc, (0, 2, 1)))
            Bu = u @ WB.T

            def step(h, bu):
                h = DECAY * h + INP * bu
                return (h, h)
            h0 = jnp.zeros((x.shape[0], Bu.shape[-1]), x.dtype)
            _, hs = jax.lax.scan(step, h0, jnp.swapaxes(Bu, 0, 1))
            hs = jnp.swapaxes(hs, 0, 1)
            y = hs @ WC.T + Dv * u
            y = y * _silu(x_gate)
            y = y @ Wo.T
            z = y + x
            mu = jnp.mean(z, axis=-1, keepdims=True)
            var = jnp.var(z, axis=-1, keepdims=True)
            return (z - mu) * jax.lax.rsqrt(var + 1e-05) * g + b
        key = jax.random.key(seed)
        ks = jax.random.split(key, 10)
        s = 0.02
        return {'tokens': jax.random.randint(ks[0], (B, T), 0, V), 'tok_emb': jax.random.normal(ks[1], (V, D), jnp.float32) * s, 'pos_emb': jax.random.normal(ks[2], (P, D), jnp.float32) * s, 'W_in': jax.random.normal(ks[3], (L, 2 * INNER, D), jnp.float32) * s, 'conv_w': jax.random.normal(ks[4], (L, INNER, 1, 4), jnp.float32) * s, 'conv_b': jnp.zeros((L, INNER), jnp.float32), 'W_B': jax.random.normal(ks[5], (L, N, INNER), jnp.float32) * s, 'W_C': jax.random.normal(ks[6], (L, INNER, N), jnp.float32) * s, 'D_vec': jax.random.normal(ks[7], (L, INNER), jnp.float32) * s, 'W_out': jax.random.normal(ks[8], (L, D, INNER), jnp.float32) * s, 'ln_g': jnp.ones((L, D), jnp.float32), 'ln_b': jnp.zeros((L, D), jnp.float32)}
    _L0_tok_all = _L0_tok_setup()
    _L0_tok_in = {k: v for k, v in _L0_tok_all.items() if k in ('tok_emb', 'pos_emb', 'W_in', 'conv_w', 'conv_b', 'W_B', 'W_C', 'D_vec', 'W_out', 'ln_g', 'ln_b')}
    del _L0_tok_all

    def _L0_attn_setup():
        import jax, jax.numpy as jnp
        import numpy as np
        DIM = 256
        HEADS = 16
        DIM_HEAD = 64
        INNER = HEADS * DIM_HEAD
        HALF = DIM_HEAD // 2
        SCALE = DIM_HEAD ** (-0.5)

        def _apply_rope(x):
            n = x.shape[-2]
            theta = 1.0 / 10000.0 ** (jnp.arange(HALF, dtype=jnp.float32) / HALF)
            angles = jnp.arange(n, dtype=x.dtype)[:, None] * theta[None, :]
            cos = jnp.cos(angles)[None, None]
            sin = jnp.sin(angles)[None, None]
            x1, x2 = (x[..., :HALF], x[..., HALF:])
            return jnp.concatenate([x1 * cos - x2 * sin, x1 * sin + x2 * cos], axis=-1)
        key = jax.random.key(seed)
        k1, k2, k3, k4 = jax.random.split(key, 4)
        x = jax.random.normal(k1, (2, 512, DIM), dtype=jnp.float32)
        w_qkv = jax.random.normal(k2, (DIM, 3 * INNER), dtype=jnp.float32) * DIM ** (-0.5)
        w_out = jax.random.normal(k3, (INNER, DIM), dtype=jnp.float32) * INNER ** (-0.5)
        b_out = jax.random.normal(k4, (DIM,), dtype=jnp.float32) * 0.02
        return {'x': x, 'w_qkv': w_qkv, 'w_out': w_out, 'b_out': b_out}
    _L0_attn_all = _L0_attn_setup()
    _L0_attn_in = {k: v for k, v in _L0_attn_all.items() if k in ('w_qkv', 'w_out', 'b_out')}
    del _L0_attn_all

    def _L0_ffn_setup():
        import jax, jax.numpy as jnp
        import numpy as np
        D_MODEL = 256
        NHEAD = 16
        HEAD_DIM = D_MODEL // NHEAD
        FF = 512
        NUM_EXPERTS = 8
        EPS = 1e-05

        def _ln(x, g, b):
            m = x.mean(-1, keepdims=True)
            v = ((x - m) ** 2).mean(-1, keepdims=True)
            return (x - m) / jnp.sqrt(v + EPS) * g + b

        def _attention(src, Wq, bq, Wk, bk, Wv, bv, Wo, bo):
            B, T, d = src.shape
            scale = HEAD_DIM ** (-0.5)
            q = (src @ Wq + bq).reshape(B, T, NHEAD, HEAD_DIM)
            k = (src @ Wk + bk).reshape(B, T, NHEAD, HEAD_DIM)
            v = (src @ Wv + bv).reshape(B, T, NHEAD, HEAD_DIM)
            scores = jnp.einsum('bqhd,bkhd->bhqk', q, k) * scale
            probs = jax.nn.softmax(scores, axis=-1)
            out = jnp.einsum('bhqk,bkhd->bqhd', probs, v).reshape(B, T, d)
            return out @ Wo + bo

        def _moe(x, gW, gb, W1, b1, W2, b2):
            B, T, d = x.shape
            xf = x.reshape(-1, d)
            gates = jax.nn.softmax(xf @ gW + gb, axis=-1)
            top2_scores, top2_idx = jax.lax.top_k(gates, 2)
            w = (jax.nn.one_hot(top2_idx, NUM_EXPERTS, dtype=xf.dtype) * top2_scores[..., None]).sum(1)
            h = jax.nn.relu(jnp.einsum('nd,edf->enf', xf, W1) + b1[:, None, :])
            y = jnp.einsum('enf,efd->end', h, W2) + b2[:, None, :]
            out = jnp.einsum('ne,end->nd', w, y)
            return out.reshape(B, T, d)
        key = jax.random.key(seed)
        ks = jax.random.split(key, 12)
        s = 0.02
        d, f, E = (D_MODEL, FF, NUM_EXPERTS)
        return {'src': jax.random.normal(ks[0], (8, 128, d), dtype=jnp.float32), 'Wq': jax.random.normal(ks[1], (d, d), dtype=jnp.float32) * s, 'bq': jnp.zeros((d,), jnp.float32), 'Wk': jax.random.normal(ks[2], (d, d), dtype=jnp.float32) * s, 'bk': jnp.zeros((d,), jnp.float32), 'Wv': jax.random.normal(ks[3], (d, d), dtype=jnp.float32) * s, 'bv': jnp.zeros((d,), jnp.float32), 'Wo': jax.random.normal(ks[4], (d, d), dtype=jnp.float32) * s, 'bo': jnp.zeros((d,), jnp.float32), 'gW': jax.random.normal(ks[5], (d, E), dtype=jnp.float32) * s, 'gb': jnp.zeros((E,), jnp.float32), 'W1': jax.random.normal(ks[6], (E, d, f), dtype=jnp.float32) * s, 'b1': jnp.zeros((E, f), jnp.float32), 'W2': jax.random.normal(ks[7], (E, f, d), dtype=jnp.float32) * s, 'b2': jnp.zeros((E, d), jnp.float32), 'ln1_g': jnp.ones((d,), jnp.float32), 'ln1_b': jnp.zeros((d,), jnp.float32), 'ln2_g': jnp.ones((d,), jnp.float32), 'ln2_b': jnp.zeros((d,), jnp.float32)}
    _L0_ffn_all = _L0_ffn_setup()
    _L0_ffn_in = {k: v for k, v in _L0_ffn_all.items() if k in ('Wq', 'bq', 'Wk', 'bk', 'Wv', 'bv', 'Wo', 'bo', 'gW', 'gb', 'W1', 'b1', 'W2', 'b2', 'ln1_g', 'ln1_b', 'ln2_g', 'ln2_b')}
    del _L0_ffn_all

    def _L1_attn_setup():
        import jax, jax.numpy as jnp
        import numpy as np
        N_HEADS = 16
        BLOCK_SIZE = 64

        def _rope(x):
            B, H, L, d = x.shape
            inv_freq = 1.0 / 10000.0 ** (jnp.arange(0, d, 2, dtype=jnp.float32) / d)
            t = jnp.arange(L, dtype=jnp.float32)[:, None] * inv_freq[None, :]
            cos, sin = (jnp.cos(t), jnp.sin(t))
            x1, x2 = (x[..., 0::2], x[..., 1::2])
            return jnp.concatenate([x1 * cos - x2 * sin, x2 * cos + x1 * sin], axis=-1)
        key = jax.random.key(seed)
        k1, k2, k3 = jax.random.split(key, 3)
        B, L, D = (2, 1024, 256)
        x = jax.random.normal(k1, (B, L, D), dtype=jnp.float32)
        Wqkv = jax.random.normal(k2, (3 * D, D), dtype=jnp.float32) * 0.02
        Wout = jax.random.normal(k3, (D, D), dtype=jnp.float32) * 0.02
        return {'x': x, 'Wqkv': Wqkv, 'Wout': Wout}
    _L1_attn_all = _L1_attn_setup()
    _L1_attn_in = {k: v for k, v in _L1_attn_all.items() if k in ('Wqkv', 'Wout')}
    del _L1_attn_all

    def _L1_ffn_setup():
        import jax, jax.numpy as jnp
        import numpy as np
        B, S, D = (1, 512, 256)
        E, F = (16, 256)
        NG, TKG, K = (4, 2, 4)
        NSH = 2
        SCALE = 2.5
        STD = 0.02
        EPG = E // NG

        def _route(x_flat, router_w, bias):
            logits = x_flat.astype(jnp.float32) @ router_w.T
            scores = jax.nn.sigmoid(logits)
            s = scores + bias[None, :]
            sg = s.reshape(-1, NG, EPG)
            group_score = jax.lax.top_k(sg, 2)[0].sum(-1)
            gidx = jax.lax.top_k(group_score, TKG)[1]
            gmask = jnp.sum(jax.nn.one_hot(gidx, NG, dtype=jnp.float32), axis=1) > 0
            emask = jnp.repeat(gmask, EPG, axis=1)
            masked = jnp.where(emask, s, -1.0)
            topk_idx = jax.lax.top_k(masked, K)[1]
            tw = jnp.take_along_axis(scores, topk_idx, axis=1)
            tw = tw / (tw.sum(-1, keepdims=True) + 1e-20)
            tw = tw * SCALE
            return (topk_idx, tw)
        key = jax.random.key(seed)
        ks = jax.random.split(key, 8)
        return {'hidden_states': jax.random.normal(ks[0], (B, S, D), jnp.float32), 'router_w': jax.random.normal(ks[1], (E, D), jnp.float32) * STD, 'bias': jnp.zeros((E,), jnp.float32), 'gate_w': jax.random.normal(ks[2], (E, D, F), jnp.float32) * STD, 'up_w': jax.random.normal(ks[3], (E, D, F), jnp.float32) * STD, 'down_w': jax.random.normal(ks[4], (E, F, D), jnp.float32) * STD, 'sh_gate_w': jax.random.normal(ks[5], (D, NSH * F), jnp.float32) * STD, 'sh_up_w': jax.random.normal(ks[6], (D, NSH * F), jnp.float32) * STD, 'sh_down_w': jax.random.normal(ks[7], (NSH * F, D), jnp.float32) * STD}
    _L1_ffn_all = _L1_ffn_setup()
    _L1_ffn_in = {k: v for k, v in _L1_ffn_all.items() if k in ('router_w', 'bias', 'gate_w', 'up_w', 'down_w', 'sh_gate_w', 'sh_up_w', 'sh_down_w')}
    del _L1_ffn_all
    return {'x': x, 'L0_tok_tok_emb': _L0_tok_in['tok_emb'], 'L0_tok_pos_emb': _L0_tok_in['pos_emb'], 'L0_tok_W_in': _L0_tok_in['W_in'], 'L0_tok_conv_w': _L0_tok_in['conv_w'], 'L0_tok_conv_b': _L0_tok_in['conv_b'], 'L0_tok_W_B': _L0_tok_in['W_B'], 'L0_tok_W_C': _L0_tok_in['W_C'], 'L0_tok_D_vec': _L0_tok_in['D_vec'], 'L0_tok_W_out': _L0_tok_in['W_out'], 'L0_tok_ln_g': _L0_tok_in['ln_g'], 'L0_tok_ln_b': _L0_tok_in['ln_b'], 'L0_attn_w_qkv': _L0_attn_in['w_qkv'], 'L0_attn_w_out': _L0_attn_in['w_out'], 'L0_attn_b_out': _L0_attn_in['b_out'], 'L0_ffn_Wq': _L0_ffn_in['Wq'], 'L0_ffn_bq': _L0_ffn_in['bq'], 'L0_ffn_Wk': _L0_ffn_in['Wk'], 'L0_ffn_bk': _L0_ffn_in['bk'], 'L0_ffn_Wv': _L0_ffn_in['Wv'], 'L0_ffn_bv': _L0_ffn_in['bv'], 'L0_ffn_Wo': _L0_ffn_in['Wo'], 'L0_ffn_bo': _L0_ffn_in['bo'], 'L0_ffn_gW': _L0_ffn_in['gW'], 'L0_ffn_gb': _L0_ffn_in['gb'], 'L0_ffn_W1': _L0_ffn_in['W1'], 'L0_ffn_b1': _L0_ffn_in['b1'], 'L0_ffn_W2': _L0_ffn_in['W2'], 'L0_ffn_b2': _L0_ffn_in['b2'], 'L0_ffn_ln1_g': _L0_ffn_in['ln1_g'], 'L0_ffn_ln1_b': _L0_ffn_in['ln1_b'], 'L0_ffn_ln2_g': _L0_ffn_in['ln2_g'], 'L0_ffn_ln2_b': _L0_ffn_in['ln2_b'], 'L1_attn_Wqkv': _L1_attn_in['Wqkv'], 'L1_attn_Wout': _L1_attn_in['Wout'], 'L1_ffn_router_w': _L1_ffn_in['router_w'], 'L1_ffn_bias': _L1_ffn_in['bias'], 'L1_ffn_gate_w': _L1_ffn_in['gate_w'], 'L1_ffn_up_w': _L1_ffn_in['up_w'], 'L1_ffn_down_w': _L1_ffn_in['down_w'], 'L1_ffn_sh_gate_w': _L1_ffn_in['sh_gate_w'], 'L1_ffn_sh_up_w': _L1_ffn_in['sh_up_w'], 'L1_ffn_sh_down_w': _L1_ffn_in['sh_down_w']}

def reference(x, L0_tok_tok_emb, L0_tok_pos_emb, L0_tok_W_in, L0_tok_conv_w, L0_tok_conv_b, L0_tok_W_B, L0_tok_W_C, L0_tok_D_vec, L0_tok_W_out, L0_tok_ln_g, L0_tok_ln_b, L0_attn_w_qkv, L0_attn_w_out, L0_attn_b_out, L0_ffn_Wq, L0_ffn_bq, L0_ffn_Wk, L0_ffn_bk, L0_ffn_Wv, L0_ffn_bv, L0_ffn_Wo, L0_ffn_bo, L0_ffn_gW, L0_ffn_gb, L0_ffn_W1, L0_ffn_b1, L0_ffn_W2, L0_ffn_b2, L0_ffn_ln1_g, L0_ffn_ln1_b, L0_ffn_ln2_g, L0_ffn_ln2_b, L1_attn_Wqkv, L1_attn_Wout, L1_ffn_router_w, L1_ffn_bias, L1_ffn_gate_w, L1_ffn_up_w, L1_ffn_down_w, L1_ffn_sh_gate_w, L1_ffn_sh_up_w, L1_ffn_sh_down_w):
    import jax
    import jax.numpy as jnp

    def _L0_tok_ref(tokens, tok_emb, pos_emb, W_in, conv_w, conv_b, W_B, W_C, D_vec, W_out, ln_g, ln_b):
        import jax, jax.numpy as jnp
        import numpy as np
        B, T, D, INNER, N, V, L, P = (4, 1024, 256, 512, 64, 50257, 4, 5000)
        DECAY, INP = (0.95, 0.05)

        def _silu(x):
            return x * jax.nn.sigmoid(x)

        def _layer(x, W_in_l, cw, cb, WB, WC, Dv, Wo, g, b):
            xp = x @ W_in_l.T
            x_in, x_gate = jnp.split(xp, 2, axis=-1)
            xc = jnp.transpose(x_in, (0, 2, 1))
            xc = jnp.pad(xc, ((0, 0), (0, 0), (3, 0)))
            xc = jax.lax.conv_general_dilated(xc, cw, window_strides=(1,), padding='VALID', dimension_numbers=('NCH', 'OIH', 'NCH'), feature_group_count=INNER)
            xc = xc + cb[None, :, None]
            u = _silu(jnp.transpose(xc, (0, 2, 1)))
            Bu = u @ WB.T

            def step(h, bu):
                h = DECAY * h + INP * bu
                return (h, h)
            h0 = jnp.zeros((x.shape[0], Bu.shape[-1]), x.dtype)
            _, hs = jax.lax.scan(step, h0, jnp.swapaxes(Bu, 0, 1))
            hs = jnp.swapaxes(hs, 0, 1)
            y = hs @ WC.T + Dv * u
            y = y * _silu(x_gate)
            y = y @ Wo.T
            z = y + x
            mu = jnp.mean(z, axis=-1, keepdims=True)
            var = jnp.var(z, axis=-1, keepdims=True)
            return (z - mu) * jax.lax.rsqrt(var + 1e-05) * g + b
        x = tok_emb[tokens] + pos_emb[jnp.arange(tokens.shape[1])][None]
        for l in range(L):
            x = _layer(x, W_in[l], conv_w[l], conv_b[l], W_B[l], W_C[l], D_vec[l], W_out[l], ln_g[l], ln_b[l])
        return x

    def _L0_attn_ref(x, w_qkv, w_out, b_out):
        import jax, jax.numpy as jnp
        import numpy as np
        DIM = 256
        HEADS = 16
        DIM_HEAD = 64
        INNER = HEADS * DIM_HEAD
        HALF = DIM_HEAD // 2
        SCALE = DIM_HEAD ** (-0.5)

        def _apply_rope(x):
            n = x.shape[-2]
            theta = 1.0 / 10000.0 ** (jnp.arange(HALF, dtype=jnp.float32) / HALF)
            angles = jnp.arange(n, dtype=x.dtype)[:, None] * theta[None, :]
            cos = jnp.cos(angles)[None, None]
            sin = jnp.sin(angles)[None, None]
            x1, x2 = (x[..., :HALF], x[..., HALF:])
            return jnp.concatenate([x1 * cos - x2 * sin, x1 * sin + x2 * cos], axis=-1)
        b, n, _ = x.shape
        qkv = x @ w_qkv
        qkv = qkv.reshape(b, n, 3, HEADS, DIM_HEAD)
        qkv = jnp.transpose(qkv, (2, 0, 3, 1, 4))
        q, k, v = (qkv[0], qkv[1], qkv[2])
        q = _apply_rope(q)
        k = _apply_rope(k)
        scores = jnp.einsum('bhnd,bhmd->bhnm', q, k) * SCALE
        attn = jax.nn.softmax(scores, axis=-1)
        out = jnp.einsum('bhnm,bhmd->bhnd', attn, v)
        out = jnp.transpose(out, (0, 2, 1, 3)).reshape(b, n, INNER)
        return out @ w_out + b_out

    def _L0_ffn_ref(src, Wq, bq, Wk, bk, Wv, bv, Wo, bo, gW, gb, W1, b1, W2, b2, ln1_g, ln1_b, ln2_g, ln2_b):
        import jax, jax.numpy as jnp
        import numpy as np
        D_MODEL = 256
        NHEAD = 16
        HEAD_DIM = D_MODEL // NHEAD
        FF = 512
        NUM_EXPERTS = 8
        EPS = 1e-05

        def _ln(x, g, b):
            m = x.mean(-1, keepdims=True)
            v = ((x - m) ** 2).mean(-1, keepdims=True)
            return (x - m) / jnp.sqrt(v + EPS) * g + b

        def _attention(src, Wq, bq, Wk, bk, Wv, bv, Wo, bo):
            B, T, d = src.shape
            scale = HEAD_DIM ** (-0.5)
            q = (src @ Wq + bq).reshape(B, T, NHEAD, HEAD_DIM)
            k = (src @ Wk + bk).reshape(B, T, NHEAD, HEAD_DIM)
            v = (src @ Wv + bv).reshape(B, T, NHEAD, HEAD_DIM)
            scores = jnp.einsum('bqhd,bkhd->bhqk', q, k) * scale
            probs = jax.nn.softmax(scores, axis=-1)
            out = jnp.einsum('bhqk,bkhd->bqhd', probs, v).reshape(B, T, d)
            return out @ Wo + bo

        def _moe(x, gW, gb, W1, b1, W2, b2):
            B, T, d = x.shape
            xf = x.reshape(-1, d)
            gates = jax.nn.softmax(xf @ gW + gb, axis=-1)
            top2_scores, top2_idx = jax.lax.top_k(gates, 2)
            w = (jax.nn.one_hot(top2_idx, NUM_EXPERTS, dtype=xf.dtype) * top2_scores[..., None]).sum(1)
            h = jax.nn.relu(jnp.einsum('nd,edf->enf', xf, W1) + b1[:, None, :])
            y = jnp.einsum('enf,efd->end', h, W2) + b2[:, None, :]
            out = jnp.einsum('ne,end->nd', w, y)
            return out.reshape(B, T, d)
        attn_out = _attention(src, Wq, bq, Wk, bk, Wv, bv, Wo, bo)
        x = _ln(src + attn_out, ln1_g, ln1_b)
        ff = _moe(x, gW, gb, W1, b1, W2, b2)
        return _ln(x + ff, ln2_g, ln2_b)

    def _L1_attn_ref(x, Wqkv, Wout):
        import jax, jax.numpy as jnp
        import numpy as np
        N_HEADS = 16
        BLOCK_SIZE = 64

        def _rope(x):
            B, H, L, d = x.shape
            inv_freq = 1.0 / 10000.0 ** (jnp.arange(0, d, 2, dtype=jnp.float32) / d)
            t = jnp.arange(L, dtype=jnp.float32)[:, None] * inv_freq[None, :]
            cos, sin = (jnp.cos(t), jnp.sin(t))
            x1, x2 = (x[..., 0::2], x[..., 1::2])
            return jnp.concatenate([x1 * cos - x2 * sin, x2 * cos + x1 * sin], axis=-1)
        H, BS = (N_HEADS, BLOCK_SIZE)
        B, L, D = x.shape
        HD = D // H
        scale = HD ** (-0.5)
        nb = L // BS
        qkv = (x @ Wqkv.T).reshape(B, L, 3, H, HD).transpose(2, 0, 3, 1, 4)
        q, k, v = (qkv[0], qkv[1], qkv[2])
        q, k = (_rope(q), _rope(k))
        qb = q.reshape(B, H, nb, BS, HD)
        kb = k.reshape(B, H, nb, BS, HD)
        vb = v.reshape(B, H, nb, BS, HD)
        att = jnp.einsum('bhnqd,bhnkd->bhnqk', qb, kb) * scale
        causal = jnp.tril(jnp.ones((BS, BS), dtype=bool))
        att = jnp.where(causal, att, jnp.finfo(att.dtype).min)
        att = jax.nn.softmax(att, axis=-1)
        out = jnp.einsum('bhnqk,bhnkd->bhnqd', att, vb)
        out = out.reshape(B, H, L, HD).transpose(0, 2, 1, 3).reshape(B, L, D)
        return out @ Wout.T

    def _L1_ffn_ref(hidden_states, router_w, bias, gate_w, up_w, down_w, sh_gate_w, sh_up_w, sh_down_w):
        import jax, jax.numpy as jnp
        import numpy as np
        B, S, D = (1, 512, 256)
        E, F = (16, 256)
        NG, TKG, K = (4, 2, 4)
        NSH = 2
        SCALE = 2.5
        STD = 0.02
        EPG = E // NG

        def _route(x_flat, router_w, bias):
            logits = x_flat.astype(jnp.float32) @ router_w.T
            scores = jax.nn.sigmoid(logits)
            s = scores + bias[None, :]
            sg = s.reshape(-1, NG, EPG)
            group_score = jax.lax.top_k(sg, 2)[0].sum(-1)
            gidx = jax.lax.top_k(group_score, TKG)[1]
            gmask = jnp.sum(jax.nn.one_hot(gidx, NG, dtype=jnp.float32), axis=1) > 0
            emask = jnp.repeat(gmask, EPG, axis=1)
            masked = jnp.where(emask, s, -1.0)
            topk_idx = jax.lax.top_k(masked, K)[1]
            tw = jnp.take_along_axis(scores, topk_idx, axis=1)
            tw = tw / (tw.sum(-1, keepdims=True) + 1e-20)
            tw = tw * SCALE
            return (topk_idx, tw)
        x = hidden_states.reshape(-1, D)
        topk_idx, tw = _route(x, router_w, bias)
        combine = (jax.nn.one_hot(topk_idx, E, dtype=tw.dtype) * tw[..., None]).sum(1)
        h = jnp.einsum('td,edf->etf', x, gate_w)
        u = jnp.einsum('td,edf->etf', x, up_w)
        y = jnp.einsum('etf,efd->etd', jax.nn.silu(h) * u, down_w)
        routed = jnp.einsum('etd,te->td', y, combine)
        sh = jax.nn.silu(x @ sh_gate_w) * (x @ sh_up_w) @ sh_down_w
        return (routed + sh).reshape(hidden_states.shape)
    h = _L0_tok_ref(x, L0_tok_tok_emb, L0_tok_pos_emb, L0_tok_W_in, L0_tok_conv_w, L0_tok_conv_b, L0_tok_W_B, L0_tok_W_C, L0_tok_D_vec, L0_tok_W_out, L0_tok_ln_g, L0_tok_ln_b)
    h = h + _L0_attn_ref(_layernorm(h, axis=-1), L0_attn_w_qkv, L0_attn_w_out, L0_attn_b_out)
    h = h + _L0_ffn_ref(_layernorm(h, axis=-1), L0_ffn_Wq, L0_ffn_bq, L0_ffn_Wk, L0_ffn_bk, L0_ffn_Wv, L0_ffn_bv, L0_ffn_Wo, L0_ffn_bo, L0_ffn_gW, L0_ffn_gb, L0_ffn_W1, L0_ffn_b1, L0_ffn_W2, L0_ffn_b2, L0_ffn_ln1_g, L0_ffn_ln1_b, L0_ffn_ln2_g, L0_ffn_ln2_b)
    h = h + _L1_attn_ref(_layernorm(h, axis=-1), L1_attn_Wqkv, L1_attn_Wout)
    h = h + _L1_ffn_ref(_layernorm(h, axis=-1), L1_ffn_router_w, L1_ffn_bias, L1_ffn_gate_w, L1_ffn_up_w, L1_ffn_down_w, L1_ffn_sh_gate_w, L1_ffn_sh_up_w, L1_ffn_sh_down_w)
    return h

_drawn_inputs = setup_inputs


def setup_inputs(seed=0):
    import zlib

    import numpy as np

    out = dict(_drawn_inputs(seed))
    spreads = {'L0_tok_conv_b': (0.0, 0.8),
     'L0_tok_ln_g': (1.0, 0.2),
     'L0_tok_ln_b': (0.0, 0.1),
     'L0_ffn_bq': (0.0, 0.8),
     'L0_ffn_bk': (0.0, 0.8),
     'L0_ffn_bv': (0.0, 0.551),
     'L0_ffn_bo': (0.0, 0.1),
     'L0_ffn_gb': (0.0, 0.8),
     'L0_ffn_b1': (0.0, 0.8),
     'L0_ffn_b2': (0.0, 0.682),
     'L0_ffn_ln1_g': (1.0, 0.2),
     'L0_ffn_ln1_b': (0.0, 0.1),
     'L0_ffn_ln2_g': (1.0, 0.2),
     'L0_ffn_ln2_b': (0.0, 0.1),
     'L1_ffn_bias': (0.0, 0.8)}
    factors = {'L0_tok_W_in': 8.0,
     'L0_tok_conv_w': 8.0,
     'L0_tok_W_B': 8.0,
     'L0_tok_W_C': 8.0,
     'L0_tok_D_vec': 8.0,
     'L0_tok_W_out': 8.0,
     'L0_attn_b_out': 3.313,
     'L0_ffn_Wq': 8.0,
     'L0_ffn_Wk': 8.0,
     'L0_ffn_Wv': 3.571,
     'L0_ffn_gW': 3.558,
     'L0_ffn_W1': 5.286,
     'L0_ffn_W2': 4.199,
     'L1_attn_Wqkv': 2.884,
     'L1_attn_Wout': 2.81,
     'L1_ffn_router_w': 8.0,
     'L1_ffn_gate_w': 5.616,
     'L1_ffn_up_w': 5.529,
     'L1_ffn_down_w': 5.518,
     'L1_ffn_sh_gate_w': 4.954,
     'L1_ffn_sh_up_w': 4.87,
     'L1_ffn_sh_down_w': 4.884}
    for name, (base, spread) in spreads.items():
        noise = np.random.default_rng([zlib.crc32(name.encode()), seed]).standard_normal(out[name].shape)
        drawn = base * np.exp(spread * noise) if base else spread * noise
        out[name] = jnp.asarray(drawn.astype(out[name].dtype))
    for name, factor in factors.items():
        out[name] = (out[name] * factor).astype(out[name].dtype)
    return out
```

```python
from contextlib import ExitStack

import concourse.bass as bass
from concourse import mybir

F32 = mybir.dt.float32
I32 = mybir.dt.int32
U32 = mybir.dt.uint32
ALU = mybir.AluOpType
ACT = mybir.ActivationFunctionType
AX_X = mybir.AxisListType.X

P = 128
SEQS = 16
TOK = 128
D = 256
KD = D // P
GROUPS = 4
TPG = SEQS // GROUPS
GT = TPG * TOK
LAYERS = 4
INNER = 512
KI = INNER // P
STATE = 64
TAPS = 4
DECAY, INP = 0.95, 0.05
EPS = 1e-5
HEADS = 16
BANK = 512


def after(eng, sem, count):
    if isinstance(count, int) and count <= 0:
        return
    eng.wait_ge(sem, count)


def at(i):
    return slice(i, i + 1) if isinstance(i, int) else bass.ds(i, 1)


class Kit:

    def __init__(self, nc, sems):
        self.nc, self.sems, self.mem = nc, sems, ExitStack()

    def sem(self, name):
        return self.sems.enter_context(self.nc.semaphore(name))

    def sb(self, name, shape, dt=F32):
        return self.mem.enter_context(self.nc.sbuf_tensor(name, shape, dt))

    def ps(self, name, shape):
        return self.mem.enter_context(self.nc.psum_tensor(name, shape, F32))


def token_stage(nc, sems, io, res, ident, eps):
    k = Kit(nc, sems)
    with k.mem:
        ids = k.sb("ids", [P, SEQS], I32)
        pos = k.sb("pos", [P, D])
        xT = k.sb("tok_xT", [P, KD, SEQS * TOK])
        w_in = k.sb("w_in", [P, KD, 2 * INNER])
        w_b = k.sb("w_b", [P, KI, STATE])
        w_c = k.sb("w_c", [STATE, INNER])
        w_o = k.sb("w_o", [P, KI, D])
        conv_w = k.sb("conv_w", [P, LAYERS, KI, TAPS])
        conv_b = k.sb("conv_b", [P, LAYERS, KI])
        d_vec = k.sb("d_vec", [P, LAYERS, KI])
        ln_g = k.sb("tok_ln_g", [P, LAYERS, D])
        ln_b = k.sb("tok_ln_b", [P, LAYERS, D])
        gain = k.sb("gain", [P, 2, D])
        decay = k.sb("decay", [STATE, GT])
        u = k.sb("u", [P, 2, KI, GT])
        gate = k.sb("gate", [P, 2, KI, GT])
        y = k.sb("y", [P, 2, KI, GT])
        bu = k.sb("bu", [STATE, GT])
        state = k.sb("state", [STATE, GT])
        z = k.sb("tok_z", [P, TPG, D])
        stats = k.sb("tok_stats", [P, TPG, 6])
        mv = k.sb("tok_mv", [P, TPG, 2])
        std = k.sb("tok_std", [P, TPG])
        rstd = k.sb("tok_rstd", [P, TPG])
        xp_ps = k.ps("xp_ps", [P, 2, BANK])
        b_ps = k.ps("b_ps", [P, BANK])
        c_ps = k.ps("c_ps", [P, 2, BANK])
        d_ps = k.ps("d_ps", [P, 2, BANK])
        t_ps = k.ps("t_ps", [P, BANK])

        ids_in, consts_in, w_in_in, w_rest_in, gathered = (
            k.sem(n) for n in ("ids_in", "tok_consts_in", "w_in_in", "w_rest_in", "gathered"))
        xp_full, conv_done, gate_done, u_ready = (k.sem(n) for n in ("xp_full", "conv_done", "gate_done", "u_ready"))
        bu_full, bu_ready, scan_done = (k.sem(n) for n in ("bu_full", "bu_ready", "scan_done"))
        c_full, comb_done, y_ready = (k.sem(n) for n in ("c_full", "comb_done", "y_ready"))
        d_full, z_done, var_ready, std_ready, xn_ready = (
            k.sem(n) for n in ("d_full", "z_done", "tok_var_ready", "tok_std_ready", "tok_xn_ready"))
        res_ready, t_full, xT_ready = (k.sem(n) for n in ("res_ready", "tok_t_full", "tok_xT_ready"))
        CONSTS = 7

        def unit(l, g, back):
            lay, grp = l + (g - back) // GROUPS, (g - back) % GROUPS
            if isinstance(lay, int) and not 0 <= lay < LAYERS:
                return None
            return lay * GROUPS + grp, lay, grp

        def run(eng, step):
            for g in range(GROUPS):
                step(0, g)
            with eng.Fori(1, LAYERS) as l:
                for g in range(GROUPS):
                    step(l, g)
            step(LAYERS, 0)
            step(LAYERS, 1)

        block = k.mem.enter_context(nc.Block())

        @block.sync
        def _(sp):
            sp.dma_start(ids[:], io["ids"]).then_inc(ids_in, 16)
            sp.dma_start(pos[:], io["pos"]).then_inc(consts_in, 16)
            sp.dma_start(w_in[:], io["w_in"][0]).then_inc(w_in_in, 16)
            sp.dma_start(conv_w[:], io["conv_w"]).then_inc(consts_in, 16)
            sp.dma_start(conv_b[:], io["conv_b"]).then_inc(consts_in, 16)
            sp.dma_start(w_b[:], io["w_b"][0]).then_inc(w_rest_in, 16)
            sp.dma_start(w_c[:], io["w_c"][0]).then_inc(w_rest_in, 16)
            sp.dma_start(w_o[:], io["w_o"][0]).then_inc(w_rest_in, 16)
            sp.dma_start(d_vec[:], io["d_vec"]).then_inc(consts_in, 16)
            sp.dma_start(decay[:], io["decay"]).then_inc(consts_in, 16)
            sp.dma_start(ln_g[:], io["tok_ln_g"].unsqueeze(0).to_broadcast([P, LAYERS, D])).then_inc(consts_in, 16)
            sp.dma_start(ln_b[:], io["tok_ln_b"].unsqueeze(0).to_broadcast([P, LAYERS, D])).then_inc(consts_in, 16)
            with sp.Fori(1, LAYERS) as l:
                sp.wait_ge(xp_full, l * GROUPS * 2 * KI)
                sp.dma_start(w_in[:], io["w_in"][at(l)].rearrange("l p k n -> (l p) k n")).then_inc(w_in_in, 16)
                sp.wait_ge(d_full, l * GROUPS * 2)
                sp.dma_start(w_b[:], io["w_b"][at(l)].rearrange("l p k n -> (l p) k n")).then_inc(w_rest_in, 16)
                sp.dma_start(w_c[:], io["w_c"][at(l)].rearrange("l p n -> (l p) n")).then_inc(w_rest_in, 16)
                sp.dma_start(w_o[:], io["w_o"][at(l)].rearrange("l p k n -> (l p) k n")).then_inc(w_rest_in, 16)

        @block.gpsimd
        def _(pool):
            pool.wait_ge(ids_in, 16)
            for t in range(SEQS):
                pool.indirect_dma_start(res[:, t, :], None, io["emb"], bass.IndirectOffsetOnAxis(
                    ap=ids[:, t:t + 1].bitcast(U32), axis=0)).then_inc(gathered, 16)
            pool.wait_ge(consts_in, 16 * CONSTS)
            pool.wait_ge(gathered, 16 * SEQS)
            for g in range(GROUPS):
                rows = res[:, g * TPG:(g + 1) * TPG, :]
                pool.tensor_tensor(rows, rows, pos[:].unsqueeze(1).to_broadcast([P, TPG, D]),
                                   ALU.add).then_inc(res_ready, 1)

            def step(l, g):
                fin, mid = unit(l, g, 2), unit(l, g, 1)
                if fin:
                    n, lay, grp = fin
                    rows = res[:, grp * TPG:(grp + 1) * TPG, :]
                    pool.drain()
                    if grp == 0:
                        pool.tensor_copy(gain[:, 0:1, :], ln_g[:, at(lay), :])
                        pool.tensor_copy(gain[:, 1:2, :], ln_b[:, at(lay), :])
                        pool.drain()
                    after(pool, xn_ready, n + 1)
                    pool.tensor_tensor(rows, z[:], gain[:, 0:1, :].to_broadcast([P, TPG, D]), ALU.mult)
                    pool.drain()
                    pool.tensor_tensor(rows, rows, gain[:, 1:2, :].to_broadcast([P, TPG, D]),
                                       ALU.add).then_inc(res_ready, 1)
                if mid:
                    n, lay, grp = mid
                    after(pool, gate_done, n * KI + KI)
                    for c in range(KI):
                        after(pool, comb_done, n * KI + c + 1)
                        pool.tensor_tensor(y[:, grp % 2, c, :], y[:, grp % 2, c, :], gate[:, grp % 2, c, :],
                                           ALU.mult).then_inc(y_ready, 1)

            run(pool, step)

        @block.scalar
        def _(act):
            def turn_back(n, grp):
                for kc in range(KD):
                    after(act, t_full, n * KD + kc + 1)
                    act.activation(xT[:, kc, grp * GT:(grp + 1) * GT], t_ps[:], ACT.Copy).then_inc(xT_ready, 1)

            for g in range(GROUPS):
                turn_back(g, g)

            def step(l, g):
                new, mid, fin = unit(l, g, 0), unit(l, g, 1), unit(l, g, 2)
                if mid:
                    n = mid[0]
                    after(act, bu_full, n + 1)
                    after(act, scan_done, n)
                    act.activation(bu[:], b_ps[0:STATE, :], ACT.Copy, scale=INP).then_inc(bu_ready, 1)
                if fin:
                    n = fin[0]
                    after(act, var_ready, n + 1)
                    act.activation(std[:], mv[:, :, 1], ACT.Sqrt, bias=eps[:, 0:1]).then_inc(std_ready, 1)
                if new:
                    n, lay, grp = new
                    for m in range(KI):
                        after(act, conv_done, n * KI + m + 1)
                        act.activation(u[:, grp % 2, m, :], u[:, grp % 2, m, :], ACT.Silu).then_inc(u_ready, 1)
                    after(act, y_ready, (n - 2) * KI + KI)
                    for m in range(KI):
                        after(act, xp_full, n * 2 * KI + KI + m + 1)
                        act.activation(gate[:, grp % 2, m, :], xp_ps[:, m % 2, :], ACT.Silu).then_inc(gate_done, 1)
                if fin:
                    turn_back(fin[0] + GROUPS, fin[2])

            run(act, step)

        @block.vector
        def _(dve):
            dve.wait_ge(consts_in, 16 * CONSTS)

            def conv(new, m):
                dve.drain()
                n, lay, grp = new
                after(dve, xp_full, n * 2 * KI + m + 1)
                acc = u[:, grp % 2, m, :].rearrange("p (s t) -> p s t", s=TPG)
                xin = xp_ps[:, m % 2, :].rearrange("p (s t) -> p s t", s=TPG)
                w = lambda tap: conv_w[:, at(lay), m, tap]
                dve.tensor_scalar(u[:, grp % 2, m, :], xp_ps[:, m % 2, :], w(TAPS - 1), conv_b[:, at(lay), m],
                                  ALU.mult, ALU.add)
                for back in range(1, TAPS):
                    dve.drain()
                    last = dve.scalar_tensor_tensor(acc[:, :, back:], xin[:, :, :TOK - back], w(TAPS - 1 - back),
                                                    acc[:, :, back:], ALU.mult, ALU.add)
                last.then_inc(conv_done, 1)

            def step(l, g):
                new, mid, fin = unit(l, g, 0), unit(l, g, 1), unit(l, g, 2)
                if new:
                    conv(new, 0)
                    conv(new, 1)
                if fin:
                    n, lay, grp = fin
                    for b in range(2):
                        dve.drain()
                        if b == 0:
                            after(dve, res_ready, GROUPS + n)
                        after(dve, d_full, n * 2 + b + 1)
                        dve.tensor_tensor(z[:, 2 * b:2 * b + 2, :], d_ps[:, b, :].rearrange("p (j d) -> p j d", j=2),
                                          res[:, grp * TPG + 2 * b:grp * TPG + 2 * b + 2, :],
                                          ALU.add).then_inc(z_done, 1)
                    dve.drain()
                    for j in range(TPG):
                        dve.bn_stats(stats[:, j, :], z[:, j, :])
                    dve.drain()
                    for j in range(TPG):
                        last = dve.bn_aggr(mv[:, j, :], stats[:, j, :])
                    last.then_inc(var_ready, 1)
                if mid:
                    n = mid[0]
                    dve.drain()
                    after(dve, bu_ready, n + 1)
                    dve.tensor_tensor_scan(state[:], decay[:], bu[:], 0.0, ALU.mult, ALU.add).then_inc(scan_done, 1)
                if new:
                    conv(new, 2)
                    conv(new, 3)
                if fin:
                    dve.drain()
                    n, lay, grp = fin
                    after(dve, std_ready, n + 1)
                    dve.reciprocal(rstd[:], std[:])
                    dve.drain()
                    for j in range(TPG):
                        last = dve.tensor_scalar(z[:, j, :], z[:, j, :], mv[:, j, 0:1], rstd[:, j:j + 1],
                                                 ALU.subtract, ALU.mult)
                    last.then_inc(xn_ready, 1)
                if mid:
                    n, lay, grp = mid
                    for c in range(KI):
                        dve.drain()
                        if c == 0:
                            after(dve, u_ready, n * KI + KI)
                        after(dve, c_full, n * KI + c + 1)
                        dve.scalar_tensor_tensor(y[:, grp % 2, c, :], u[:, grp % 2, c, :], d_vec[:, at(lay), c],
                                                 c_ps[:, c % 2, :], ALU.mult, ALU.add).then_inc(comb_done, 1)

            run(dve, step)

        @block.tensor
        def _(pe):
            def turn(n, grp, kc):
                after(pe, res_ready, n + 1)
                after(pe, xT_ready, n * KD + kc)
                for j in range(TPG):
                    last = pe.transpose(t_ps[:, j * TOK:(j + 1) * TOK],
                                        res[:, grp * TPG + j, kc * P:(kc + 1) * P], ident[:])
                last.then_inc(t_full, 1)

            for g in range(GROUPS):
                for kc in range(KD):
                    turn(g, g, kc)

            def project_in(new, m):
                n, lay, grp = new
                if m == 0:
                    after(pe, w_in_in, (lay + 1) * 16)
                    after(pe, xT_ready, (n + 1) * KD)
                if m < 2:
                    after(pe, gate_done, (n - 1) * KI + 2 + m + 1)
                elif m < KI + 2:
                    after(pe, conv_done, n * KI + m - 1)
                else:
                    after(pe, gate_done, n * KI + m - KI - 1)
                for kc in range(KD):
                    last = pe.matmul(xp_ps[:, m % 2, :], w_in[:, kc, m * P:(m + 1) * P],
                                     xT[:, kc, grp * GT:(grp + 1) * GT], start=(kc == 0), stop=(kc == KD - 1))
                last.then_inc(xp_full, 1)

            def mix(mid, cs):
                n, lay, grp = mid
                for c in cs:
                    after(pe, comb_done, n * KI + c - 1)
                    pe.matmul(c_ps[:, c % 2, :], w_c[:, c * P:(c + 1) * P], state[:], start=True,
                              stop=True).then_inc(c_full, 1)

            def step(l, g):
                new, mid, fin = unit(l, g, 0), unit(l, g, 1), unit(l, g, 2)
                if new:
                    project_in(new, 0)
                    project_in(new, 1)
                if mid:
                    n, lay, grp = mid
                    after(pe, w_rest_in, (lay + 1) * 48)
                    after(pe, u_ready, n * KI + KI)
                    after(pe, bu_ready, n)
                    for c in range(KI):
                        last = pe.matmul(b_ps[0:STATE, :], w_b[:, c, :], u[:, grp % 2, c, :],
                                         start=(c == 0), stop=(c == KI - 1))
                    last.then_inc(bu_full, 1)
                if new:
                    project_in(new, 2)
                    project_in(new, 3)
                if mid:
                    after(pe, scan_done, mid[0] + 1)
                    mix(mid, (0, 1))
                if new:
                    project_in(new, 4)
                    project_in(new, 5)
                if mid:
                    mix(mid, (2, 3))
                if new:
                    project_in(new, 6)
                    project_in(new, 7)
                for b in range(2):
                    if fin:
                        turn(fin[0] + GROUPS, fin[2], b)
                    if mid:
                        n, lay, grp = mid
                        after(pe, y_ready, n * KI + KI)
                        after(pe, z_done, (n - 1) * 2 + b + 1)
                        for j in (2 * b, 2 * b + 1):
                            for c in range(KI):
                                last = pe.matmul(d_ps[:, b, (j % 2) * D:(j % 2 + 1) * D],
                                                 y[:, grp % 2, c, j * TOK:(j + 1) * TOK], w_o[:, c, :],
                                                 start=(c == 0), stop=(c == KI - 1))
                        last.then_inc(d_full, 1)

            run(pe, step)


def attention_stage(nc, sems, io, res, ident, eps, name, hd, w_qkv_dram, w_out_dram,
                    rope=None, qkv_bias=None, out_bias=None, mask_dram=None, onto=None):
    k = Kit(nc, sems)
    inner = HEADS * hd
    pad = 64 if hd == 64 else 32
    half = hd // 2
    hpc = P // pad
    nch = HEADS // hpc
    no = inner // P
    qk_slices = 2 * inner // BANK
    vw = min(inner, BANK)
    v_slices = inner // vw
    nq = qk_slices + v_slices
    hps = 2 * HEADS // qk_slices
    vh = HEADS // v_slices
    nb, hb = 4, HEADS // 4
    scale = hd ** -0.5
    UNROLL = 4
    TR = {"qk": (1, 2 * nch // 4), "probs": (2, nb), "out": (3, -(-no // 4)), "norm": (-1, 1)}
    TR_ORDER = ("qk", "probs", "out", "norm")
    AV = {"heads": (2, nb), "proj": (3, 1)}
    AV_ORDER = ("heads", "proj")

    def ring_count(uses, order, s, phase, i):
        total = sum(n for _, n in uses.values())
        inside = 0
        for p in order:
            if p == phase:
                break
            back, n = uses[p]
            if not isinstance(s, int) or 0 <= s - back < SEQS:
                inside += n
        if isinstance(s, int):
            before = sum(n * min(max(s - back, 0), SEQS) for back, n in uses.values())
        else:
            before = s * total - sum(n * back for back, n in uses.values())
        return before + inside + i + 1

    with k.mem:
        w_qkv = k.sb(name + "w_qkv", [P, KD, 3 * inner])
        w_out = k.sb(name + "w_out", [P, no, D])
        xs = k.sb(name + "xs", [P, D])
        xT = k.sb(name + "xT", [P, KD, TOK])
        qk = k.sb(name + "qk", [P, 2, 2 * HEADS, pad])
        vals = k.sb(name + "vals", [P, UNROLL, HEADS, hd + 1])
        qkT = k.sb(name + "qkT", [P, 2, nch, TOK])
        probs = k.sb(name + "probs", [P, 2, HEADS, TOK])
        pT = k.sb(name + "pT", [P, HEADS, TOK])
        heads = k.sb(name + "heads", [P, 2, HEADS, hd])
        oT = k.sb(name + "oT", [P, no, TOK])
        top = k.sb(name + "top", [P, hb])
        rsum = k.sb(name + "rsum", [P, hb])
        stats = k.sb(name + "stats", [P, 6])
        mv = k.sb(name + "mv", [P, 2])
        std = k.sb(name + "std", [P, 1])
        rstd = k.sb(name + "rstd", [P, 1])
        if onto is not None:
            means = k.sb(name + "means", [P, SEQS])
            rstds = k.sb(name + "rstds", [P, SEQS])
        if rope:
            cos = k.sb(name + "cos", [P, half])
            sin = k.sb(name + "sin", [P, half])
            nsin = k.sb(name + "nsin", [P, half])
            turned = k.sb(name + "turned", [P, 2, hps, 2, half])
        if qkv_bias is not None:
            bias = k.sb(name + "bias", [P, 3 * inner])
        if out_bias is not None:
            bias_o = k.sb(name + "bias_o", [P, D])
            part = k.sb(name + "part", [P, D])
        if mask_dram is not None:
            mask = k.sb(name + "mask", [P, TOK])
        q_ps = k.ps(name + "q_ps", [P, 2, BANK])
        tr_ps = k.ps(name + "tr_ps", [P, 2, BANK])
        s_ps = k.ps(name + "s_ps", [P, 2, BANK])
        av_ps = k.ps(name + "av_ps", [P, 2, BANK])

        S = lambda n: k.sem(name + n)
        w_qkv_in, consts_in = S("w_qkv_in"), S("consts_in")
        set_up, var_ready, std_ready, xs_ready = S("set_up"), S("var_ready"), S("std_ready"), S("xs_ready")
        q_full, qk_taken, qk_ready, v_taken = S("q_full"), S("qk_taken"), S("qk_ready"), S("v_taken")
        tr_full, tr_taken = S("tr_full"), S("tr_taken")
        s_full, s_taken, p_ready = S("s_full"), S("s_taken"), S("p_ready")
        av_full, av_taken = S("av_full"), S("av_taken")
        n_consts = 1 + 3 * bool(rope) + (qkv_bias is not None) + (out_bias is not None) + (mask_dram is not None)
        qk_done = qk_ready if rope else qk_taken
        v_on_dve = qkv_bias is not None

        def tile(s, back):
            t = s - back
            return None if isinstance(s, int) and not 0 <= t < SEQS else t

        def run(eng, step):
            for s in range(-1, UNROLL - 1):
                step(s, s)
            with eng.Fori(1, SEQS // UNROLL) as i:
                for j in range(UNROLL):
                    step(i * UNROLL + (j - 1), (j - 1) % UNROLL)
            for s in range(SEQS - 1, SEQS + 3):
                step(s, s)

        block = k.mem.enter_context(nc.Block())

        @block.sync
        def _(sp):
            sp.dma_start(w_qkv[:], w_qkv_dram).then_inc(w_qkv_in, 16)
            if rope:
                sp.dma_start(cos[:], rope[0]).then_inc(consts_in, 16)
                sp.dma_start(sin[:], rope[1]).then_inc(consts_in, 16)
                sp.dma_start(nsin[:], rope[2]).then_inc(consts_in, 16)
            if qkv_bias is not None:
                sp.dma_start(bias[:], qkv_bias.to_broadcast([P, 3 * inner])).then_inc(consts_in, 16)
            if out_bias is not None:
                sp.dma_start(bias_o[:], out_bias.to_broadcast([P, D])).then_inc(consts_in, 16)
            if mask_dram is not None:
                sp.dma_start(mask[:], mask_dram).then_inc(consts_in, 16)
            sp.dma_start(w_out[:], w_out_dram).then_inc(consts_in, 16)

        def head_batch(view, b):
            if hpc == 2:
                return view.rearrange("p (a c two) d -> p a two c d", a=2, two=2)[:, b // 2, b % 2]
            return view.rearrange("p (c j) d -> p j c d", j=4)[:, b]

        def heads_of(b):
            return [(b // 2) * 8 + b % 2 + 2 * c for c in range(hb)] if hpc == 2 else [4 * c + b for c in range(hb)]

        def place(uses, order, s, j, phase, i):
            return (ring_count(uses, order, s if isinstance(s, int) else UNROLL + j, phase, i) - 1) % 2

        def qk_view(t, j0, h0, n):
            return qk[:, j0 % 2, h0:h0 + n, 0:hd]

        @block.gpsimd
        def _(pool):
            pool.memset(vals[:, :, :, hd:hd + 1], 1.0)
            pool.memset(qk[:], 0.0).then_inc(set_up, 1)

            def step(s, j):
                t = tile(s, 0)
                if t is not None and rope:
                    for i in range(qk_slices):
                        pool.drain()
                        after(pool, qk_taken, t * qk_slices + i + 1)
                        out = qk_view(t, j, i * hps, hps)
                        pool.tensor_tensor(out, out, turned[:, i % 2].rearrange("p h a d -> p h (a d)"),
                                           ALU.add).then_inc(qk_ready, 1)

            run(pool, step)

        @block.scalar
        def _(act):
            def copy_back(s, j, phase, i, out, width):
                at_ = ring_count(TR, TR_ORDER, s, phase, i)
                after(act, tr_full, at_)
                act.activation(out, tr_ps[:, place(TR, TR_ORDER, s, j, phase, i), 0:width],
                               ACT.Copy).then_inc(tr_taken, 1)

            act.wait_ge(set_up, 1)

            def step(s, j):
                if tile(s, 0) is not None and not v_on_dve:
                    t = tile(s, 0)
                    for i in range(v_slices):
                        after(act, q_full, t * nq + qk_slices + i + 1)
                        act.activation(vals[:, j % UNROLL, i * vh:(i + 1) * vh, 0:hd],
                                       q_ps[:, (qk_slices + i) % 2, 0:vw].rearrange("p (h d) -> p h d", d=hd),
                                       ACT.Copy).then_inc(v_taken, 1)
                if tile(s, 1) is not None:
                    t = tile(s, 1)
                    for i in range(TR["qk"][1]):
                        flat = qkT[:].rearrange("p a c t -> p (a c t)")
                        copy_back(s, j, "qk", i, flat[:, i * BANK:(i + 1) * BANK], BANK)
                    for b in range(nb):
                        after(act, s_taken, t * nb + b + 1)
                        rows = probs[:, (j - 1) % 2, b * hb:(b + 1) * hb, :]
                        act.activation(rows, rows, ACT.Exp, scale=scale).then_inc(p_ready, 1)
                if tile(s, 2) is not None:
                    for b in range(nb):
                        copy_back(s, j, "probs", b, pT[:, b * hb:(b + 1) * hb, :].rearrange("p h t -> p (h t)"), BANK)
                if tile(s, 3) is not None:
                    for i in range(TR["out"][1]):
                        w = min(4, no) * TOK
                        copy_back(s, j, "out", i, oT[:, 4 * i:4 * i + min(4, no), :].rearrange("p c t -> p (c t)"), w)
                if tile(s, -1) is not None:
                    t = tile(s, -1)
                    after(act, var_ready, t + 1)
                    act.activation(std[:], mv[:, 1:2], ACT.Sqrt, bias=eps[:, 0:1]).then_inc(std_ready, 1)
                    copy_back(s, j, "norm", 0, xT[:].rearrange("p c t -> p (c t)"), KD * TOK)

            run(act, step)

        @block.vector
        def _(dve):
            dve.wait_ge(consts_in, 16 * n_consts)
            dve.wait_ge(set_up, 1)

            def rotate(t, j, i):
                x = q_ps[:, i % 2, :].rearrange("p (h a d) -> p h a d", h=hps, a=2)
                out = qk_view(t, j, i * hps, hps).rearrange("p h (a d) -> p h a d", a=2)
                wide = lambda c: c[:].unsqueeze(1).to_broadcast([P, hps, half])
                both = cos[:].unsqueeze(1).unsqueeze(1).to_broadcast([P, hps, 2, half])
                after(dve, qk_ready, t * qk_slices + i + 1 - min(qk_slices, 2))
                dve.tensor_tensor(out, x, both, ALU.mult)
                dve.tensor_tensor(turned[:, i % 2, :, 0, :], x[:, :, 1, :], wide(nsin), ALU.mult)
                dve.tensor_tensor(turned[:, i % 2, :, 1, :], x[:, :, 0, :], wide(sin),
                                  ALU.mult).then_inc(qk_taken, 1)

            def step(s, j):
                t = tile(s, 0)
                if t is not None:
                    for i in range(qk_slices):
                        dve.drain()
                        after(dve, q_full, t * nq + i + 1)
                        if rope:
                            rotate(t, j, i)
                        else:
                            dve.tensor_tensor(qk_view(t, j, i * hps, hps),
                                              q_ps[:, i % 2, :].rearrange("p (h d) -> p h d", d=hd),
                                              bias[:, i * BANK:(i + 1) * BANK].rearrange("p (h d) -> p h d", d=hd),
                                              ALU.add).then_inc(qk_taken, 1)
                    if v_on_dve:
                        for i in range(v_slices):
                            dve.drain()
                            after(dve, q_full, t * nq + qk_slices + i + 1)
                            dve.tensor_tensor(
                                vals[:, j % UNROLL, i * vh:(i + 1) * vh, 0:hd],
                                q_ps[:, (qk_slices + i) % 2, 0:vw].rearrange("p (h d) -> p h d", d=hd),
                                bias[:, 2 * inner + i * vw:2 * inner + (i + 1) * vw].rearrange("p (h d) -> p h d", d=hd),
                                ALU.add).then_inc(v_taken, 1)
                t = tile(s, 1)
                if t is not None:
                    for b in range(nb):
                        dve.drain()
                        after(dve, s_full, t * nb + b + 1)
                        rows = probs[:, (j - 1) % 2, b * hb:(b + 1) * hb, :]
                        sc = s_ps[:, b % 2, :].rearrange("p (h t) -> p h t", h=hb)
                        if mask_dram is not None:
                            dve.tensor_tensor(rows, sc, mask[:].unsqueeze(1).to_broadcast([P, hb, TOK]), ALU.add)
                            sc = rows
                            dve.drain()
                        dve.tensor_reduce(top[:], sc, AX_X, ALU.max)
                        dve.drain()
                        dve.tensor_tensor(rows, sc, top[:].unsqueeze(2).to_broadcast([P, hb, TOK]),
                                          ALU.subtract).then_inc(s_taken, 1)
                t = tile(s, 2)
                if t is not None:
                    for b in range(nb):
                        dve.drain()
                        after(dve, av_full, ring_count(AV, AV_ORDER, s, "heads", b))
                        o = av_ps[:, place(AV, AV_ORDER, s, j, "heads", b), 0:hb * (hd + 1)].rearrange(
                            "p (h e) -> p h e", h=hb)
                        dve.reciprocal(rsum[:], o[:, :, hd])
                        dve.drain()
                        dve.tensor_tensor(head_batch(heads[:, (j - 2) % 2], b), o[:, :, 0:hd],
                                          rsum[:].unsqueeze(2).to_broadcast([P, hb, hd]),
                                          ALU.mult).then_inc(av_taken, 1)
                t = tile(s, 3)
                if t is not None:
                    dve.drain()
                    after(dve, av_full, ring_count(AV, AV_ORDER, s, "proj", 0))
                    o = av_ps[:, place(AV, AV_ORDER, s, j, "proj", 0), 0:D]
                    row = res[:, at(t), :].rearrange("p o d -> p (o d)")
                    if onto is not None:
                        src = onto[:, at(t), :].rearrange("p o d -> p (o d)")
                        dve.tensor_scalar(src, row, means[:, at(t)], rstds[:, at(t)], ALU.subtract, ALU.mult)
                        row = src
                    if out_bias is not None:
                        dve.tensor_tensor(part[:], o, bias_o[:], ALU.add).then_inc(av_taken, 1)
                        dve.drain()
                        dve.tensor_tensor(row, row, part[:], ALU.add)
                    else:
                        dve.tensor_tensor(row, row, o, ALU.add).then_inc(av_taken, 1)
                t = tile(s, -1)
                if t is not None:
                    row = res[:, at(t), :].rearrange("p o d -> p (o d)")
                    dve.drain()
                    dve.bn_stats(stats[:], row)
                    dve.drain()
                    dve.bn_aggr(mv[:], stats[:]).then_inc(var_ready, 1)
                    after(dve, std_ready, t + 1)
                    dve.reciprocal(rstd[:], std[:])
                    dve.drain()
                    after(dve, tr_full, ring_count(TR, TR_ORDER, s - 1, "norm", 0) if not (
                        isinstance(s, int) and s < 0) else 0)
                    dve.tensor_scalar(xs[:], row, mv[:, 0:1], rstd[:],
                                      ALU.subtract, ALU.mult).then_inc(xs_ready, 1)
                    if onto is not None:
                        dve.tensor_copy(means[:, at(t)], mv[:, 0:1])
                        dve.tensor_copy(rstds[:, at(t)], rstd[:])

            run(dve, step)

        @block.tensor
        def _(pe):
            pe.wait_ge(set_up, 1)

            def turn(s, j, phase, i, blocks):
                at_ = ring_count(TR, TR_ORDER, s, phase, i)
                after(pe, tr_taken, at_ - 2)
                for n, blk in enumerate(blocks):
                    last = pe.transpose(tr_ps[:, place(TR, TR_ORDER, s, j, phase, i), n * TOK:(n + 1) * TOK],
                                        blk, ident[:])
                last.then_inc(tr_full, 1)

            def step(s, j):
                t = tile(s, 0)
                if t is not None:
                    pe.wait_ge(w_qkv_in, 16)
                    after(pe, tr_taken, ring_count(TR, TR_ORDER, s - 1, "norm", 0))
                    for i in range(nq):
                        prev = i - 2
                        if prev < 0:
                            prev += nq
                            before = t - 1
                        else:
                            before = t
                        if nq == 2:
                            before = t - 1
                        if prev < qk_slices:
                            after(pe, qk_taken, before * qk_slices + prev + 1)
                        else:
                            after(pe, v_taken, before * v_slices + prev - qk_slices + 1)
                        width = BANK if i < qk_slices else vw
                        for kc in range(KD):
                            last = pe.matmul(q_ps[:, i % 2, 0:width], xT[:, kc, :],
                                             w_qkv[:, kc, i * BANK:i * BANK + width],
                                             start=(kc == 0), stop=(kc == KD - 1))
                        last.then_inc(q_full, 1)
                t = tile(s, 1)
                if t is not None:
                    after(pe, qk_done, (t + 1) * qk_slices)
                    flat = qk[:, (j - 1) % 2].rearrange("p h d -> p (h d)")
                    for i in range(TR["qk"][1]):
                        turn(s, j, "qk", i, [flat[:, (4 * i + n) * P:(4 * i + n + 1) * P] for n in range(4)])
                    after(pe, tr_taken, ring_count(TR, TR_ORDER, s, "qk", TR["qk"][1] - 1))
                    for b in range(nb):
                        after(pe, s_taken, t * nb + b - 1)
                        for n, h in enumerate(heads_of(b)):
                            r = (h % hpc) * pad
                            last = pe.matmul(s_ps[:, b % 2, n * TOK:(n + 1) * TOK],
                                             qkT[r:r + hd, 0, h // hpc, :], qkT[r:r + hd, 1, h // hpc, :],
                                             start=True, stop=True)
                        last.then_inc(s_full, 1)
                t = tile(s, 2)
                if t is not None:
                    after(pe, v_taken, (t + 1) * v_slices)

                    def weigh(b):
                        after(pe, tr_taken, ring_count(TR, TR_ORDER, s, "probs", b))
                        after(pe, av_taken, ring_count(AV, AV_ORDER, s, "heads", b) - 2)
                        for n, h in enumerate(heads_of(b)):
                            last = pe.matmul(av_ps[:, place(AV, AV_ORDER, s, j, "heads", b),
                                                   n * (hd + 1):(n + 1) * (hd + 1)],
                                             pT[:, b * hb + n, :], vals[:, (j - 2) % UNROLL, h, :],
                                             start=True, stop=True)
                        last.then_inc(av_full, 1)

                    for b in range(nb):
                        after(pe, p_ready, t * nb + b + 1)
                        turn(s, j, "probs", b, [probs[:, (j - 2) % 2, b * hb + n, :] for n in range(hb)])
                        if b:
                            weigh(b - 1)
                    weigh(nb - 1)
                t = tile(s, 3)
                if t is not None:
                    pe.wait_ge(consts_in, 16 * n_consts)
                    after(pe, av_taken, ring_count(AV, AV_ORDER, s - 1, "heads", nb - 1))
                    flat = heads[:, (j - 3) % 2].rearrange("p h d -> p (h d)")
                    for i in range(TR["out"][1]):
                        turn(s, j, "out", i, [flat[:, c * P:(c + 1) * P] for c in range(4 * i, min(4 * i + 4, no))])
                    after(pe, tr_taken, ring_count(TR, TR_ORDER, s, "out", TR["out"][1] - 1))
                    after(pe, av_taken, ring_count(AV, AV_ORDER, s, "proj", 0) - 2)
                    for c in range(no):
                        last = pe.matmul(av_ps[:, place(AV, AV_ORDER, s, j, "proj", 0), 0:D], oT[:, c, :],
                                         w_out[:, c, :], start=(c == 0), stop=(c == no - 1))
                    last.then_inc(av_full, 1)
                t = tile(s, -1)
                if t is not None:
                    after(pe, xs_ready, t + 1)
                    turn(s, j, "norm", 0, [xs[:, c * P:(c + 1) * P] for c in range(KD)])

            run(pe, step)


def experts_stage(nc, sems, io, res, ident, eps, name, n_exp, n_routed, chunks, gated, acc, out=None):
    k = Kit(nc, sems)
    E, R = n_exp, n_routed
    NUP = 4
    UNITS = E * GROUPS
    with k.mem:
        xT = k.sb(name + "xT", [P, KD, SEQS * TOK])
        w_up = k.sb(name + "w_up", [P, 2, KD, NUP * P])
        w_dn = k.sb(name + "w_dn", [P, 2, chunks, D])
        h = k.sb(name + "h", [P, 2, chunks, GT])
        router = k.sb(name + "router", [P, KD, R])
        r_bias = k.sb(name + "r_bias", [P, R])
        lt = k.sb(name + "lt", [P, R, R])
        xn = k.sb(name + "xn", [P, TPG, D])
        stats = k.sb(name + "stats", [P, TPG, 6])
        mv = k.sb(name + "mv", [P, TPG, 2])
        std = k.sb(name + "std", [P, TPG])
        rstd = k.sb(name + "rstd", [P, TPG])
        score = k.sb(name + "score", [P, SEQS, R])
        choice = k.sb(name + "choice", [P, SEQS, R])
        rank = k.sb(name + "rank", [P, SEQS, R])
        greater = k.sb(name + "greater", [P, SEQS * R * R])
        equal = k.sb(name + "equal", [P, SEQS * R * R])
        total = k.sb(name + "total", [P, SEQS])
        weight = k.sb(name + "weight", [P, SEQS, E])
        if gated:
            silu = k.sb(name + "silu", [P, chunks, GT])
            lt4 = k.sb(name + "lt4", [P, 4, 4])
            group = k.sb(name + "group", [P, SEQS, 4])
            g_rank = k.sb(name + "g_rank", [P, SEQS, 4])
        else:
            b_up = k.sb(name + "b_up", [P, 2, NUP])
            b_dn = k.sb(name + "b_dn", [E, D])
            wT = k.sb(name + "wT", [E, SEQS * TOK])
            ln = k.sb(name + "ln", [P, 4, D])
        up_ps = k.ps(name + "up_ps", [P, 4, BANK])
        dn_ps = k.ps(name + "dn_ps", [P, 4, BANK])

        S = lambda n: k.sem(name + n)
        consts_in, w_in = S("consts_in"), [S("w_in_even"), S("w_in_odd")]
        var_ready, std_ready, xn_ready, x_ready = S("var_ready"), S("std_ready"), S("xn_ready"), S("x_ready")
        t_full, xT_ready, r_full = S("t_full"), S("xT_ready"), S("r_full")
        score_in, score_out, weights_ready = S("score_in"), S("score_out"), S("weights_ready")
        up_full, silu_ready, h_ready = S("up_full"), S("silu_ready"), S("h_ready")
        dn_full, acc_done = S("dn_full"), S("acc_done")
        wT_full, wT_ready, bias_full, bias_done = S("wT_full"), S("wT_ready"), S("bias_full"), S("bias_done")
        var2_ready, std2_ready, xn2_ready, stored = S("var2_ready"), S("std2_ready"), S("xn2_ready"), S("stored")
        n_consts = 4 if gated else 8
        PER_EXPERT = 32 if gated else 48

        def run(eng, step):
            for par in range(2):
                for g in range(GROUPS):
                    step(par * GROUPS + g, par, par, g)
            with eng.Fori(1, E // 2) as i:
                for par in range(2):
                    for g in range(GROUPS):
                        step(i * 2 * GROUPS + par * GROUPS + g, i * 2 + par, par, g)
            step(UNITS, None, 0, 0)

        def before(n, e, par, g):
            if isinstance(n, int) and n == 0:
                return None
            if e is None:
                return n - 1, E - 1, 1, GROUPS - 1
            return (n - 1, e, par, g - 1) if g else (n - 1, e - 1, 1 - par, GROUPS - 1)

        block = k.mem.enter_context(nc.Block())

        @block.sync
        def _(sp):
            def load(e, par):
                up, dn = io[name + "up"][at(e)], io[name + "dn"][at(e)]
                sp.dma_start(w_up[:, par], up.rearrange("e p k n -> (e p) k n")).then_inc(w_in[par], 16)
                sp.dma_start(w_dn[:, par], dn.rearrange("e p k n -> (e p) k n")).then_inc(w_in[par], 16)
                if not gated:
                    b = io[name + "b_up"][at(e)]
                    sp.dma_start(b_up[:, par], b.rearrange("e p c -> (e p) c")).then_inc(w_in[par], 16)

            sp.dma_start(router[:], io[name + "router"]).then_inc(consts_in, 16)
            sp.dma_start(r_bias[:], io[name + "r_bias"].to_broadcast([P, R])).then_inc(consts_in, 16)
            sp.dma_start(lt[:], io["lt%d" % R]).then_inc(consts_in, 16)
            if gated:
                sp.dma_start(lt4[:], io["lt4"]).then_inc(consts_in, 16)
            else:
                sp.dma_start(b_dn[:], io[name + "b_dn"]).then_inc(consts_in, 16)
                for n, key in enumerate(("ln1_g", "ln1_b", "ln2_g", "ln2_b")):
                    sp.dma_start(ln[:, n, :], io[name + key].to_broadcast([P, D])).then_inc(consts_in, 16)
            load(0, 0)
            load(1, 1)
            with sp.Fori(1, E // 2) as i:
                for par in range(2):
                    sp.wait_ge(dn_full, i * 16 + (8 * par - 8))
                    load(i * 2 + par, par)
            if out is not None:
                for g in range(GROUPS):
                    sp.wait_ge(acc_done, 2 * (UNITS - GROUPS + g + 1))
                    sp.dma_start(out.rearrange("(t p) d -> p t d", p=P)[:, g * TPG:(g + 1) * TPG, :],
                                 acc[:, g * TPG:(g + 1) * TPG, :]).then_inc(stored, 16)
                sp.wait_ge(stored, 16 * GROUPS)

        def scaled(n):
            return ln[:, n:n + 1, :].to_broadcast([P, TPG, D])

        if not gated:
            @block.gpsimd
            def _(pool):
                pool.wait_ge(consts_in, 16 * n_consts)
                for g in range(GROUPS):
                    pool.drain()
                    rows = acc[:, g * TPG:(g + 1) * TPG, :]
                    pool.wait_ge(xn_ready, g + 1)
                    pool.tensor_tensor(rows, xn[:], scaled(0), ALU.mult)
                    pool.drain()
                    pool.tensor_tensor(rows, rows, scaled(1), ALU.add).then_inc(x_ready, 1)
                for g in range(GROUPS):
                    pool.drain()
                    rows = res[:, g * TPG:(g + 1) * TPG, :]
                    pool.wait_ge(xn2_ready, g + 1)
                    pool.tensor_tensor(xn[:], xn[:], scaled(2), ALU.mult)
                    pool.drain()
                    pool.tensor_tensor(xn[:], xn[:], scaled(3), ALU.add)
                    pool.drain()
                    pool.tensor_tensor(rows, rows, xn[:], ALU.add).then_inc(x_ready, 1)

        @block.scalar
        def _(act):
            act.wait_ge(consts_in, 16 * n_consts)
            for g in range(GROUPS):
                act.wait_ge(var_ready, g + 1)
                act.activation(std[:], mv[:, :, 1], ACT.Sqrt, bias=eps[:, 0:1]).then_inc(std_ready, 1)
                for kc in range(KD):
                    act.wait_ge(t_full, g * KD + kc + 1)
                    act.activation(xT[:, kc, g * GT:(g + 1) * GT], up_ps[:, kc, :], ACT.Copy).then_inc(xT_ready, 1)
            if gated:
                act.wait_ge(r_full, 1)
                act.activation(score[:], up_ps[:, 2, 0:SEQS * R].rearrange("p (t r) -> p t r", r=R),
                               ACT.Sigmoid).then_inc(score_out, 1)
            else:
                act.wait_ge(score_in, 1)
                act.activation(score[:], score[:], ACT.Exp).then_inc(score_out, 1)
                for g in range(GROUPS):
                    act.wait_ge(wT_full, g + 1)
                    act.activation(wT[:, g * GT:(g + 1) * GT], up_ps[0:E, g, :], ACT.Copy).then_inc(wT_ready, 1)

            def step(n, e, par, g):
                if e is None:
                    return
                for f in range(chunks):
                    if gated:
                        after(act, up_full, n * 4 + 2 * f + 1)
                        after(act, h_ready, (n - 1) * chunks + f + 1)
                        act.activation(silu[:, f, :], up_ps[:, 2 * f, :], ACT.Silu).then_inc(silu_ready, 1)
                    else:
                        after(act, up_full, n * 4 + f + 1)
                        act.activation(h[:, g % 2, f, :], up_ps[:, f, :], ACT.Relu,
                                       bias=b_up[:, par, f:f + 1]).then_inc(h_ready, 1)

            run(act, step)
            if not gated:
                for g in range(GROUPS):
                    act.wait_ge(var2_ready, g + 1)
                    act.activation(std[:], mv[:, :, 1], ACT.Sqrt, bias=eps[:, 0:1]).then_inc(std2_ready, 1)

        @block.vector
        def _(dve):
            dve.wait_ge(consts_in, 16 * n_consts)

            def norm(g, var, stdr, xnr, xn_free, count):
                rows = acc[:, g * TPG:(g + 1) * TPG, :]
                dve.drain()
                for j in range(TPG):
                    dve.bn_stats(stats[:, j, :], rows[:, j, :])
                dve.drain()
                for j in range(TPG):
                    last = dve.bn_aggr(mv[:, j, :], stats[:, j, :])
                last.then_inc(var, 1)
                dve.wait_ge(stdr, g + 1)
                dve.reciprocal(rstd[:], std[:])
                dve.drain()
                after(dve, xn_free, count)
                for j in range(TPG):
                    last = dve.tensor_scalar(xn[:, j, :], rows[:, j, :], mv[:, j, 0:1], rstd[:, j:j + 1],
                                             ALU.subtract, ALU.mult)
                last.then_inc(xnr, 1)

            def ranks(values, out_rank, tri, groups, n):
                shape = [P, groups, n, n]
                g4 = greater[:, 0:groups * n * n].rearrange("p (g e j) -> p g e j", e=n, j=n)
                e4 = equal[:, 0:groups * n * n].rearrange("p (g e j) -> p g e j", e=n, j=n)
                other = values.unsqueeze(2).to_broadcast(shape)
                own = values.unsqueeze(3).to_broadcast(shape)
                dve.drain()
                dve.tensor_tensor(g4, other, own, ALU.is_gt)
                dve.tensor_tensor(e4, other, own, ALU.is_equal)
                dve.drain()
                dve.tensor_tensor(e4, e4, tri[:].unsqueeze(1).to_broadcast(shape), ALU.mult)
                dve.drain()
                dve.tensor_tensor(g4, g4, e4, ALU.add)
                dve.drain()
                dve.tensor_reduce(out_rank, g4, AX_X, ALU.add)
                dve.drain()

            def wide(t, n):
                return t.unsqueeze(2).to_broadcast([P, SEQS, n])

            for g in range(GROUPS):
                norm(g, var_ready, std_ready, xn_ready, t_full if gated else x_ready, g * KD if gated else g)
            dve.drain()
            if gated:
                dve.memset(weight[:, :, R:E], 1.0)
                dve.wait_ge(score_out, 1)
                dve.tensor_tensor(choice[:], score[:], r_bias[:].unsqueeze(1).to_broadcast([P, SEQS, R]), ALU.add)
                quads = choice[:].rearrange("p t (g e) -> p (t g) e", e=4)
                q_rank = rank[:].rearrange("p t (g e) -> p (t g) e", e=4)
                ranks(quads, q_rank, lt4, SEQS * 4, 4)
                dve.scalar_tensor_tensor(rank[:], rank[:], 2.0, choice[:], ALU.is_lt, ALU.mult)
                dve.drain()
                dve.tensor_reduce(group[:].rearrange("p t g -> p (t g)"), q_rank, AX_X, ALU.add)
                ranks(group[:], g_rank[:], lt4, SEQS, 4)
                dve.tensor_scalar(group[:], g_rank[:], 2.0, None, ALU.is_lt)
                dve.drain()
                dve.tensor_scalar(g_rank[:], group[:], -1.0, None, ALU.add)
                keep = lambda t: t[:].rearrange("p t g -> p (t g)").unsqueeze(2).to_broadcast([P, SEQS * 4, 4])
                dve.tensor_tensor(quads, quads, keep(group), ALU.mult)
                dve.drain()
                dve.tensor_tensor(quads, quads, keep(g_rank), ALU.add)
                ranks(choice[:], rank[:], lt, SEQS, R)
                dve.scalar_tensor_tensor(choice[:], rank[:], 4.0, score[:], ALU.is_lt, ALU.mult)
                dve.drain()
                dve.tensor_reduce(total[:], choice[:], AX_X, ALU.add)
                dve.drain()
                dve.tensor_scalar(total[:], total[:], 1e-20, None, ALU.add)
                dve.drain()
                dve.reciprocal(total[:], total[:])
                dve.drain()
                dve.scalar_tensor_tensor(weight[:, :, 0:R], choice[:], 2.5, wide(total[:], R),
                                         ALU.mult, ALU.mult).then_inc(weights_ready, 1)
            else:
                dve.wait_ge(r_full, 1)
                dve.tensor_tensor(score[:], up_ps[:, 2, 0:SEQS * R].rearrange("p (t r) -> p t r", r=R),
                                  r_bias[:].unsqueeze(1).to_broadcast([P, SEQS, R]), ALU.add)
                dve.drain()
                dve.tensor_reduce(total[:], score[:], AX_X, ALU.max)
                dve.drain()
                dve.tensor_tensor(score[:], score[:], wide(total[:], R), ALU.subtract).then_inc(score_in, 1)
                dve.wait_ge(score_out, 1)
                dve.tensor_reduce(total[:], score[:], AX_X, ALU.add)
                dve.drain()
                dve.reciprocal(total[:], total[:])
                dve.drain()
                dve.tensor_tensor(score[:], score[:], wide(total[:], R), ALU.mult)
                ranks(score[:], rank[:], lt, SEQS, R)
                dve.scalar_tensor_tensor(weight[:], rank[:], 2.0, score[:], ALU.is_lt,
                                         ALU.mult).then_inc(weights_ready, 1)
                for b in range(SEQS // 2):
                    dve.drain()
                    dve.wait_ge(bias_full, b + 1)
                    rows = acc[:, 2 * b:2 * b + 2, :]
                    dve.tensor_tensor(rows, rows, dn_ps[:, b % 4, :].rearrange("p (j d) -> p j d", j=2),
                                      ALU.add).then_inc(bias_done, 1)

            def step(n, e, par, g):
                if gated and e is not None:
                    for f in range(chunks):
                        after(dve, up_full, n * 4 + 2 * f + 2)
                        after(dve, silu_ready, n * chunks + f + 1)
                        dve.tensor_tensor(h[:, g % 2, f, :], silu[:, f, :], up_ps[:, 2 * f + 1, :],
                                          ALU.mult).then_inc(h_ready, 1)
                prev = before(n, e, par, g)
                if prev:
                    m, pe_, ppar, pg = prev
                    dve.drain()
                    for b in range(2):
                        after(dve, dn_full, m * 2 + b + 1)
                        for j in range(2):
                            t = pg * TPG + 2 * b + j
                            last = dve.scalar_tensor_tensor(
                                acc[:, t, :], dn_ps[:, 2 * (pg % 2) + b, j * D:(j + 1) * D], weight[:, t, at(pe_)],
                                acc[:, t, :], ALU.mult, ALU.add)
                        last.then_inc(acc_done, 1)

            run(dve, step)
            if not gated:
                for g in range(GROUPS):
                    norm(g, var2_ready, std2_ready, xn2_ready, x_ready, GROUPS + g)

        @block.tensor
        def _(pe):
            pe.wait_ge(consts_in, 16 * n_consts)
            for g in range(GROUPS):
                pe.wait_ge(xn_ready if gated else x_ready, g + 1)
                for kc in range(KD):
                    after(pe, xT_ready, (g - 1) * KD + kc + 1)
                    for j in range(TPG):
                        src = xn[:, j, kc * P:(kc + 1) * P] if gated else acc[:, g * TPG + j, kc * P:(kc + 1) * P]
                        last = pe.transpose(up_ps[:, kc, j * TOK:(j + 1) * TOK], src, ident[:])
                    last.then_inc(t_full, 1)
            pe.wait_ge(xT_ready, GROUPS * KD)
            for t in range(SEQS):
                for kc in range(KD):
                    last = pe.matmul(up_ps[:, 2, t * R:(t + 1) * R], xT[:, kc, t * TOK:(t + 1) * TOK],
                                     router[:, kc, :], start=(kc == 0), stop=(kc == KD - 1))
            last.then_inc(r_full, 1)
            if gated:
                pe.wait_ge(score_out, 1)
            else:
                pe.wait_ge(weights_ready, 1)
                for g in range(GROUPS):
                    for j in range(TPG):
                        t = g * TPG + j
                        last = pe.transpose(up_ps[0:E, g, j * TOK:(j + 1) * TOK], weight[:, t, :], ident[:])
                    last.then_inc(wT_full, 1)
                pe.wait_ge(wT_ready, GROUPS)
                for b in range(SEQS // 2):
                    after(pe, bias_done, b - 3)
                    for j in range(2):
                        t = 2 * b + j
                        last = pe.matmul(dn_ps[:, b % 4, j * D:(j + 1) * D], wT[:, t * TOK:(t + 1) * TOK],
                                         b_dn[:], start=True, stop=True)
                    last.then_inc(bias_full, 1)

            def step(n, e, par, g):
                if e is not None:
                    pair = 0 if isinstance(e, int) else (e - par)
                    pe.wait_ge(w_in[par], pair * (PER_EXPERT // 2) + PER_EXPERT)
                    for c in range(NUP):
                        if gated:
                            after(pe, h_ready if c % 2 else silu_ready, (n - 1) * chunks + c // 2 + 1)
                        else:
                            after(pe, h_ready, (n - 1) * chunks + c + 1)
                        for kc in range(KD):
                            last = pe.matmul(up_ps[:, c, :], w_up[:, par, kc, c * P:(c + 1) * P],
                                             xT[:, kc, g * GT:(g + 1) * GT], start=(kc == 0), stop=(kc == KD - 1))
                        last.then_inc(up_full, 1)
                prev = before(n, e, par, g)
                if prev:
                    m, pe_, ppar, pg = prev
                    after(pe, h_ready, m * chunks + chunks)
                    if not gated and isinstance(n, int) and n == 1:
                        pe.wait_ge(bias_done, SEQS // 2)
                    for b in range(2):
                        after(pe, acc_done, (m - 2) * 2 + b + 1)
                        for j in range(2):
                            for f in range(chunks):
                                t = 2 * b + j
                                last = pe.matmul(dn_ps[:, 2 * (pg % 2) + b, j * D:(j + 1) * D],
                                                 h[:, pg % 2, f, t * TOK:(t + 1) * TOK], w_dn[:, ppar, f, :],
                                                 start=(f == 0), stop=(f == chunks - 1))
                        last.then_inc(dn_full, 1)

            run(pe, step)


def build(nc, io, out):
    with ExitStack() as sems:
        res = sems.enter_context(nc.sbuf_tensor("res", [P, SEQS, D], F32))
        ident = sems.enter_context(nc.sbuf_tensor("ident", [P, P], F32))
        eps = sems.enter_context(nc.sbuf_tensor("eps", [P, 1], F32))
        ident_in = sems.enter_context(nc.semaphore("ident_in"))
        eps_set = sems.enter_context(nc.semaphore("eps_set"))
        with nc.Block() as block:
            @block.sync
            def _(sp):
                sp.dma_start(ident[:], io["ident"]).then_inc(ident_in, 16)
                sp.wait_ge(ident_in, 16)

            @block.vector
            def _(dve):
                dve.memset(eps[:], EPS).then_inc(eps_set, 1)
                dve.wait_ge(eps_set, 1)

        token_stage(nc, sems, io, res, ident, eps)
        attention_stage(nc, sems, io, res, ident, eps, "a0_", 64, io["a0_w_qkv"], io["a0_w_out"],
                        rope=(io["cos64"], io["sin64"], io["nsin64"]), out_bias=io["a0_b_out"])
        with nc.sbuf_tensor("mixed", [P, SEQS, D], F32) as mixed:
            attention_stage(nc, sems, io, res, ident, eps, "f0_", 16, io["f0_w_qkv"], io["f0_w_out"],
                            qkv_bias=io["f0_b_qkv"], out_bias=io["f0_b_out"], onto=mixed)
            experts_stage(nc, sems, io, res, ident, eps, "m0_", 8, 8, 4, False, mixed)
        attention_stage(nc, sems, io, res, ident, eps, "a1_", 16, io["a1_w_qkv"], io["a1_w_out"],
                        rope=(io["cos16"], io["sin16"], io["nsin16"]), mask_dram=io["mask"])
        experts_stage(nc, sems, io, res, ident, eps, "m1_", 18, 16, 2, True, res, out=out)


def kernel(**inputs):
    import numpy as np
    import concourse.bacc as bacc
    from concourse.bass_utils import run_bass_kernel_spmd

    a = {n: np.asarray(v) for n, v in inputs.items()}

    def rows(w):
        *lead, kk, n = w.shape
        return np.moveaxis(w.reshape(*lead, kk // P, P, n), -3, -2)

    def cols(v):
        *lead, kk = v.shape
        return np.moveaxis(v.reshape(*lead, kk // P, P), -1, 0)

    def rope(n, half):
        theta = (np.float32(1.0) / np.float32(10000.0) ** (np.arange(half, dtype=np.float32) / np.float32(half)))
        angle = np.arange(n, dtype=np.float32)[:, None] * theta.astype(np.float32)[None, :]
        return np.cos(angle).astype(np.float32), np.sin(angle).astype(np.float32)

    def lower(n):
        return np.broadcast_to(np.tril(np.ones((n, n), np.float32), -1), (P, n, n))

    t = {"ids": a["x"].T, "emb": a["L0_tok_tok_emb"], "pos": a["L0_tok_pos_emb"][:TOK]}
    t["w_in"] = rows(a["L0_tok_W_in"].transpose(0, 2, 1))
    t["w_b"] = rows(a["L0_tok_W_B"].transpose(0, 2, 1))
    t["w_c"] = a["L0_tok_W_C"].transpose(0, 2, 1)
    t["w_o"] = rows(a["L0_tok_W_out"].transpose(0, 2, 1))
    t["conv_w"] = np.moveaxis(a["L0_tok_conv_w"][:, :, 0, :].reshape(LAYERS, KI, P, TAPS), 2, 0)
    t["conv_b"] = cols(a["L0_tok_conv_b"])
    t["d_vec"] = cols(a["L0_tok_D_vec"])
    t["tok_ln_g"], t["tok_ln_b"] = a["L0_tok_ln_g"], a["L0_tok_ln_b"]
    decay = np.full((STATE, GT), DECAY, np.float32)
    decay[:, ::TOK] = 0.0
    t["decay"] = decay
    t["ident"] = np.eye(P, dtype=np.float32)
    t["cos64"], t["sin64"] = rope(TOK, 32)
    t["cos16"], t["sin16"] = rope(TOK, 8)
    t["nsin64"], t["nsin16"] = -t["sin64"], -t["sin16"]
    i = np.arange(TOK)
    seen = (i[:, None] // 64 == i[None, :] // 64) & (i[None, :] <= i[:, None])
    t["mask"] = np.where(seen, np.float32(0), np.float32(-3e38)).astype(np.float32)
    for n in (4, 8, 16):
        t["lt%d" % n] = lower(n)
    t["a0_w_qkv"] = rows(a["L0_attn_w_qkv"])
    t["a0_w_out"] = rows(a["L0_attn_w_out"])
    t["a0_b_out"] = a["L0_attn_b_out"][None]
    t["f0_w_qkv"] = rows(np.concatenate([a["L0_ffn_Wq"], a["L0_ffn_Wk"], a["L0_ffn_Wv"]], 1))
    t["f0_b_qkv"] = np.concatenate([a["L0_ffn_bq"], a["L0_ffn_bk"], a["L0_ffn_bv"]])[None]
    t["f0_w_out"] = rows(a["L0_ffn_Wo"])
    t["f0_b_out"] = a["L0_ffn_bo"][None]
    t["m0_router"] = rows(a["L0_ffn_gW"])
    t["m0_r_bias"] = a["L0_ffn_gb"][None]
    t["m0_up"] = rows(a["L0_ffn_W1"])
    t["m0_b_up"] = a["L0_ffn_b1"].reshape(8, 4, P).transpose(0, 2, 1)
    t["m0_dn"] = rows(a["L0_ffn_W2"])
    t["m0_b_dn"] = a["L0_ffn_b2"]
    for n in ("ln1_g", "ln1_b", "ln2_g", "ln2_b"):
        t["m0_" + n] = a["L0_ffn_" + n][None]
    w = a["L1_attn_Wqkv"].reshape(3, HEADS, 8, 2, D)
    q_k = w[:2].transpose(0, 1, 3, 2, 4).reshape(2 * D, D)
    t["a1_w_qkv"] = rows(np.concatenate([q_k, a["L1_attn_Wqkv"][2 * D:]]).T)
    t["a1_w_out"] = rows(a["L1_attn_Wout"].T)
    t["m1_router"] = rows(a["L1_ffn_router_w"].T)
    t["m1_r_bias"] = a["L1_ffn_bias"][None]

    def experts(routed, shared):
        return np.concatenate([routed, shared.reshape(D, 2, D).transpose(1, 0, 2)])

    gate = experts(a["L1_ffn_gate_w"], a["L1_ffn_sh_gate_w"]).reshape(18, D, 2, P)
    up = experts(a["L1_ffn_up_w"], a["L1_ffn_sh_up_w"]).reshape(18, D, 2, P)
    t["m1_up"] = rows(np.stack([gate, up], 3).reshape(18, D, 4 * P))
    t["m1_dn"] = rows(np.concatenate([a["L1_ffn_down_w"], a["L1_ffn_sh_down_w"].reshape(2, D, D)]))

    nc = bacc.Bacc("TRN2", target_bir_lowering=False, num_devices=1)
    arrays, io = {}, {}
    for n, v in t.items():
        arrays["in_" + n] = np.ascontiguousarray(v)
        io[n] = nc.dram_tensor("in_" + n, v.shape, mybir.dt.from_np(v.dtype), kind="ExternalInput").ap()
    out = nc.dram_tensor("out_0", (SEQS * TOK, D), F32, kind="ExternalOutput").ap()
    build(nc, io, out)
    r = run_bass_kernel_spmd(nc, [arrays], core_ids=[0])
    return r.results[0]["out_0"].reshape(SEQS, TOK, D)
```

```python
from contextlib import ExitStack

import concourse.bass as bass
from concourse import mybir

F32 = mybir.dt.float32
I32 = mybir.dt.int32
U32 = mybir.dt.uint32
ALU = mybir.AluOpType
ACT = mybir.ActivationFunctionType
AX_X = mybir.AxisListType.X

P = 128
SEQS = 16
TOK = 128
D = 256
KD = D // P
GROUPS = 4
TPG = SEQS // GROUPS
GT = TPG * TOK
LAYERS = 4
INNER = 512
KI = INNER // P
STATE = 64
TAPS = 4
DECAY, INP = 0.95, 0.05
EPS = 1e-5
HEADS = 16
BANK = 512


def after(eng, sem, count):
    if isinstance(count, int) and count <= 0:
        return
    eng.wait_ge(sem, count)


def at(i):
    return slice(i, i + 1) if isinstance(i, int) else bass.ds(i, 1)


class Kit:

    def __init__(self, nc, sems):
        self.nc, self.sems, self.mem = nc, sems, ExitStack()

    def sem(self, name):
        return self.sems.enter_context(self.nc.semaphore(name))

    def sb(self, name, shape, dt=F32):
        return self.mem.enter_context(self.nc.sbuf_tensor(name, shape, dt))

    def ps(self, name, shape):
        return self.mem.enter_context(self.nc.psum_tensor(name, shape, F32))


def token_stage(nc, sems, io, res, ident, eps, prefetch):
    k = Kit(nc, sems)
    with k.mem:
        ids = k.sb("ids", [P, SEQS], I32)
        pos = k.sb("pos", [P, D])
        xT = k.sb("tok_xT", [P, KD, SEQS * TOK])
        w_in = k.sb("w_in", [P, KD, 2 * INNER])
        w_b = k.sb("w_b", [P, KI, STATE])
        w_c = k.sb("w_c", [STATE, INNER])
        w_o = k.sb("w_o", [P, KI, D])
        conv_w = k.sb("conv_w", [P, LAYERS, KI, TAPS])
        conv_b = k.sb("conv_b", [P, LAYERS, KI])
        d_vec = k.sb("d_vec", [P, LAYERS, KI])
        ln_g = k.sb("tok_ln_g", [P, LAYERS, D])
        ln_b = k.sb("tok_ln_b", [P, LAYERS, D])
        gain = k.sb("gain", [P, 2, D])
        decay = k.sb("decay", [STATE, GT])
        u = k.sb("u", [P, 2, KI, GT])
        gate = k.sb("gate", [P, 2, KI, GT])
        y = k.sb("y", [P, 2, KI, GT])
        bu = k.sb("bu", [STATE, GT])
        state = k.sb("state", [STATE, GT])
        z = k.sb("tok_z", [P, TPG, D])
        stats = k.sb("tok_stats", [P, TPG, 6])
        mv = k.sb("tok_mv", [P, TPG, 2])
        std = k.sb("tok_std", [P, TPG])
        rstd = k.sb("tok_rstd", [P, TPG])
        xp_ps = k.ps("xp_ps", [P, 2, BANK])
        b_ps = k.ps("b_ps", [P, BANK])
        c_ps = k.ps("c_ps", [P, 2, BANK])
        d_ps = k.ps("d_ps", [P, 2, BANK])
        t_ps = k.ps("t_ps", [P, BANK])

        ids_in, consts_in, w_in_in, w_rest_in, gathered = (
            k.sem(n) for n in ("ids_in", "tok_consts_in", "w_in_in", "w_rest_in", "gathered"))
        xp_full, conv_done, gate_done, u_ready = (k.sem(n) for n in ("xp_full", "conv_done", "gate_done", "u_ready"))
        bu_full, bu_ready, scan_done = (k.sem(n) for n in ("bu_full", "bu_ready", "scan_done"))
        c_full, comb_done, y_ready = (k.sem(n) for n in ("c_full", "comb_done", "y_ready"))
        d_full, z_done, var_ready, std_ready, xn_ready = (
            k.sem(n) for n in ("d_full", "z_done", "tok_var_ready", "tok_std_ready", "tok_xn_ready"))
        res_ready, t_full, xT_ready = (k.sem(n) for n in ("res_ready", "tok_t_full", "tok_xT_ready"))
        CONSTS = 7

        def unit(l, g, back):
            lay, grp = l + (g - back) // GROUPS, (g - back) % GROUPS
            if isinstance(lay, int) and not 0 <= lay < LAYERS:
                return None
            return lay * GROUPS + grp, lay, grp

        def run(eng, step):
            for g in range(GROUPS):
                step(0, g)
            with eng.Fori(1, LAYERS) as l:
                for g in range(GROUPS):
                    step(l, g)
            step(LAYERS, 0)
            step(LAYERS, 1)

        block = k.mem.enter_context(nc.Block())

        @block.sync
        def _(sp):
            sp.dma_start(ids[:], io["ids"]).then_inc(ids_in, 16)
            sp.dma_start(pos[:], io["pos"]).then_inc(consts_in, 16)
            sp.dma_start(w_in[:], io["w_in"][0]).then_inc(w_in_in, 16)
            sp.dma_start(conv_w[:], io["conv_w"]).then_inc(consts_in, 16)
            sp.dma_start(conv_b[:], io["conv_b"]).then_inc(consts_in, 16)
            sp.dma_start(w_b[:], io["w_b"][0]).then_inc(w_rest_in, 16)
            sp.dma_start(w_c[:], io["w_c"][0]).then_inc(w_rest_in, 16)
            sp.dma_start(w_o[:], io["w_o"][0]).then_inc(w_rest_in, 16)
            sp.dma_start(d_vec[:], io["d_vec"]).then_inc(consts_in, 16)
            sp.dma_start(decay[:], io["decay"]).then_inc(consts_in, 16)
            sp.dma_start(ln_g[:], io["tok_ln_g"].unsqueeze(0).to_broadcast([P, LAYERS, D])).then_inc(consts_in, 16)
            sp.dma_start(ln_b[:], io["tok_ln_b"].unsqueeze(0).to_broadcast([P, LAYERS, D])).then_inc(consts_in, 16)
            prefetch(sp)
            with sp.Fori(1, LAYERS) as l:
                sp.wait_ge(xp_full, l * GROUPS * 2 * KI)
                sp.dma_start(w_in[:], io["w_in"][at(l)].rearrange("l p k n -> (l p) k n")).then_inc(w_in_in, 16)
                sp.wait_ge(d_full, l * GROUPS * 2)
                sp.dma_start(w_b[:], io["w_b"][at(l)].rearrange("l p k n -> (l p) k n")).then_inc(w_rest_in, 16)
                sp.dma_start(w_c[:], io["w_c"][at(l)].rearrange("l p n -> (l p) n")).then_inc(w_rest_in, 16)
                sp.dma_start(w_o[:], io["w_o"][at(l)].rearrange("l p k n -> (l p) k n")).then_inc(w_rest_in, 16)

        @block.gpsimd
        def _(pool):
            pool.wait_ge(ids_in, 16)
            for t in range(SEQS):
                pool.indirect_dma_start(res[:, t, :], None, io["emb"], bass.IndirectOffsetOnAxis(
                    ap=ids[:, t:t + 1].bitcast(U32), axis=0)).then_inc(gathered, 16)
            pool.wait_ge(consts_in, 16 * CONSTS)
            pool.wait_ge(gathered, 16 * SEQS)
            for g in range(GROUPS):
                rows = res[:, g * TPG:(g + 1) * TPG, :]
                pool.tensor_tensor(rows, rows, pos[:].unsqueeze(1).to_broadcast([P, TPG, D]),
                                   ALU.add).then_inc(res_ready, 1)

            def step(l, g):
                fin, mid = unit(l, g, 2), unit(l, g, 1)
                if fin:
                    n, lay, grp = fin
                    rows = res[:, grp * TPG:(grp + 1) * TPG, :]
                    pool.drain()
                    if grp == 0:
                        pool.tensor_copy(gain[:, 0:1, :], ln_g[:, at(lay), :])
                        pool.tensor_copy(gain[:, 1:2, :], ln_b[:, at(lay), :])
                        pool.drain()
                    after(pool, xn_ready, n + 1)
                    pool.tensor_tensor(rows, z[:], gain[:, 0:1, :].to_broadcast([P, TPG, D]), ALU.mult)
                    pool.drain()
                    pool.tensor_tensor(rows, rows, gain[:, 1:2, :].to_broadcast([P, TPG, D]),
                                       ALU.add).then_inc(res_ready, 1)
                if mid:
                    n, lay, grp = mid
                    after(pool, gate_done, n * KI + KI)
                    for c in range(KI):
                        after(pool, comb_done, n * KI + c + 1)
                        pool.tensor_tensor(y[:, grp % 2, c, :], y[:, grp % 2, c, :], gate[:, grp % 2, c, :],
                                           ALU.mult).then_inc(y_ready, 1)

            run(pool, step)

        @block.scalar
        def _(act):
            def turn_back(n, grp):
                for kc in range(KD):
                    after(act, t_full, n * KD + kc + 1)
                    act.activation(xT[:, kc, grp * GT:(grp + 1) * GT], t_ps[:], ACT.Copy).then_inc(xT_ready, 1)

            for g in range(GROUPS):
                turn_back(g, g)

            def step(l, g):
                new, mid, fin = unit(l, g, 0), unit(l, g, 1), unit(l, g, 2)
                if mid and not new:
                    n = mid[0]
                    after(act, bu_full, n + 1)
                    after(act, scan_done, n)
                    act.activation(bu[:], b_ps[0:STATE, :], ACT.Copy, scale=INP).then_inc(bu_ready, 1)
                if fin:
                    n = fin[0]
                    after(act, var_ready, n + 1)
                    act.activation(std[:], mv[:, :, 1], ACT.Sqrt, bias=eps[:, 0:1]).then_inc(std_ready, 1)
                if new:
                    n, lay, grp = new
                    after(act, y_ready, (n - 2) * KI + KI)
                    for m in range(KI):
                        after(act, xp_full, n * 2 * KI + 2 * m + 2)
                        act.activation(gate[:, grp % 2, m, :], xp_ps[:, 1, :], ACT.Silu).then_inc(gate_done, 1)
                        if m == 0 and mid:
                            after(act, bu_full, mid[0] + 1)
                            after(act, scan_done, mid[0])
                            act.activation(bu[:], b_ps[0:STATE, :], ACT.Copy, scale=INP).then_inc(bu_ready, 1)
                        after(act, conv_done, n * KI + m + 1)
                        act.activation(u[:, grp % 2, m, :], u[:, grp % 2, m, :], ACT.Silu).then_inc(u_ready, 1)
                if fin:
                    turn_back(fin[0] + GROUPS, fin[2])

            run(act, step)

        @block.vector
        def _(dve):
            dve.wait_ge(consts_in, 16 * CONSTS)

            def conv(new, m):
                dve.drain()
                n, lay, grp = new
                after(dve, xp_full, n * 2 * KI + 2 * m + 1)
                acc = u[:, grp % 2, m, :].rearrange("p (s t) -> p s t", s=TPG)
                xin = xp_ps[:, 0, :].rearrange("p (s t) -> p s t", s=TPG)
                w = lambda tap: conv_w[:, at(lay), m, tap]
                dve.tensor_scalar(u[:, grp % 2, m, :], xp_ps[:, 0, :], w(TAPS - 1), conv_b[:, at(lay), m],
                                  ALU.mult, ALU.add)
                for back in range(1, TAPS):
                    dve.drain()
                    last = dve.scalar_tensor_tensor(acc[:, :, back:], xin[:, :, :TOK - back], w(TAPS - 1 - back),
                                                    acc[:, :, back:], ALU.mult, ALU.add)
                last.then_inc(conv_done, 1)

            def combine(mid, cs):
                n, lay, grp = mid
                for c in cs:
                    dve.drain()
                    after(dve, u_ready, n * KI + KI)
                    after(dve, c_full, n * KI + c + 1)
                    dve.scalar_tensor_tensor(y[:, grp % 2, c, :], u[:, grp % 2, c, :], d_vec[:, at(lay), c],
                                             c_ps[:, c % 2, :], ALU.mult, ALU.add).then_inc(comb_done, 1)

            def step(l, g):
                new, mid, fin = unit(l, g, 0), unit(l, g, 1), unit(l, g, 2)
                if new:
                    conv(new, 0)
                if fin:
                    n, lay, grp = fin
                    for b in range(2):
                        dve.drain()
                        if b == 0:
                            after(dve, res_ready, GROUPS + n)
                        after(dve, d_full, n * 2 + b + 1)
                        dve.tensor_tensor(z[:, 2 * b:2 * b + 2, :], d_ps[:, b, :].rearrange("p (j d) -> p j d", j=2),
                                          res[:, grp * TPG + 2 * b:grp * TPG + 2 * b + 2, :],
                                          ALU.add).then_inc(z_done, 1)
                    dve.drain()
                    for j in range(TPG):
                        dve.bn_stats(stats[:, j, :], z[:, j, :])
                    dve.drain()
                    for j in range(TPG):
                        last = dve.bn_aggr(mv[:, j, :], stats[:, j, :])
                    last.then_inc(var_ready, 1)
                if mid:
                    n = mid[0]
                    dve.drain()
                    after(dve, bu_ready, n + 1)
                    dve.tensor_tensor_scan(state[:], decay[:], bu[:], 0.0, ALU.mult, ALU.add).then_inc(scan_done, 1)
                if new:
                    conv(new, 1)
                if fin:
                    dve.drain()
                    n, lay, grp = fin
                    after(dve, std_ready, n + 1)
                    dve.reciprocal(rstd[:], std[:])
                    dve.drain()
                    for j in range(TPG):
                        last = dve.tensor_scalar(z[:, j, :], z[:, j, :], mv[:, j, 0:1], rstd[:, j:j + 1],
                                                 ALU.subtract, ALU.mult)
                    last.then_inc(xn_ready, 1)
                if mid:
                    combine(mid, (0, 1))
                if new:
                    conv(new, 2)
                if mid:
                    combine(mid, (2, 3))
                if new:
                    conv(new, 3)

            run(dve, step)

        @block.tensor
        def _(pe):
            def turn(n, grp, kc):
                after(pe, res_ready, n + 1)
                after(pe, xT_ready, n * KD + kc)
                for j in range(TPG):
                    last = pe.transpose(t_ps[:, j * TOK:(j + 1) * TOK],
                                        res[:, grp * TPG + j, kc * P:(kc + 1) * P], ident[:])
                last.then_inc(t_full, 1)

            for g in range(GROUPS):
                for kc in range(KD):
                    turn(g, g, kc)

            def project_in(new, m):
                n, lay, grp = new
                if m == 0:
                    after(pe, w_in_in, (lay + 1) * 16)
                    after(pe, xT_ready, (n + 1) * KD)
                gated = m >= KI
                after(pe, gate_done if gated else conv_done, n * KI + m % KI)
                for kc in range(KD):
                    last = pe.matmul(xp_ps[:, int(gated), :], w_in[:, kc, m * P:(m + 1) * P],
                                     xT[:, kc, grp * GT:(grp + 1) * GT], start=(kc == 0), stop=(kc == KD - 1))
                last.then_inc(xp_full, 1)

            def mix(mid, cs):
                n, lay, grp = mid
                for c in cs:
                    after(pe, comb_done, n * KI + c - 1)
                    pe.matmul(c_ps[:, c % 2, :], w_c[:, c * P:(c + 1) * P], state[:], start=True,
                              stop=True).then_inc(c_full, 1)

            def step(l, g):
                new, mid, fin = unit(l, g, 0), unit(l, g, 1), unit(l, g, 2)
                if new:
                    project_in(new, 0)
                    project_in(new, KI + 0)
                if mid:
                    n, lay, grp = mid
                    after(pe, w_rest_in, (lay + 1) * 48)
                    after(pe, u_ready, n * KI + KI)
                    after(pe, bu_ready, n)
                    for c in range(KI):
                        last = pe.matmul(b_ps[0:STATE, :], w_b[:, c, :], u[:, grp % 2, c, :],
                                         start=(c == 0), stop=(c == KI - 1))
                    last.then_inc(bu_full, 1)
                if new:
                    project_in(new, 1)
                    project_in(new, KI + 1)
                if mid:
                    after(pe, scan_done, mid[0] + 1)
                    mix(mid, (0, 1))
                if new:
                    project_in(new, 2)
                    project_in(new, KI + 2)
                if mid:
                    mix(mid, (2, 3))
                if new:
                    project_in(new, 3)
                    project_in(new, KI + 3)
                for b in range(2):
                    if fin:
                        turn(fin[0] + GROUPS, fin[2], b)
                    if mid:
                        n, lay, grp = mid
                        after(pe, y_ready, n * KI + KI)
                        after(pe, z_done, (n - 1) * 2 + b + 1)
                        for j in (2 * b, 2 * b + 1):
                            for c in range(KI):
                                last = pe.matmul(d_ps[:, b, (j % 2) * D:(j % 2 + 1) * D],
                                                 y[:, grp % 2, c, j * TOK:(j + 1) * TOK], w_o[:, c, :],
                                                 start=(c == 0), stop=(c == KI - 1))
                        last.then_inc(d_full, 1)

            run(pe, step)


def attention_stage(nc, sems, io, res, ident, eps, name, hd, w_qkv, w_out, weights_in, weights_count,
                    rope=None, qkv_bias=None, out_bias=None, mask_dram=None, onto=None, prefetch=None):
    k = Kit(nc, sems)
    inner = HEADS * hd
    pad = 64 if hd == 64 else 32
    half = hd // 2
    hpc = P // pad
    nch = HEADS // hpc
    no = inner // P
    qk_slices = 2 * inner // BANK
    vw = min(inner, BANK)
    v_slices = inner // vw
    nq = qk_slices + v_slices
    hps = 2 * HEADS // qk_slices
    vh = HEADS // v_slices
    nb, hb = 4, HEADS // 4
    scale = hd ** -0.5
    UNROLL = 4
    BACK = {"q": 0, "qk": 1, "s": 1, "probs": 2, "av": 2, "out": 3, "proj": 3, "norm": -1}
    if hd == 64:
        PE_ORDER = [("qk", 0), ("probs", 0), ("q", 0), ("qk", 1), ("probs", 1), ("q", 1), ("av", 0), ("qk", 2),
                    ("probs", 2), ("q", 2), ("av", 1), ("qk", 3), ("probs", 3), ("q", 3), ("av", 2), ("s", 0),
                    ("q", 4), ("av", 3), ("s", 1), ("q", 5), ("out", 0), ("s", 2), ("out", 1), ("norm", 0),
                    ("s", 3), ("proj", 0)]
        ACT_ORDER = [("qk", 0), ("probs", 0), ("qk", 1), ("probs", 1), ("qk", 2), ("probs", 2), ("qk", 3),
                     ("probs", 3), ("v", 0), ("exp", 0), ("v", 1), ("out", 0), ("exp", 1), ("out", 1), ("norm", 0),
                     ("exp", 2), ("exp", 3)]
        DVE_ORDER = [("xs", 0), ("q", 0), ("q", 1), ("av", 0), ("q", 2), ("av", 1), ("q", 3), ("av", 2), ("s", 0),
                     ("av", 3), ("s", 1), ("s", 2), ("s", 3), ("proj", 0)]
    else:
        PE_ORDER = [("qk", 0), ("probs", 0), ("qk", 1), ("probs", 1), ("av", 0), ("s", 0), ("probs", 2), ("av", 1),
                    ("s", 1), ("probs", 3), ("av", 2), ("q", 0), ("s", 2), ("av", 3), ("q", 1), ("out", 0),
                    ("s", 3), ("norm", 0), ("proj", 0)]
        ACT_ORDER = [("qk", 0), ("probs", 0), ("qk", 1), ("probs", 1), ("probs", 2), ("exp", 0), ("probs", 3),
                     ("exp", 1), ("v", 0), ("out", 0), ("exp", 2), ("norm", 0), ("exp", 3)]
        DVE_ORDER = [("xs", 0), ("av", 0), ("s", 0), ("av", 1), ("s", 1), ("av", 2), ("q", 0), ("s", 2), ("av", 3),
                     ("v", 0), ("s", 3), ("proj", 0)]
    TR = [u for u in PE_ORDER if u[0] in ("qk", "probs", "out", "norm")]
    AV = [u for u in PE_ORDER if u[0] in ("av", "proj")]

    def ring_count(ring, s, phase, i):
        if isinstance(s, int):
            before = sum(min(max(s - BACK[p], 0), SEQS) for p, _ in ring)
        else:
            before = s * len(ring) - sum(BACK[p] for p, _ in ring)
        n = ring.index((phase, i))
        return before + 1 + sum(1 for p, _ in ring[:n] if not isinstance(s, int) or 0 <= s - BACK[p] < SEQS)

    with k.mem:
        xs = k.sb(name + "xs", [P, D])
        xT = k.sb(name + "xT", [P, KD, TOK])
        qk = k.sb(name + "qk", [P, 2, 2 * HEADS, pad])
        vals = k.sb(name + "vals", [P, UNROLL, HEADS, hd + 1])
        qkT = k.sb(name + "qkT", [P, 2, nch, TOK])
        probs = k.sb(name + "probs", [P, 2, HEADS, TOK])
        pT = k.sb(name + "pT", [P, HEADS, TOK])
        heads = k.sb(name + "heads", [P, 2, HEADS, hd])
        oT = k.sb(name + "oT", [P, no, TOK])
        top = k.sb(name + "top", [P, hb])
        rsum = k.sb(name + "rsum", [P, hb])
        stats = k.sb(name + "stats", [P, SEQS, 6])
        mv = k.sb(name + "mv", [P, SEQS, 2])
        std = k.sb(name + "std", [P, SEQS])
        rstd = k.sb(name + "rstd", [P, SEQS])
        if rope:
            cos = k.sb(name + "cos", [P, half])
            sin = k.sb(name + "sin", [P, half])
            nsin = k.sb(name + "nsin", [P, half])
            turned = k.sb(name + "turned", [P, 2, hps, 2, half])
        if qkv_bias is not None:
            bias = k.sb(name + "bias", [P, 3 * inner])
        if out_bias is not None:
            bias_o = k.sb(name + "bias_o", [P, D])
            part = k.sb(name + "part", [P, D])
        if mask_dram is not None:
            mask = k.sb(name + "mask", [P, TOK])
        q_ps = k.ps(name + "q_ps", [P, 2, BANK])
        tr_ps = k.ps(name + "tr_ps", [P, 2, BANK])
        s_ps = k.ps(name + "s_ps", [P, 2, BANK])
        av_ps = k.ps(name + "av_ps", [P, 2, BANK])

        S = lambda n: k.sem(name + n)
        consts_in = S("consts_in")
        set_up, var_ready, std_ready, xs_ready = S("set_up"), S("var_ready"), S("std_ready"), S("xs_ready")
        q_full, qk_taken, qk_ready, v_taken = S("q_full"), S("qk_taken"), S("qk_ready"), S("v_taken")
        tr_full, tr_taken = S("tr_full"), S("tr_taken")
        s_full, s_taken, p_ready = S("s_full"), S("s_taken"), S("p_ready")
        av_full, av_taken = S("av_full"), S("av_taken")
        n_consts = 3 * bool(rope) + (qkv_bias is not None) + (out_bias is not None) + (mask_dram is not None)
        qk_done = qk_ready if rope else qk_taken
        v_on_dve = qkv_bias is not None

        def tile(s, back):
            t = s - back
            return None if isinstance(s, int) and not 0 <= t < SEQS else t

        def run(eng, step):
            for s in range(-1, UNROLL - 1):
                step(s, s)
            with eng.Fori(1, SEQS // UNROLL) as i:
                for j in range(UNROLL):
                    step(i * UNROLL + (j - 1), (j - 1) % UNROLL)
            for s in range(SEQS - 1, SEQS + 3):
                step(s, s)

        block = k.mem.enter_context(nc.Block())

        @block.sync
        def _(sp):
            if rope:
                sp.dma_start(cos[:], rope[0]).then_inc(consts_in, 16)
                sp.dma_start(sin[:], rope[1]).then_inc(consts_in, 16)
                sp.dma_start(nsin[:], rope[2]).then_inc(consts_in, 16)
            if qkv_bias is not None:
                sp.dma_start(bias[:], qkv_bias.to_broadcast([P, 3 * inner])).then_inc(consts_in, 16)
            if out_bias is not None:
                sp.dma_start(bias_o[:], out_bias.to_broadcast([P, D])).then_inc(consts_in, 16)
            if mask_dram is not None:
                sp.dma_start(mask[:], mask_dram).then_inc(consts_in, 16)
            if prefetch is not None:
                prefetch(sp)

        def head_batch(view, b):
            if hpc == 2:
                return view.rearrange("p (a c two) d -> p a two c d", a=2, two=2)[:, b // 2, b % 2]
            return view.rearrange("p (c j) d -> p j c d", j=4)[:, b]

        def heads_of(b):
            return [(b // 2) * 8 + b % 2 + 2 * c for c in range(hb)] if hpc == 2 else [4 * c + b for c in range(hb)]

        def place(ring, s, j, phase, i):
            return (ring_count(ring, s if isinstance(s, int) else UNROLL + j, phase, i) - 1) % 2

        def qk_view(t, j0, h0, n):
            return qk[:, j0 % 2, h0:h0 + n, 0:hd]

        @block.gpsimd
        def _(pool):
            pool.memset(vals[:, :, :, hd:hd + 1], 1.0)
            pool.memset(qk[:], 0.0).then_inc(set_up, 1)

            def step(s, j):
                t = tile(s, 0)
                if t is not None and rope:
                    for i in range(qk_slices):
                        pool.drain()
                        after(pool, qk_taken, t * qk_slices + i + 1)
                        out = qk_view(t, j, i * hps, hps)
                        pool.tensor_tensor(out, out, turned[:, i % 2].rearrange("p h a d -> p h (a d)"),
                                           ALU.add).then_inc(qk_ready, 1)

            run(pool, step)

        @block.scalar
        def _(act):
            def copy_back(s, j, phase, i, out, width):
                at_ = ring_count(TR, s, phase, i)
                after(act, tr_full, at_)
                act.activation(out, tr_ps[:, place(TR, s, j, phase, i), 0:width],
                               ACT.Copy).then_inc(tr_taken, 1)

            act.wait_ge(set_up, 1)
            act.wait_ge(var_ready, 1)
            act.activation(std[:], mv[:, :, 1], ACT.Sqrt, bias=eps[:, 0:1]).then_inc(std_ready, 1)

            def step(s, j):
                for what, i in ACT_ORDER:
                    t = tile(s, BACK[{"v": "q", "exp": "s"}.get(what, what)])
                    if t is None:
                        continue
                    if what == "v" and not v_on_dve:
                        after(act, q_full, t * nq + qk_slices + i + 1)
                        act.activation(vals[:, j % UNROLL, i * vh:(i + 1) * vh, 0:hd],
                                       q_ps[:, (qk_slices + i) % 2, 0:vw].rearrange("p (h d) -> p h d", d=hd),
                                       ACT.Copy).then_inc(v_taken, 1)
                    if what == "exp":
                        after(act, s_taken, t * nb + i + 1)
                        rows = probs[:, (j - 1) % 2, i * hb:(i + 1) * hb, :]
                        act.activation(rows, rows, ACT.Exp, scale=scale).then_inc(p_ready, 1)
                    if what == "qk":
                        flat = qkT[:].rearrange("p a c t -> p (a c t)")
                        copy_back(s, j, "qk", i, flat[:, i * BANK:(i + 1) * BANK], BANK)
                    if what == "probs":
                        copy_back(s, j, "probs", i, pT[:, i * hb:(i + 1) * hb, :].rearrange("p h t -> p (h t)"), BANK)
                    if what == "out":
                        w = min(4, no) * TOK
                        copy_back(s, j, "out", i, oT[:, 4 * i:4 * i + min(4, no), :].rearrange("p c t -> p (c t)"), w)
                    if what == "norm":
                        copy_back(s, j, "norm", 0, xT[:].rearrange("p c t -> p (c t)"), KD * TOK)

            run(act, step)

        @block.vector
        def _(dve):
            dve.wait_ge(consts_in, 16 * n_consts)
            dve.wait_ge(set_up, 1)

            def rotate(t, j, i):
                x = q_ps[:, i % 2, :].rearrange("p (h a d) -> p h a d", h=hps, a=2)
                out = qk_view(t, j, i * hps, hps).rearrange("p h (a d) -> p h a d", a=2)
                wide = lambda c: c[:].unsqueeze(1).to_broadcast([P, hps, half])
                both = cos[:].unsqueeze(1).unsqueeze(1).to_broadcast([P, hps, 2, half])
                after(dve, qk_ready, t * qk_slices + i + 1 - min(qk_slices, 2))
                dve.tensor_tensor(out, x, both, ALU.mult)
                dve.tensor_tensor(turned[:, i % 2, :, 0, :], x[:, :, 1, :], wide(nsin), ALU.mult)
                dve.tensor_tensor(turned[:, i % 2, :, 1, :], x[:, :, 0, :], wide(sin),
                                  ALU.mult).then_inc(qk_taken, 1)

            for t in range(SEQS):
                dve.bn_stats(stats[:, t, :], res[:, t, :])
            dve.drain()
            for t in range(SEQS):
                last = dve.bn_aggr(mv[:, t, :], stats[:, t, :])
            last.then_inc(var_ready, 1)
            dve.wait_ge(std_ready, 1)
            dve.reciprocal(rstd[:], std[:])

            def slice_qk(t, s, j, i):
                after(dve, q_full, t * nq + i + 1)
                if rope:
                    rotate(t, j, i)
                else:
                    dve.tensor_tensor(qk_view(t, j, i * hps, hps),
                                      q_ps[:, i % 2, :].rearrange("p (h d) -> p h d", d=hd),
                                      bias[:, i * BANK:(i + 1) * BANK].rearrange("p (h d) -> p h d", d=hd),
                                      ALU.add).then_inc(qk_taken, 1)

            def slice_v(t, s, j, i):
                if v_on_dve:
                    after(dve, q_full, t * nq + qk_slices + i + 1)
                    dve.tensor_tensor(
                        vals[:, j % UNROLL, i * vh:(i + 1) * vh, 0:hd],
                        q_ps[:, (qk_slices + i) % 2, 0:vw].rearrange("p (h d) -> p h d", d=hd),
                        bias[:, 2 * inner + i * vw:2 * inner + (i + 1) * vw].rearrange("p (h d) -> p h d", d=hd),
                        ALU.add).then_inc(v_taken, 1)

            def softmax_in(t, s, j, b):
                after(dve, s_full, t * nb + b + 1)
                rows = probs[:, (j - 1) % 2, b * hb:(b + 1) * hb, :]
                sc = s_ps[:, b % 2, :].rearrange("p (h t) -> p h t", h=hb)
                if mask_dram is not None:
                    dve.tensor_tensor(rows, sc, mask[:].unsqueeze(1).to_broadcast([P, hb, TOK]), ALU.add)
                    sc = rows
                    dve.drain()
                dve.tensor_reduce(top[:], sc, AX_X, ALU.max)
                dve.drain()
                dve.tensor_tensor(rows, sc, top[:].unsqueeze(2).to_broadcast([P, hb, TOK]),
                                  ALU.subtract).then_inc(s_taken, 1)

            def heads_out(t, s, j, b):
                after(dve, av_full, ring_count(AV, s, "av", b))
                o = av_ps[:, place(AV, s, j, "av", b), 0:hb * (hd + 1)].rearrange("p (h e) -> p h e", h=hb)
                dve.reciprocal(rsum[:], o[:, :, hd])
                dve.drain()
                dve.tensor_tensor(head_batch(heads[:, (j - 2) % 2], b), o[:, :, 0:hd],
                                  rsum[:].unsqueeze(2).to_broadcast([P, hb, hd]), ALU.mult).then_inc(av_taken, 1)

            def project_out(t, s, j, i):
                row = res[:, at(t), :].rearrange("p o d -> p (o d)")
                if onto is not None:
                    src = onto[:, at(t), :].rearrange("p o d -> p (o d)")
                    dve.tensor_scalar(src, row, mv[:, at(t), 0], rstd[:, at(t)], ALU.subtract, ALU.mult)
                    row = src
                o = av_ps[:, place(AV, s, j, "proj", 0), 0:D]
                after(dve, av_full, ring_count(AV, s, "proj", 0))
                if out_bias is not None:
                    dve.tensor_tensor(part[:], o, bias_o[:], ALU.add).then_inc(av_taken, 1)
                    dve.drain()
                    dve.tensor_tensor(row, row, part[:], ALU.add)
                else:
                    dve.tensor_tensor(row, row, o, ALU.add).then_inc(av_taken, 1)

            def norm_next(t, s, j, i):
                row = res[:, at(t), :].rearrange("p o d -> p (o d)")
                if not isinstance(s, int) or s >= 0:
                    after(dve, tr_full, ring_count(TR, s - 1, "norm", 0))
                dve.tensor_scalar(xs[:], row, mv[:, at(t), 0], rstd[:, at(t)],
                                  ALU.subtract, ALU.mult).then_inc(xs_ready, 1)

            WORK = {"q": (slice_qk, "q"), "v": (slice_v, "q"), "s": (softmax_in, "s"), "av": (heads_out, "av"),
                    "proj": (project_out, "proj"), "xs": (norm_next, "norm")}

            def step(s, j):
                for what, i in DVE_ORDER:
                    work, kind = WORK[what]
                    t = tile(s, BACK[kind])
                    if t is not None:
                        dve.drain()
                        work(t, s, j, i)

            run(dve, step)

        @block.tensor
        def _(pe):
            pe.wait_ge(set_up, 1)
            pe.wait_ge(weights_in, weights_count)

            def turn(s, j, phase, i, blocks):
                at_ = ring_count(TR, s, phase, i)
                after(pe, tr_taken, at_ - 2)
                for n, blk in enumerate(blocks):
                    last = pe.transpose(tr_ps[:, place(TR, s, j, phase, i), n * TOK:(n + 1) * TOK],
                                        blk, ident[:])
                last.then_inc(tr_full, 1)

            def project(t, s, j, i):
                if i == 0:
                    after(pe, tr_taken, ring_count(TR, s - 1, "norm", 0))
                prev, owner = (i - 2, t) if i >= 2 else (i - 2 + nq, t - 1)
                if prev < qk_slices:
                    after(pe, qk_taken, owner * qk_slices + prev + 1)
                else:
                    after(pe, v_taken, owner * v_slices + prev - qk_slices + 1)
                width = BANK if i < qk_slices else vw
                for kc in range(KD):
                    last = pe.matmul(q_ps[:, i % 2, 0:width], xT[:, kc, :], w_qkv[:, kc, i * BANK:i * BANK + width],
                                     start=(kc == 0), stop=(kc == KD - 1))
                last.then_inc(q_full, 1)

            def turn_qk(t, s, j, i):
                after(pe, qk_done, (t + 1) * qk_slices)
                flat = qk[:, (j - 1) % 2].rearrange("p h d -> p (h d)")
                turn(s, j, "qk", i, [flat[:, (4 * i + n) * P:(4 * i + n + 1) * P] for n in range(4)])

            def score(t, s, j, b):
                after(pe, tr_taken, ring_count(TR, s, "qk", 2 * nch // 4 - 1))
                after(pe, s_taken, t * nb + b - 1)
                for n, h in enumerate(heads_of(b)):
                    r = (h % hpc) * pad
                    last = pe.matmul(s_ps[:, b % 2, n * TOK:(n + 1) * TOK], qkT[r:r + hd, 0, h // hpc, :],
                                     qkT[r:r + hd, 1, h // hpc, :], start=True, stop=True)
                last.then_inc(s_full, 1)

            def turn_probs(t, s, j, b):
                after(pe, p_ready, t * nb + b + 1)
                turn(s, j, "probs", b, [probs[:, (j - 2) % 2, b * hb + n, :] for n in range(hb)])

            def weigh(t, s, j, b):
                after(pe, v_taken, (t + 1) * v_slices)
                after(pe, tr_taken, ring_count(TR, s, "probs", b))
                after(pe, av_taken, ring_count(AV, s, "av", b) - 2)
                for n, h in enumerate(heads_of(b)):
                    last = pe.matmul(av_ps[:, place(AV, s, j, "av", b), n * (hd + 1):(n + 1) * (hd + 1)],
                                     pT[:, b * hb + n, :], vals[:, (j - 2) % UNROLL, h, :], start=True, stop=True)
                last.then_inc(av_full, 1)

            def turn_heads(t, s, j, i):
                after(pe, av_taken, ring_count(AV, s - 1, "av", nb - 1))
                flat = heads[:, (j - 3) % 2].rearrange("p h d -> p (h d)")
                turn(s, j, "out", i, [flat[:, c * P:(c + 1) * P] for c in range(4 * i, min(4 * i + 4, no))])

            def project_out(t, s, j, i):
                after(pe, tr_taken, ring_count(TR, s, "out", -(-no // 4) - 1))
                after(pe, av_taken, ring_count(AV, s, "proj", 0) - 2)
                for c in range(no):
                    last = pe.matmul(av_ps[:, place(AV, s, j, "proj", 0), 0:D], oT[:, c, :], w_out[:, c, :],
                                     start=(c == 0), stop=(c == no - 1))
                last.then_inc(av_full, 1)

            def turn_norm(t, s, j, i):
                after(pe, xs_ready, t + 1)
                turn(s, j, "norm", 0, [xs[:, c * P:(c + 1) * P] for c in range(KD)])

            WORK = {"q": project, "qk": turn_qk, "s": score, "probs": turn_probs, "av": weigh, "out": turn_heads,
                    "proj": project_out, "norm": turn_norm}

            def step(s, j):
                for what, i in PE_ORDER:
                    t = tile(s, BACK[what])
                    if t is not None:
                        WORK[what](t, s, j, i)

            run(pe, step)


def load_expert(sp, io, name, store, e, par, biased):
    w_up, w_dn, b_up, w_in = store
    up, dn = io[name + "up"][at(e)], io[name + "dn"][at(e)]
    chunks = dn.shape[2]
    sp.dma_start(w_up[:, par], up.rearrange("e p k n -> (e p) k n")).then_inc(w_in[par], 16)
    sp.dma_start(w_dn[:, par, 0:chunks], dn.rearrange("e p k n -> (e p) k n")).then_inc(w_in[par], 16)
    if biased:
        b = io[name + "b_up"][at(e)]
        sp.dma_start(b_up[:, par], b.rearrange("e p c -> (e p) c")).then_inc(w_in[par], 16)


def experts_stage(nc, sems, io, res, ident, eps, name, n_exp, n_routed, chunks, gated, acc, store, out=None):
    k = Kit(nc, sems)
    E, R = n_exp, n_routed
    w_up, w_dn, b_up, w_in = store
    NUP = 4
    UNITS = E * GROUPS
    with k.mem:
        xT = k.sb(name + "xT", [P, KD, SEQS * TOK])
        h = k.sb(name + "h", [P, 2, chunks, GT])
        router = k.sb(name + "router", [P, KD, R])
        r_bias = k.sb(name + "r_bias", [P, R])
        xn = k.sb(name + "xn", [P, TPG, D])
        stats = k.sb(name + "stats", [P, TPG, 6])
        mv = k.sb(name + "mv", [P, TPG, 2])
        std = k.sb(name + "std", [P, TPG])
        rstd = k.sb(name + "rstd", [P, TPG])
        score = k.sb(name + "score", [P, SEQS, R])
        choice = k.sb(name + "choice", [P, SEQS, R])
        rank = k.sb(name + "rank", [P, SEQS, R])
        lt = k.sb(name + "lt", [P, 4, 4] if gated else [P, R, R])
        greater = k.sb(name + "greater", [P, SEQS * 64])
        equal = k.sb(name + "equal", [P, SEQS * 64])
        total = k.sb(name + "total", [P, SEQS])
        weight = k.sb(name + "weight", [P, SEQS, E])
        if gated:
            silu = k.sb(name + "silu", [P, chunks, GT])
            group = k.sb(name + "group", [P, SEQS, 4])
            best = k.sb(name + "best", [P, SEQS, 8])
            above = k.sb(name + "above", [P, SEQS, R])
            level = k.sb(name + "level", [P, SEQS, R])
            going = k.sb(name + "going", [P, SEQS, R])
            g_rank = k.sb(name + "g_rank", [P, SEQS, 4])
        else:
            b_dn = k.sb(name + "b_dn", [E, D])
            wT = k.sb(name + "wT", [E, SEQS * TOK])
            ln = k.sb(name + "ln", [P, 4, D])
        up_ps = k.ps(name + "up_ps", [P, 4, BANK])
        dn_ps = k.ps(name + "dn_ps", [P, 4, BANK])

        S = lambda n: k.sem(name + n)
        consts_in = S("consts_in")
        var_ready, std_ready, xn_ready, x_ready = S("var_ready"), S("std_ready"), S("xn_ready"), S("x_ready")
        t_full, xT_ready, r_full = S("t_full"), S("xT_ready"), S("r_full")
        score_in, score_out, weights_ready = S("score_in"), S("score_out"), S("weights_ready")
        up_full, silu_ready, h_ready = S("up_full"), S("silu_ready"), S("h_ready")
        dn_full, acc_done = S("dn_full"), S("acc_done")
        wT_full, wT_ready, bias_full, bias_done = S("wT_full"), S("wT_ready"), S("bias_full"), S("bias_done")
        var2_ready, std2_ready, xn2_ready, stored = S("var2_ready"), S("std2_ready"), S("xn2_ready"), S("stored")
        n_consts = 3 if gated else 8
        PER_EXPERT = 32 if gated else 48

        def run(eng, step):
            for par in range(2):
                for g in range(GROUPS):
                    step(par * GROUPS + g, par, par, g)
            with eng.Fori(1, E // 2) as i:
                for par in range(2):
                    for g in range(GROUPS):
                        step(i * 2 * GROUPS + par * GROUPS + g, i * 2 + par, par, g)
            step(UNITS, None, 0, 0)

        def before(n, e, par, g):
            if isinstance(n, int) and n == 0:
                return None
            if e is None:
                return n - 1, E - 1, 1, GROUPS - 1
            return (n - 1, e, par, g - 1) if g else (n - 1, e - 1, 1 - par, GROUPS - 1)

        block = k.mem.enter_context(nc.Block())

        @block.sync
        def _(sp):
            sp.dma_start(router[:], io[name + "router"]).then_inc(consts_in, 16)
            sp.dma_start(r_bias[:], io[name + "r_bias"].to_broadcast([P, R])).then_inc(consts_in, 16)
            sp.dma_start(lt[:], io["lt%d" % lt.shape[1]]).then_inc(consts_in, 16)
            if not gated:
                sp.dma_start(b_dn[:], io[name + "b_dn"]).then_inc(consts_in, 16)
                for n, key in enumerate(("ln1_g", "ln1_b", "ln2_g", "ln2_b")):
                    sp.dma_start(ln[:, n, :], io[name + key].to_broadcast([P, D])).then_inc(consts_in, 16)
            with sp.Fori(1, E // 2) as i:
                for par in range(2):
                    sp.wait_ge(dn_full, i * 16 + (8 * par - 8))
                    load_expert(sp, io, name, store, i * 2 + par, par, not gated)
            if out is not None:
                for g in range(GROUPS):
                    sp.wait_ge(acc_done, 2 * (UNITS - GROUPS + g + 1))
                    sp.dma_start(out.rearrange("(t p) d -> p t d", p=P)[:, g * TPG:(g + 1) * TPG, :],
                                 acc[:, g * TPG:(g + 1) * TPG, :]).then_inc(stored, 16)
                sp.wait_ge(stored, 16 * GROUPS)

        def scaled(n):
            return ln[:, n:n + 1, :].to_broadcast([P, TPG, D])

        if not gated:
            @block.gpsimd
            def _(pool):
                pool.wait_ge(consts_in, 16 * n_consts)
                for g in range(GROUPS):
                    pool.drain()
                    rows = acc[:, g * TPG:(g + 1) * TPG, :]
                    pool.wait_ge(xn_ready, g + 1)
                    pool.tensor_tensor(rows, xn[:], scaled(0), ALU.mult)
                    pool.drain()
                    pool.tensor_tensor(rows, rows, scaled(1), ALU.add).then_inc(x_ready, 1)
                for g in range(GROUPS):
                    pool.drain()
                    rows = res[:, g * TPG:(g + 1) * TPG, :]
                    pool.wait_ge(xn2_ready, g + 1)
                    pool.tensor_tensor(xn[:], xn[:], scaled(2), ALU.mult)
                    pool.drain()
                    pool.tensor_tensor(xn[:], xn[:], scaled(3), ALU.add)
                    pool.drain()
                    pool.tensor_tensor(rows, rows, xn[:], ALU.add).then_inc(x_ready, 1)

        @block.scalar
        def _(act):
            act.wait_ge(consts_in, 16 * n_consts)
            for g in range(GROUPS):
                act.wait_ge(var_ready, g + 1)
                act.activation(std[:], mv[:, :, 1], ACT.Sqrt, bias=eps[:, 0:1]).then_inc(std_ready, 1)
                for kc in range(KD):
                    act.wait_ge(t_full, g * KD + kc + 1)
                    act.activation(xT[:, kc, g * GT:(g + 1) * GT], up_ps[:, kc, :], ACT.Copy).then_inc(xT_ready, 1)
            if gated:
                act.wait_ge(r_full, 1)
                act.activation(score[:], up_ps[:, 2, 0:SEQS * R].rearrange("p (t r) -> p t r", r=R),
                               ACT.Sigmoid).then_inc(score_out, 1)
            else:
                act.wait_ge(score_in, 1)
                act.activation(score[:], score[:], ACT.Exp).then_inc(score_out, 1)

            def step(n, e, par, g):
                if e is None:
                    return
                for f in range(chunks):
                    if gated:
                        after(act, up_full, n * 4 + 2 * f + 1)
                        after(act, h_ready, (n - 1) * chunks + f + 1)
                        act.activation(silu[:, f, :], up_ps[:, 2 * f, :], ACT.Silu).then_inc(silu_ready, 1)
                    else:
                        after(act, up_full, n * 4 + f + 1)
                        act.activation(h[:, g % 2, f, :], up_ps[:, f, :], ACT.Relu,
                                       bias=b_up[:, par, f:f + 1]).then_inc(h_ready, 1)

            run(act, step)
            if not gated:
                for g in range(GROUPS):
                    act.wait_ge(wT_full, g + 1)
                    act.activation(wT[:, g * GT:(g + 1) * GT], up_ps[0:E, g, :], ACT.Copy).then_inc(wT_ready, 1)
                for g in range(GROUPS):
                    act.wait_ge(var2_ready, g + 1)
                    act.activation(std[:], mv[:, :, 1], ACT.Sqrt, bias=eps[:, 0:1]).then_inc(std2_ready, 1)

        @block.vector
        def _(dve):
            dve.wait_ge(consts_in, 16 * n_consts)

            def norm(g, var, stdr, xnr, xn_free, count):
                rows = acc[:, g * TPG:(g + 1) * TPG, :]
                dve.drain()
                for j in range(TPG):
                    dve.bn_stats(stats[:, j, :], rows[:, j, :])
                dve.drain()
                for j in range(TPG):
                    last = dve.bn_aggr(mv[:, j, :], stats[:, j, :])
                last.then_inc(var, 1)
                dve.wait_ge(stdr, g + 1)
                dve.reciprocal(rstd[:], std[:])
                dve.drain()
                after(dve, xn_free, count)
                for j in range(TPG):
                    last = dve.tensor_scalar(xn[:, j, :], rows[:, j, :], mv[:, j, 0:1], rstd[:, j:j + 1],
                                             ALU.subtract, ALU.mult)
                last.then_inc(xnr, 1)

            def ranks(values, out_rank, tri, groups, n):
                shape = [P, groups, n, n]
                g4 = greater[:, 0:groups * n * n].rearrange("p (g e j) -> p g e j", e=n, j=n)
                e4 = equal[:, 0:groups * n * n].rearrange("p (g e j) -> p g e j", e=n, j=n)
                other = values.unsqueeze(2).to_broadcast(shape)
                own = values.unsqueeze(3).to_broadcast(shape)
                dve.drain()
                dve.tensor_tensor(g4, other, own, ALU.is_gt)
                dve.tensor_tensor(e4, other, own, ALU.is_equal)
                dve.drain()
                dve.tensor_tensor(e4, e4, tri[:].unsqueeze(1).to_broadcast(shape), ALU.mult)
                dve.drain()
                dve.tensor_tensor(g4, g4, e4, ALU.add)
                dve.drain()
                dve.tensor_reduce(out_rank, g4, AX_X, ALU.add)
                dve.drain()

            def wide(t, n):
                return t.unsqueeze(2).to_broadcast([P, SEQS, n])

            for g in range(GROUPS):
                norm(g, var_ready, std_ready, xn_ready, t_full if gated else x_ready, g * KD if gated else g)
            dve.drain()
            if gated:
                dve.memset(weight[:, :, R:E], 1.0)
                dve.memset(going[:], 1.0)
                dve.drain()
                dve.memset(going[:, :, 0:1], 0.0)
                dve.wait_ge(score_out, 1)
                dve.tensor_tensor(choice[:], score[:], r_bias[:].unsqueeze(1).to_broadcast([P, SEQS, R]), ALU.add)
                quads = choice[:].rearrange("p t (g e) -> p (t g) e", e=4)
                q_rank = rank[:].rearrange("p t (g e) -> p (t g) e", e=4)
                ranks(quads, q_rank, lt, SEQS * 4, 4)
                dve.scalar_tensor_tensor(rank[:], rank[:], 2.0, choice[:], ALU.is_lt, ALU.mult)
                dve.drain()
                dve.tensor_reduce(group[:].rearrange("p t g -> p (t g)"), q_rank, AX_X, ALU.add)
                ranks(group[:], g_rank[:], lt, SEQS, 4)
                dve.tensor_scalar(group[:], g_rank[:], 2.0, None, ALU.is_lt)
                dve.drain()
                dve.tensor_scalar(g_rank[:], group[:], -1.0, None, ALU.add)
                keep = lambda t: t[:].rearrange("p t g -> p (t g)").unsqueeze(2).to_broadcast([P, SEQS * 4, 4])
                dve.tensor_tensor(quads, quads, keep(group), ALU.mult)
                dve.drain()
                dve.tensor_tensor(quads, quads, keep(g_rank), ALU.add)
                dve.drain()
                for t in range(SEQS):
                    dve.max(best[:, t, :], choice[:, t, :])
                dve.drain()
                fourth = best[:, :, 3].unsqueeze(2).to_broadcast([P, SEQS, R])
                dve.tensor_tensor(above[:], choice[:], fourth, ALU.is_gt)
                dve.tensor_tensor(level[:], choice[:], fourth, ALU.is_equal)
                dve.drain()
                dve.tensor_reduce(total[:], above[:], AX_X, ALU.add)
                flat = lambda x: x[:].rearrange("p t r -> p (t r)")
                dve.tensor_tensor_scan(flat(rank), flat(going), flat(level), 0.0, ALU.mult, ALU.add)
                dve.drain()
                dve.tensor_tensor(rank[:], rank[:], wide(total[:], R), ALU.add)
                dve.drain()
                dve.scalar_tensor_tensor(level[:], rank[:], 4.5, level[:], ALU.is_lt, ALU.mult)
                dve.drain()
                dve.tensor_tensor(above[:], above[:], level[:], ALU.add)
                dve.drain()
                dve.tensor_tensor(choice[:], above[:], score[:], ALU.mult)
                dve.drain()
                dve.tensor_reduce(total[:], choice[:], AX_X, ALU.add)
                dve.drain()
                dve.tensor_scalar(total[:], total[:], 1e-20, None, ALU.add)
                dve.drain()
                dve.reciprocal(total[:], total[:])
                dve.drain()
                dve.scalar_tensor_tensor(weight[:, :, 0:R], choice[:], 2.5, wide(total[:], R),
                                         ALU.mult, ALU.mult).then_inc(weights_ready, 1)
            else:
                dve.wait_ge(r_full, 1)
                dve.tensor_tensor(score[:], up_ps[:, 2, 0:SEQS * R].rearrange("p (t r) -> p t r", r=R),
                                  r_bias[:].unsqueeze(1).to_broadcast([P, SEQS, R]), ALU.add)
                dve.drain()
                dve.tensor_reduce(total[:], score[:], AX_X, ALU.max)
                dve.drain()
                dve.tensor_tensor(score[:], score[:], wide(total[:], R), ALU.subtract).then_inc(score_in, 1)
                dve.wait_ge(score_out, 1)
                dve.tensor_reduce(total[:], score[:], AX_X, ALU.add)
                dve.drain()
                dve.reciprocal(total[:], total[:])
                dve.drain()
                dve.tensor_tensor(score[:], score[:], wide(total[:], R), ALU.mult)
                ranks(score[:], rank[:], lt, SEQS, R)
                dve.scalar_tensor_tensor(weight[:], rank[:], 2.0, score[:], ALU.is_lt,
                                         ALU.mult).then_inc(weights_ready, 1)

            def step(n, e, par, g):
                if gated and e is not None:
                    for f in range(chunks):
                        after(dve, up_full, n * 4 + 2 * f + 2)
                        after(dve, silu_ready, n * chunks + f + 1)
                        dve.tensor_tensor(h[:, g % 2, f, :], silu[:, f, :], up_ps[:, 2 * f + 1, :],
                                          ALU.mult).then_inc(h_ready, 1)
                prev = before(n, e, par, g)
                if prev:
                    m, pe_, ppar, pg = prev
                    dve.drain()
                    for b in range(2):
                        after(dve, dn_full, m * 2 + b + 1)
                        for j in range(2):
                            t = pg * TPG + 2 * b + j
                            last = dve.scalar_tensor_tensor(
                                acc[:, t, :], dn_ps[:, 2 * (pg % 2) + b, j * D:(j + 1) * D], weight[:, t, at(pe_)],
                                acc[:, t, :], ALU.mult, ALU.add)
                        last.then_inc(acc_done, 1)

            run(dve, step)
            if not gated:
                for b in range(SEQS // 2):
                    dve.drain()
                    dve.wait_ge(bias_full, b + 1)
                    rows = acc[:, 2 * b:2 * b + 2, :]
                    dve.tensor_tensor(rows, rows, dn_ps[:, b % 4, :].rearrange("p (j d) -> p j d", j=2),
                                      ALU.add).then_inc(bias_done, 1)
                for g in range(GROUPS):
                    norm(g, var2_ready, std2_ready, xn2_ready, x_ready, GROUPS + g)

        @block.tensor
        def _(pe):
            pe.wait_ge(consts_in, 16 * n_consts)
            for g in range(GROUPS):
                pe.wait_ge(xn_ready if gated else x_ready, g + 1)
                for kc in range(KD):
                    after(pe, xT_ready, (g - 1) * KD + kc + 1)
                    for j in range(TPG):
                        src = xn[:, j, kc * P:(kc + 1) * P] if gated else acc[:, g * TPG + j, kc * P:(kc + 1) * P]
                        last = pe.transpose(up_ps[:, kc, j * TOK:(j + 1) * TOK], src, ident[:])
                    last.then_inc(t_full, 1)
            pe.wait_ge(xT_ready, GROUPS * KD)
            for t in range(SEQS):
                for kc in range(KD):
                    last = pe.matmul(up_ps[:, 2, t * R:(t + 1) * R], xT[:, kc, t * TOK:(t + 1) * TOK],
                                     router[:, kc, :], start=(kc == 0), stop=(kc == KD - 1))
            last.then_inc(r_full, 1)
            pe.wait_ge(score_out if gated else score_in, 1)

            def step(n, e, par, g):
                if e is not None:
                    pair = 0 if isinstance(e, int) else (e - par)
                    pe.wait_ge(w_in[par], pair * (PER_EXPERT // 2) + PER_EXPERT)
                    for c in range(NUP):
                        if gated:
                            after(pe, h_ready if c % 2 else silu_ready, (n - 1) * chunks + c // 2 + 1)
                        else:
                            after(pe, h_ready, (n - 1) * chunks + c + 1)
                        for kc in range(KD):
                            last = pe.matmul(up_ps[:, c, :], w_up[:, par, kc, c * P:(c + 1) * P],
                                             xT[:, kc, g * GT:(g + 1) * GT], start=(kc == 0), stop=(kc == KD - 1))
                        last.then_inc(up_full, 1)
                prev = before(n, e, par, g)
                if prev:
                    m, pe_, ppar, pg = prev
                    after(pe, h_ready, m * chunks + chunks)
                    for b in range(2):
                        after(pe, acc_done, (m - 2) * 2 + b + 1)
                        for j in range(2):
                            for f in range(chunks):
                                t = 2 * b + j
                                last = pe.matmul(dn_ps[:, 2 * (pg % 2) + b, j * D:(j + 1) * D],
                                                 h[:, pg % 2, f, t * TOK:(t + 1) * TOK], w_dn[:, ppar, f, :],
                                                 start=(f == 0), stop=(f == chunks - 1))
                        last.then_inc(dn_full, 1)

            run(pe, step)
            if not gated:
                pe.wait_ge(weights_ready, 1)
                for g in range(GROUPS):
                    for j in range(TPG):
                        t = g * TPG + j
                        last = pe.transpose(up_ps[0:E, g, j * TOK:(j + 1) * TOK], weight[:, t, :], ident[:])
                    last.then_inc(wT_full, 1)
                pe.wait_ge(wT_ready, GROUPS)
                pe.wait_ge(acc_done, 2 * UNITS)
                for b in range(SEQS // 2):
                    after(pe, bias_done, b - 3)
                    for j in range(2):
                        t = 2 * b + j
                        last = pe.matmul(dn_ps[:, b % 4, j * D:(j + 1) * D], wT[:, t * TOK:(t + 1) * TOK],
                                         b_dn[:], start=True, stop=True)
                    last.then_inc(bias_full, 1)


def build(nc, io, out):
    with ExitStack() as sems:
        res = sems.enter_context(nc.sbuf_tensor("res", [P, SEQS, D], F32))
        ident = sems.enter_context(nc.sbuf_tensor("ident", [P, P], F32))
        eps = sems.enter_context(nc.sbuf_tensor("eps", [P, 1], F32))
        ident_in = sems.enter_context(nc.semaphore("ident_in"))
        eps_set = sems.enter_context(nc.semaphore("eps_set"))
        with nc.Block() as block:
            @block.sync
            def _(sp):
                sp.dma_start(ident[:], io["ident"]).then_inc(ident_in, 16)
                sp.wait_ge(ident_in, 16)

            @block.vector
            def _(dve):
                dve.memset(eps[:], EPS).then_inc(eps_set, 1)
                dve.wait_ge(eps_set, 1)

        heads_dim = {"a0_": 64, "f0_": 16, "a1_": 16}
        w = {}
        for name, hd in heads_dim.items():
            w[name] = (sems.enter_context(nc.sbuf_tensor(name + "w_qkv", [P, KD, 3 * HEADS * hd], F32)),
                       sems.enter_context(nc.sbuf_tensor(name + "w_out", [P, HEADS * hd // P, D], F32)),
                       sems.enter_context(nc.semaphore(name + "weights_in")), 32)

        def load_attention(sp):
            for name in heads_dim:
                sp.dma_start(w[name][0][:], io[name + "w_qkv"]).then_inc(w[name][2], 16)
                sp.dma_start(w[name][1][:], io[name + "w_out"]).then_inc(w[name][2], 16)

        w_up = sems.enter_context(nc.sbuf_tensor("w_up", [P, 2, KD, 4 * P], F32))
        w_dn = sems.enter_context(nc.sbuf_tensor("w_dn", [P, 2, 4, D], F32))
        b_up = sems.enter_context(nc.sbuf_tensor("b_up", [P, 2, 4], F32))
        store = {n: (w_up, w_dn, b_up, [sems.enter_context(nc.semaphore(n + "w_in_even")),
                                        sems.enter_context(nc.semaphore(n + "w_in_odd"))]) for n in ("m0_", "m1_")}

        def first_experts(name, biased):
            def load(sp):
                for e in range(2):
                    load_expert(sp, io, name, store[name], e, e, biased)
            return load

        token_stage(nc, sems, io, res, ident, eps, load_attention)
        attention_stage(nc, sems, io, res, ident, eps, "a0_", 64, *w["a0_"],
                        rope=(io["cos64"], io["sin64"], io["nsin64"]), out_bias=io["a0_b_out"])
        with nc.sbuf_tensor("mixed", [P, SEQS, D], F32) as mixed:
            attention_stage(nc, sems, io, res, ident, eps, "f0_", 16, *w["f0_"],
                            qkv_bias=io["f0_b_qkv"], out_bias=io["f0_b_out"], onto=mixed,
                            prefetch=first_experts("m0_", True))
            experts_stage(nc, sems, io, res, ident, eps, "m0_", 8, 8, 4, False, mixed, store["m0_"])
        attention_stage(nc, sems, io, res, ident, eps, "a1_", 16, *w["a1_"],
                        rope=(io["cos16"], io["sin16"], io["nsin16"]), mask_dram=io["mask"],
                        prefetch=first_experts("m1_", False))
        experts_stage(nc, sems, io, res, ident, eps, "m1_", 18, 16, 2, True, res, store["m1_"], out=out)


def kernel(**inputs):
    import numpy as np
    import concourse.bacc as bacc
    from concourse.bass_utils import run_bass_kernel_spmd

    a = {n: np.asarray(v) for n, v in inputs.items()}

    def rows(w):
        *lead, kk, n = w.shape
        return np.moveaxis(w.reshape(*lead, kk // P, P, n), -3, -2)

    def cols(v):
        *lead, kk = v.shape
        return np.moveaxis(v.reshape(*lead, kk // P, P), -1, 0)

    def rope(n, half):
        theta = (np.float32(1.0) / np.float32(10000.0) ** (np.arange(half, dtype=np.float32) / np.float32(half)))
        angle = np.arange(n, dtype=np.float32)[:, None] * theta.astype(np.float32)[None, :]
        return np.cos(angle).astype(np.float32), np.sin(angle).astype(np.float32)

    def lower(n):
        return np.broadcast_to(np.tril(np.ones((n, n), np.float32), -1), (P, n, n))

    t = {"ids": a["x"].T, "emb": a["L0_tok_tok_emb"], "pos": a["L0_tok_pos_emb"][:TOK]}
    t["w_in"] = rows(a["L0_tok_W_in"].transpose(0, 2, 1))
    t["w_b"] = rows(a["L0_tok_W_B"].transpose(0, 2, 1))
    t["w_c"] = a["L0_tok_W_C"].transpose(0, 2, 1)
    t["w_o"] = rows(a["L0_tok_W_out"].transpose(0, 2, 1))
    t["conv_w"] = np.moveaxis(a["L0_tok_conv_w"][:, :, 0, :].reshape(LAYERS, KI, P, TAPS), 2, 0)
    t["conv_b"] = cols(a["L0_tok_conv_b"])
    t["d_vec"] = cols(a["L0_tok_D_vec"])
    t["tok_ln_g"], t["tok_ln_b"] = a["L0_tok_ln_g"], a["L0_tok_ln_b"]
    decay = np.full((STATE, GT), DECAY, np.float32)
    decay[:, ::TOK] = 0.0
    t["decay"] = decay
    t["ident"] = np.eye(P, dtype=np.float32)
    t["cos64"], t["sin64"] = rope(TOK, 32)
    t["cos16"], t["sin16"] = rope(TOK, 8)
    t["nsin64"], t["nsin16"] = -t["sin64"], -t["sin16"]
    i = np.arange(TOK)
    seen = (i[:, None] // 64 == i[None, :] // 64) & (i[None, :] <= i[:, None])
    t["mask"] = np.where(seen, np.float32(0), np.float32(-3e38)).astype(np.float32)
    for n in (4, 8):
        t["lt%d" % n] = lower(n)
    t["a0_w_qkv"] = rows(a["L0_attn_w_qkv"])
    t["a0_w_out"] = rows(a["L0_attn_w_out"])
    t["a0_b_out"] = a["L0_attn_b_out"][None]
    t["f0_w_qkv"] = rows(np.concatenate([a["L0_ffn_Wq"], a["L0_ffn_Wk"], a["L0_ffn_Wv"]], 1))
    t["f0_b_qkv"] = np.concatenate([a["L0_ffn_bq"], a["L0_ffn_bk"], a["L0_ffn_bv"]])[None]
    t["f0_w_out"] = rows(a["L0_ffn_Wo"])
    t["f0_b_out"] = a["L0_ffn_bo"][None]
    t["m0_router"] = rows(a["L0_ffn_gW"])
    t["m0_r_bias"] = a["L0_ffn_gb"][None]
    t["m0_up"] = rows(a["L0_ffn_W1"])
    t["m0_b_up"] = a["L0_ffn_b1"].reshape(8, 4, P).transpose(0, 2, 1)
    t["m0_dn"] = rows(a["L0_ffn_W2"])
    t["m0_b_dn"] = a["L0_ffn_b2"]
    for n in ("ln1_g", "ln1_b", "ln2_g", "ln2_b"):
        t["m0_" + n] = a["L0_ffn_" + n][None]
    w = a["L1_attn_Wqkv"].reshape(3, HEADS, 8, 2, D)
    q_k = w[:2].transpose(0, 1, 3, 2, 4).reshape(2 * D, D)
    t["a1_w_qkv"] = rows(np.concatenate([q_k, a["L1_attn_Wqkv"][2 * D:]]).T)
    t["a1_w_out"] = rows(a["L1_attn_Wout"].T)
    t["m1_router"] = rows(a["L1_ffn_router_w"].T)
    t["m1_r_bias"] = a["L1_ffn_bias"][None]

    def experts(routed, shared):
        return np.concatenate([routed, shared.reshape(D, 2, D).transpose(1, 0, 2)])

    gate = experts(a["L1_ffn_gate_w"], a["L1_ffn_sh_gate_w"]).reshape(18, D, 2, P)
    up = experts(a["L1_ffn_up_w"], a["L1_ffn_sh_up_w"]).reshape(18, D, 2, P)
    t["m1_up"] = rows(np.stack([gate, up], 3).reshape(18, D, 4 * P))
    t["m1_dn"] = rows(np.concatenate([a["L1_ffn_down_w"], a["L1_ffn_sh_down_w"].reshape(2, D, D)]))

    nc = bacc.Bacc("TRN2", target_bir_lowering=False, num_devices=1)
    arrays, io = {}, {}
    for n, v in t.items():
        arrays["in_" + n] = np.ascontiguousarray(v)
        io[n] = nc.dram_tensor("in_" + n, v.shape, mybir.dt.from_np(v.dtype), kind="ExternalInput").ap()
    out = nc.dram_tensor("out_0", (SEQS * TOK, D), F32, kind="ExternalOutput").ap()
    build(nc, io, out)
    r = run_bass_kernel_spmd(nc, [arrays], core_ids=[0])
    return r.results[0]["out_0"].reshape(SEQS, TOK, D)
```

```python
from contextlib import ExitStack

import concourse.bass as bass
from concourse import mybir

F32 = mybir.dt.float32
I32 = mybir.dt.int32
F32R = mybir.dt.float32r
BF16 = mybir.dt.bfloat16
U32 = mybir.dt.uint32
ALU = mybir.AluOpType
ACT = mybir.ActivationFunctionType
AX_X = mybir.AxisListType.X

P = 128
SEQS = 16
TOK = 128
D = 256
KD = D // P
GROUPS = 4
TPG = SEQS // GROUPS
GT = TPG * TOK
LAYERS = 4
INNER = 512
KI = INNER // P
STATE = 64
TAPS = 4
DECAY, INP = 0.95, 0.05
EPS = 1e-5
HEADS = 16
BANK = 512


def after(eng, sem, count):
    if isinstance(count, int) and count <= 0:
        return
    eng.wait_ge(sem, count)


def at(i):
    return slice(i, i + 1) if isinstance(i, int) else bass.ds(i, 1)


class Kit:

    def __init__(self, nc, sems):
        self.nc, self.sems, self.mem = nc, sems, ExitStack()

    def sem(self, name):
        return self.sems.enter_context(self.nc.semaphore(name))

    def sb(self, name, shape, dt=F32):
        return self.mem.enter_context(self.nc.sbuf_tensor(name, shape, dt))

    def ps(self, name, shape):
        return self.mem.enter_context(self.nc.psum_tensor(name, shape, F32))


def token_stage(nc, sems, io, res, ident, eps, prefetch):
    k = Kit(nc, sems)
    with k.mem:
        ids = k.sb("ids", [P, SEQS], I32)
        pos = k.sb("pos", [P, D])
        x_hi = k.sb("tok_x_hi", [P, KD, SEQS * TOK], F32R)
        x_lo = k.sb("tok_x_lo", [P, KD, SEQS * TOK], F32R)
        w_hi = k.sb("w_in_hi", [P, KD, 2 * INNER], F32R)
        w_lo = k.sb("w_in_lo", [P, KD, 2 * INNER], F32R)
        zero = k.sb("tok_zero", [P, 1])
        w_in = k.sb("w_in", [P, KD, 2 * INNER])
        w_b = k.sb("w_b", [P, KI, STATE])
        w_c = k.sb("w_c", [STATE, INNER])
        w_o = k.sb("w_o", [P, KI, D])
        conv_w = k.sb("conv_w", [P, LAYERS, KI, TAPS])
        conv_b = k.sb("conv_b", [P, LAYERS, KI])
        d_vec = k.sb("d_vec", [P, LAYERS, KI])
        ln_g = k.sb("tok_ln_g", [P, LAYERS, D])
        ln_b = k.sb("tok_ln_b", [P, LAYERS, D])
        gain = k.sb("gain", [P, 2, D])
        decay = k.sb("decay", [STATE, GT])
        u = k.sb("u", [P, 2, KI, GT])
        gate = k.sb("gate", [P, 2, KI, GT])
        bu = k.sb("bu", [STATE, GT])
        state = k.sb("state", [STATE, GT])
        z = k.sb("tok_z", [P, TPG, D])
        stats = k.sb("tok_stats", [P, TPG, 6])
        mv = k.sb("tok_mv", [P, TPG, 2])
        std = k.sb("tok_std", [P, TPG])
        rstd = k.sb("tok_rstd", [P, TPG])
        xp_ps = k.ps("xp_ps", [P, 3, BANK])
        c_ps = k.ps("c_ps", [P, 2, BANK])
        b_ps = c_ps[:, 0, :]
        d_ps = k.ps("d_ps", [P, 2, BANK])
        t_ps = k.ps("t_ps", [P, BANK])

        ids_in, pos_in, consts_in, w_in_in = (k.sem(n) for n in ("ids_in", "pos_in", "tok_consts_in", "w_in_in"))
        w_b_in, w_c_in, w_o_in = (k.sem(n) for n in ("w_b_in", "w_c_in", "w_o_in"))
        gathered = [k.sem("gathered%d" % g) for g in range(GROUPS)]
        xp_full, conv_done, gate_done, u_ready = (k.sem(n) for n in ("xp_full", "conv_done", "gate_done", "u_ready"))
        bu_full, bu_ready, scan_done = (k.sem(n) for n in ("bu_full", "bu_ready", "scan_done"))
        c_full, comb_done, y_ready = (k.sem(n) for n in ("c_full", "comb_done", "y_ready"))
        d_full, z_done, var_ready, std_ready, xn_ready = (
            k.sem(n) for n in ("d_full", "z_done", "tok_var_ready", "tok_std_ready", "tok_xn_ready"))
        res_ready, t_full = (k.sem(n) for n in ("res_ready", "tok_t_full"))
        x_hi_ready, x_lo_ready, w_split = (k.sem(n) for n in ("tok_x_hi_ready", "tok_x_lo_ready", "w_in_split"))
        CONSTS = 6

        def unit(l, g, back):
            lay, grp = l + (g - back) // GROUPS, (g - back) % GROUPS
            if isinstance(lay, int) and not 0 <= lay < LAYERS:
                return None
            return lay * GROUPS + grp, lay, grp

        def run(eng, step):
            for g in range(GROUPS):
                step(0, g)
            with eng.Fori(1, LAYERS) as l:
                for g in range(GROUPS):
                    step(l, g)
            step(LAYERS, 0)
            step(LAYERS, 1)

        block = k.mem.enter_context(nc.Block())

        @block.sync
        def _(sp):
            sp.dma_start(ids[:], io["ids"]).then_inc(ids_in, 16)
            sp.dma_start(pos[:], io["pos"]).then_inc(pos_in, 16)
            sp.dma_start(w_in[:], io["w_in"][0]).then_inc(w_in_in, 16)
            sp.dma_start(conv_w[:], io["conv_w"]).then_inc(consts_in, 16)
            sp.dma_start(conv_b[:], io["conv_b"]).then_inc(consts_in, 16)
            sp.dma_start(w_b[:], io["w_b"][0]).then_inc(w_b_in, 16)
            sp.dma_start(w_c[:], io["w_c"][0]).then_inc(w_c_in, 16)
            sp.dma_start(w_o[:], io["w_o"][0]).then_inc(w_o_in, 16)
            sp.dma_start(d_vec[:], io["d_vec"]).then_inc(consts_in, 16)
            sp.dma_start(decay[:], io["decay"]).then_inc(consts_in, 16)
            sp.dma_start(ln_g[:], io["tok_ln_g"].unsqueeze(0).to_broadcast([P, LAYERS, D])).then_inc(consts_in, 16)
            sp.dma_start(ln_b[:], io["tok_ln_b"].unsqueeze(0).to_broadcast([P, LAYERS, D])).then_inc(consts_in, 16)
            for g in range(GROUPS):
                sp.wait_ge(gathered[g], 16 * TPG)
            prefetch(sp)
            with sp.Fori(1, LAYERS) as l:
                sp.wait_ge(w_split, l * 2 * KI)
                sp.dma_start(w_in[:], io["w_in"][at(l)].rearrange("l p k n -> (l p) k n")).then_inc(w_in_in, 16)
                sp.wait_ge(bu_full, l * GROUPS)
                sp.dma_start(w_b[:], io["w_b"][at(l)].rearrange("l p k n -> (l p) k n")).then_inc(w_b_in, 16)
                sp.wait_ge(c_full, l * GROUPS * KI)
                sp.dma_start(w_c[:], io["w_c"][at(l)].rearrange("l p n -> (l p) n")).then_inc(w_c_in, 16)
                sp.wait_ge(d_full, l * GROUPS * 2)
                sp.dma_start(w_o[:], io["w_o"][at(l)].rearrange("l p k n -> (l p) k n")).then_inc(w_o_in, 16)

        @block.gpsimd
        def _(pool):
            pool.wait_ge(ids_in, 16)
            for t in range(SEQS):
                pool.indirect_dma_start(res[:, t, :], None, io["emb"], bass.IndirectOffsetOnAxis(
                    ap=ids[:, t:t + 1].bitcast(U32), axis=0)).then_inc(gathered[t // TPG], 16)

            def split_w_in(l):
                for m in range(KI):
                    for c in (m, KI + m):
                        cols = slice(c * P, (c + 1) * P)
                        pool.drain()
                        after(pool, xp_full, (l * GROUPS - 1) * 2 * KI + 2 * m + 1 + c // KI)
                        after(pool, w_in_in, (l + 1) * 16)
                        pool.tensor_tensor(w_hi[:, :, cols], w_in[:, :, cols],
                                           zero[:].unsqueeze(1).to_broadcast([P, KD, P]), ALU.add)
                        pool.drain()
                        pool.tensor_tensor(w_lo[:, :, cols], w_in[:, :, cols], w_hi[:, :, cols].bitcast(F32),
                                           ALU.subtract).then_inc(w_split, 1)

            pool.memset(zero[:], 0.0)

            def step(l, g):
                fin, mid = unit(l, g, 2), unit(l, g, 1)
                if g == 0 and not isinstance(l, int):
                    split_w_in(l)
                if mid:
                    n, lay, grp = mid
                    after(pool, gate_done, n * KI + KI)
                    for c in range(KI):
                        after(pool, comb_done, n * KI + c + 1)
                        pool.tensor_tensor(u[:, grp % 2, c, :], u[:, grp % 2, c, :], gate[:, grp % 2, c, :],
                                           ALU.mult).then_inc(y_ready, 1)
                if fin:
                    n, lay, grp = fin
                    rows = res[:, grp * TPG:(grp + 1) * TPG, :]
                    pool.drain()
                    if grp == 0:
                        pool.tensor_copy(gain[:, 0:1, :], ln_g[:, at(lay), :])
                        pool.tensor_copy(gain[:, 1:2, :], ln_b[:, at(lay), :])
                        pool.drain()
                    after(pool, xn_ready, n + 1)
                    pool.tensor_tensor(rows, z[:], gain[:, 0:1, :].to_broadcast([P, TPG, D]), ALU.mult)
                    pool.drain()
                    pool.tensor_tensor(rows, rows, gain[:, 1:2, :].to_broadcast([P, TPG, D]),
                                       ALU.add).then_inc(res_ready, 1)

            run(pool, step)

        @block.scalar
        def _(act):
            def turn_back(n, grp, kc):
                after(act, t_full, n * KD + kc + 1)
                act.activation(x_hi[:, kc, grp * GT:(grp + 1) * GT], t_ps[:], ACT.Copy).then_inc(x_hi_ready, 1)

            for n in range(2):
                for kc in range(KD):
                    turn_back(n, n, kc)

            def step(l, g):
                new, mid, fin = unit(l, g, 0), unit(l, g, 1), unit(l, g, 2)

                def gates(m):
                    if new:
                        n, lay, grp = new
                        if m == 0:
                            after(act, y_ready, (n - 2) * KI + KI)
                        after(act, xp_full, n * 2 * KI + 2 * m + 2)
                        act.activation(gate[:, grp % 2, m, :], xp_ps[:, 2, :], ACT.Silu).then_inc(gate_done, 1)

                def inputs(m):
                    if new:
                        n, lay, grp = new
                        after(act, conv_done, n * KI + m + 1)
                        act.activation(u[:, grp % 2, m, :], u[:, grp % 2, m, :], ACT.Silu).then_inc(u_ready, 1)

                gates(0)
                if new and mid:
                    turn_back(new[0] + 1, (g + 1) % GROUPS, 0)
                if mid:
                    after(act, bu_full, mid[0] + 1)
                    after(act, scan_done, mid[0])
                    act.activation(bu[:], b_ps[0:STATE, :], ACT.Copy, scale=INP).then_inc(bu_ready, 1)
                inputs(0)
                gates(1)
                if new and mid:
                    turn_back(new[0] + 1, (g + 1) % GROUPS, 1)
                inputs(1)
                if fin:
                    after(act, var_ready, fin[0] + 1)
                    act.activation(std[:], mv[:, :, 1], ACT.Sqrt, bias=eps[:, 0:1]).then_inc(std_ready, 1)
                gates(2)
                gates(3)
                inputs(2)
                inputs(3)

            run(act, step)

        @block.vector
        def _(dve):
            dve.wait_ge(w_in_in, 16)
            dve.tensor_copy(w_hi[:], w_in[:])
            dve.drain()
            dve.tensor_tensor(w_lo[:], w_in[:], w_hi[:].bitcast(F32), ALU.subtract).then_inc(w_split, 2 * KI)
            dve.wait_ge(pos_in, 16)

            def low_part(n, grp, kc):
                there = slice(grp * GT, (grp + 1) * GT)
                dve.drain()
                after(dve, x_hi_ready, n * KD + kc + 1)
                dve.tensor_tensor(x_lo[:, kc, there], t_ps[:], x_hi[:, kc, there].bitcast(F32),
                                  ALU.subtract).then_inc(x_lo_ready, 1)

            for g in range(GROUPS):
                if g == 2:
                    for n in range(2):
                        for kc in range(KD):
                            low_part(n, n, kc)
                dve.wait_ge(gathered[g], 16 * TPG)
                rows = res[:, g * TPG:(g + 1) * TPG, :]
                dve.tensor_tensor(rows, rows, pos[:].unsqueeze(1).to_broadcast([P, TPG, D]),
                                  ALU.add).then_inc(res_ready, 1)
            dve.wait_ge(consts_in, 16 * CONSTS)

            def conv(new, m):
                dve.drain()
                n, lay, grp = new
                if m == 0:
                    after(dve, d_full, (n - 2) * 2 + 2)
                after(dve, xp_full, n * 2 * KI + 2 * m + 1)
                acc = u[:, grp % 2, m, :].rearrange("p (s t) -> p s t", s=TPG)
                xin = xp_ps[:, m % 2, :].rearrange("p (s t) -> p s t", s=TPG)
                w = lambda tap: conv_w[:, at(lay), m, tap]
                dve.tensor_scalar(u[:, grp % 2, m, :], xp_ps[:, m % 2, :], w(TAPS - 1), conv_b[:, at(lay), m],
                                  ALU.mult, ALU.add)
                for back in range(1, TAPS):
                    dve.drain()
                    last = dve.scalar_tensor_tensor(acc[:, :, back:], xin[:, :, :TOK - back], w(TAPS - 1 - back),
                                                    acc[:, :, back:], ALU.mult, ALU.add)
                last.then_inc(conv_done, 1)

            def combine(mid):
                n, lay, grp = mid
                for c in range(KI):
                    dve.drain()
                    after(dve, u_ready, n * KI + KI)
                    after(dve, c_full, n * KI + c + 1)
                    dve.scalar_tensor_tensor(u[:, grp % 2, c, :], u[:, grp % 2, c, :], d_vec[:, at(lay), c],
                                             c_ps[:, c % 2, :], ALU.mult, ALU.add).then_inc(comb_done, 1)

            def step(l, g):
                new, mid, fin = unit(l, g, 0), unit(l, g, 1), unit(l, g, 2)
                if fin:
                    n, lay, grp = fin
                    for b in range(2):
                        dve.drain()
                        if b == 0:
                            after(dve, res_ready, GROUPS + n)
                        after(dve, d_full, n * 2 + b + 1)
                        dve.tensor_tensor(z[:, 2 * b:2 * b + 2, :], d_ps[:, b, :].rearrange("p (j d) -> p j d", j=2),
                                          res[:, grp * TPG + 2 * b:grp * TPG + 2 * b + 2, :],
                                          ALU.add).then_inc(z_done, 1)
                    dve.drain()
                    for j in range(TPG):
                        dve.bn_stats(stats[:, j, :], z[:, j, :])
                    dve.drain()
                    for j in range(TPG):
                        last = dve.bn_aggr(mv[:, j, :], stats[:, j, :])
                    last.then_inc(var_ready, 1)
                if new:
                    conv(new, 0)
                if new and mid:
                    low_part(new[0] + 1, (g + 1) % GROUPS, 0)
                if mid:
                    n = mid[0]
                    dve.drain()
                    after(dve, bu_ready, n + 1)
                    dve.tensor_tensor_scan(state[:], decay[:], bu[:], 0.0, ALU.mult, ALU.add).then_inc(scan_done, 1)
                if new:
                    conv(new, 1)
                if new and mid:
                    low_part(new[0] + 1, (g + 1) % GROUPS, 1)
                if mid:
                    combine(mid)
                if fin:
                    dve.drain()
                    n, lay, grp = fin
                    after(dve, std_ready, n + 1)
                    dve.reciprocal(rstd[:], std[:])
                    dve.drain()
                    for j in range(TPG):
                        last = dve.tensor_scalar(z[:, j, :], z[:, j, :], mv[:, j, 0:1], rstd[:, j:j + 1],
                                                 ALU.subtract, ALU.mult)
                    last.then_inc(xn_ready, 1)
                if new:
                    conv(new, 2)
                    conv(new, 3)

            run(dve, step)

        @block.tensor
        def _(pe):
            def turn(n, grp, kc):
                after(pe, res_ready, n + 1)
                after(pe, x_lo_ready, n * KD + kc)
                for j in range(TPG):
                    last = pe.transpose(t_ps[:, j * TOK:(j + 1) * TOK],
                                        res[:, grp * TPG + j, kc * P:(kc + 1) * P], ident[:])
                last.then_inc(t_full, 1)

            for n in range(2):
                for kc in range(KD):
                    turn(n, n, kc)

            def project_in(new, m):
                n, lay, grp = new
                if m == 0:
                    after(pe, x_lo_ready, (n + 1) * KD)
                gated = m >= KI
                after(pe, w_split, lay * 2 * KI + 2 * (m % KI) + 1 + int(gated))
                if gated:
                    after(pe, gate_done, n * KI + m % KI)
                else:
                    after(pe, conv_done, n * KI + m - 1)
                bank = xp_ps[:, 2 if gated else m % 2, :]
                for kc in range(KD):
                    for w, x in ((w_hi, x_hi), (w_hi, x_lo), (w_lo, x_hi)):
                        last = pe.matmul(bank, w[:, kc, m * P:(m + 1) * P], x[:, kc, grp * GT:(grp + 1) * GT],
                                         start=(kc == 0 and w is w_hi and x is x_hi), stop=(kc == KD - 1 and w is w_lo))
                last.then_inc(xp_full, 1)

            def mix(mid, cs):
                n, lay, grp = mid
                after(pe, w_c_in, (lay + 1) * 16)
                for c in cs:
                    after(pe, comb_done, n * KI + c - 1)
                    pe.matmul(c_ps[:, c % 2, :], w_c[:, c * P:(c + 1) * P], state[:], start=True,
                              stop=True).then_inc(c_full, 1)

            def step(l, g):
                new, mid, fin = unit(l, g, 0), unit(l, g, 1), unit(l, g, 2)
                if new:
                    project_in(new, 0)
                    project_in(new, KI + 0)
                if new and mid:
                    turn(new[0] + 1, (g + 1) % GROUPS, 0)
                if mid:
                    n, lay, grp = mid
                    after(pe, w_b_in, (lay + 1) * 16)
                    after(pe, u_ready, n * KI + KI)
                    after(pe, comb_done, (n - 1) * KI + 3)
                    for c in range(KI):
                        last = pe.matmul(b_ps[0:STATE, :], w_b[:, c, :], u[:, grp % 2, c, :],
                                         start=(c == 0), stop=(c == KI - 1))
                    last.then_inc(bu_full, 1)
                if new:
                    project_in(new, 1)
                    project_in(new, KI + 1)
                if new and mid:
                    turn(new[0] + 1, (g + 1) % GROUPS, 1)
                if mid:
                    after(pe, scan_done, mid[0] + 1)
                    mix(mid, (0, 1))
                if new:
                    project_in(new, 2)
                    project_in(new, KI + 2)
                if mid:
                    mix(mid, (2, 3))
                if new:
                    project_in(new, 3)
                    project_in(new, KI + 3)
                for b in range(2):
                    if mid:
                        n, lay, grp = mid
                        after(pe, w_o_in, (lay + 1) * 16)
                        after(pe, y_ready, n * KI + KI)
                        after(pe, z_done, (n - 1) * 2 + b + 1)
                        for j in (2 * b, 2 * b + 1):
                            for c in range(KI):
                                last = pe.matmul(d_ps[:, b, (j % 2) * D:(j % 2 + 1) * D],
                                                 u[:, grp % 2, c, j * TOK:(j + 1) * TOK], w_o[:, c, :],
                                                 start=(c == 0), stop=(c == KI - 1))
                        last.then_inc(d_full, 1)

            run(pe, step)


def attention_stage(nc, sems, io, res, ident, eps, name, hd, w_qkv, w_out, weights_in, weights_count,
                    rope=None, qkv_bias=None, out_bias=None, mask_dram=None, onto=None, prefetch=None):
    k = Kit(nc, sems)
    inner = HEADS * hd
    pad = 64 if hd == 64 else 32
    half = hd // 2
    hpc = P // pad
    nch = HEADS // hpc
    no = inner // P
    qk_slices = 2 * inner // BANK
    vw = min(inner, BANK)
    v_slices = inner // vw
    nq = qk_slices + v_slices
    hps = 2 * HEADS // qk_slices
    vh = HEADS // v_slices
    nb, hb = 4, HEADS // 4
    nav = nb if hd == 64 else 1
    hav = HEADS // nav
    scale = hd ** -0.5
    UNROLL = 4
    FIRST, OTHERS = slice(0, 2), slice(2, SEQS)
    BACK = {"q": 0, "part": 2, "qk": 1, "s": 1, "probs": 2, "av": 2, "out": 3, "proj": 3, "norm": -1}
    if hd == 64:
        PE_ORDER = [("qk", 0), ("probs", 0), ("q", 0), ("qk", 1), ("probs", 1), ("q", 1), ("av", 0), ("qk", 2),
                    ("probs", 2), ("q", 2), ("av", 1), ("qk", 3), ("probs", 3), ("q", 3), ("av", 2), ("s", 0),
                    ("q", 4), ("av", 3), ("s", 1), ("q", 5), ("out", 0), ("s", 2), ("out", 1), ("norm", 0),
                    ("s", 3), ("proj", 0)]
        ACT_ORDER = [("qk", 0), ("probs", 0), ("qk", 1), ("probs", 1), ("qk", 2), ("probs", 2), ("qk", 3),
                     ("probs", 3), ("v", 0), ("exp", 0), ("v", 1), ("out", 0), ("exp", 1), ("out", 1), ("norm", 0),
                     ("exp", 2), ("exp", 3)]
        DVE_ORDER = [("xs", 0), ("q", 0), ("q", 1), ("av", 0), ("q", 2), ("av", 1), ("q", 3), ("av", 2), ("s", 0),
                     ("av", 3), ("s", 1), ("s", 2), ("s", 3), ("proj", 0)]
    else:
        PE_ORDER = [("probs", 0), ("qk", 0), ("qk", 1), ("part", 0), ("probs", 1), ("probs", 2), ("s", 0),
                    ("s", 1), ("q", 0), ("s", 2), ("part", 1), ("q", 1), ("probs", 3), ("part", 2), ("av", 0),
                    ("out", 0), ("s", 3), ("norm", 0), ("proj", 0)]
        ACT_ORDER = [("probs", 0), ("qk", 0), ("qk", 1), ("probs", 1), ("probs", 2), ("exp", 0), ("probs", 3),
                     ("exp", 1), ("exp", 2), ("v", 0), ("out", 0), ("norm", 0), ("exp", 3)]
        DVE_ORDER = [("s", 0), ("xs", 0), ("s", 1), ("q", 0), ("s", 2), ("av", 0), ("v", 0), ("s", 3),
                     ("proj", 0)]
    TR = [u for u in PE_ORDER if u[0] in ("qk", "probs", "out", "norm")]
    AV = [u for u in PE_ORDER if u[0] in ("av", "proj")]

    def ring_count(ring, s, phase, i):
        if isinstance(s, int):
            before = sum(min(max(s - BACK[p], 0), SEQS) for p, _ in ring)
        else:
            before = s * len(ring) - sum(BACK[p] for p, _ in ring)
        n = ring.index((phase, i))
        return before + 1 + sum(1 for p, _ in ring[:n] if not isinstance(s, int) or 0 <= s - BACK[p] < SEQS)

    with k.mem:
        xs = k.sb(name + "xs", [P, D])
        xT = k.sb(name + "xT", [P, KD, TOK])
        x_hi = k.sb(name + "x_hi", [P, KD, TOK], F32R)
        x_lo = k.sb(name + "x_lo", [P, KD, TOK], F32R)
        w_hi = k.sb(name + "w_hi", [P, KD, 3 * inner], F32R)
        w_lo = k.sb(name + "w_lo", [P, KD, 3 * inner], F32R)
        qk = k.sb(name + "qk", [P, 2, 2 * HEADS, pad])
        vals = k.sb(name + "vals", [P, UNROLL, HEADS, hd + 1])
        qkT = k.sb(name + "qkT", [P, 2, nch, TOK])
        if KD * 3 * inner >= 2 * HEADS * TOK:
            probs = w_qkv[:].rearrange("p k n -> p (k n)")[:, 0:2 * HEADS * TOK].rearrange(
                "p (a h t) -> p a h t", a=2, h=HEADS)
        else:
            probs = k.sb(name + "probs", [P, 2, HEADS, TOK])
        pT = k.sb(name + "pT", [P, HEADS, TOK])
        heads = k.sb(name + "heads", [P, 2, HEADS, hd])
        oT = k.sb(name + "oT", [P, no, TOK])
        top = k.sb(name + "top", [P, hb])
        rsum = k.sb(name + "rsum", [P, hav])
        stats = k.sb(name + "stats", [P, SEQS, 6])
        mv = k.sb(name + "mv", [P, SEQS, 2])
        std = k.sb(name + "std", [P, SEQS])
        rstd = k.sb(name + "rstd", [P, SEQS])
        if rope:
            cos = k.sb(name + "cos", [P, half])
            sin = k.sb(name + "sin", [P, half])
            nsin = k.sb(name + "nsin", [P, half])
            turned = k.sb(name + "turned", [P, 2, hps, 2, half])
        if qkv_bias is not None:
            bias = k.sb(name + "bias", [P, 3 * inner])
        if out_bias is not None:
            bias_o = k.sb(name + "bias_o", [P, D])
            part = k.sb(name + "part", [P, D])
        if mask_dram is not None:
            mask = k.sb(name + "mask", [P, TOK])
            mask_b = k.sb(name + "mask_b", [P, hb, TOK], BF16)
            ident_b = k.sb(name + "ident_b", [P, P], BF16)
        q_ps = k.ps(name + "q_ps", [P, 2, BANK])
        tr_ps = k.ps(name + "tr_ps", [P, 2, BANK])
        s_ps = k.ps(name + "s_ps", [P, 2, BANK])
        av_ps = k.ps(name + "av_ps", [P, 2, BANK])

        S = lambda n: k.sem(name + n)
        consts_in = S("consts_in")
        set_up, var_ready, std_ready, xs_ready = S("set_up"), S("var_ready"), S("std_ready"), S("xs_ready")
        x_lo_ready, w_hi_ready, w_lo_ready = S("x_lo_ready"), S("w_hi_ready"), S("w_lo_ready")
        q_full, qk_taken, qk_ready, v_taken = S("q_full"), S("qk_taken"), S("qk_ready"), S("v_taken")
        tr_full, tr_taken, mask_set = S("tr_full"), S("tr_taken"), S("mask_set")
        s_full, s_taken, p_ready = S("s_full"), S("s_taken"), S("p_ready")
        av_full, av_taken = S("av_full"), S("av_taken")
        n_consts = 3 * bool(rope) + (qkv_bias is not None) + (out_bias is not None) + (mask_dram is not None)
        qk_done = qk_ready if rope else qk_taken
        v_on_dve = qkv_bias is not None

        def columns(i):
            return slice(i * BANK, i * BANK + (BANK if i < qk_slices else vw))

        def tile(s, back):
            t = s - back
            return None if isinstance(s, int) and not 0 <= t < SEQS else t

        def run(eng, step, settle=lambda: None):
            for s in range(-1, UNROLL - 1):
                step(s, s)
                if s == -1:
                    settle()
            with eng.Fori(1, SEQS // UNROLL) as i:
                for j in range(UNROLL):
                    step(i * UNROLL + (j - 1), (j - 1) % UNROLL)
            for s in range(SEQS - 1, SEQS + 3):
                step(s, s)

        block = k.mem.enter_context(nc.Block())

        @block.sync
        def _(sp):
            if rope:
                sp.dma_start(cos[:], rope[0]).then_inc(consts_in, 16)
                sp.dma_start(sin[:], rope[1]).then_inc(consts_in, 16)
                sp.dma_start(nsin[:], rope[2]).then_inc(consts_in, 16)
            if qkv_bias is not None:
                sp.dma_start(bias[:], qkv_bias.to_broadcast([P, 3 * inner])).then_inc(consts_in, 16)
            if out_bias is not None:
                sp.dma_start(bias_o[:], out_bias.to_broadcast([P, D])).then_inc(consts_in, 16)
            if mask_dram is not None:
                sp.dma_start(mask[:], mask_dram).then_inc(consts_in, 16)
            if prefetch is not None:
                prefetch(sp)

        def head_batch(view, b):
            if hpc == 2:
                return view.rearrange("p (a c two) d -> p a two c d", a=2, two=2)[:, b // 2, b % 2]
            return view.rearrange("p (c j) d -> p j c d", j=4)[:, b]

        def heads_of(b):
            return [(b // 2) * 8 + b % 2 + 2 * c for c in range(hb)] if hpc == 2 else [4 * c + b for c in range(hb)]

        def place(ring, s, j, phase, i):
            return (ring_count(ring, s if isinstance(s, int) else UNROLL + j, phase, i) - 1) % 2

        def qk_view(t, j0, h0, n):
            return qk[:, j0 % 2, h0:h0 + n, 0:hd]

        @block.gpsimd
        def _(pool):
            pool.memset(vals[:, :, :, hd:hd + 1], 1.0)
            pool.memset(qk[:], 0.0).then_inc(set_up, 1)

            def settle():
                for i in range(nq):
                    pool.wait_ge(w_hi_ready, i + 1)
                    pool.tensor_tensor(w_lo[:, :, columns(i)], w_qkv[:, :, columns(i)],
                                       w_hi[:, :, columns(i)].bitcast(F32), ALU.subtract).then_inc(w_lo_ready, 1)

            def step(s, j):
                t = tile(s, 0)
                if t is not None and rope:
                    for i in range(qk_slices):
                        pool.drain()
                        after(pool, qk_taken, t * qk_slices + i + 1)
                        out = qk_view(t, j, i * hps, hps)
                        pool.tensor_tensor(out, out, turned[:, i % 2].rearrange("p h a d -> p h (a d)"),
                                           ALU.add).then_inc(qk_ready, 1)
                t = tile(s, -1)
                if t is not None:
                    after(pool, tr_taken, ring_count(TR, s, "norm", 0))
                    pool.tensor_tensor(x_lo[:], xT[:], x_hi[:].bitcast(F32), ALU.subtract).then_inc(x_lo_ready, 1)

            run(pool, step, settle)

        @block.scalar
        def _(act):
            def copy_back(s, j, phase, i, out, width):
                at_ = ring_count(TR, s, phase, i)
                after(act, tr_full, at_)
                act.activation(out, tr_ps[:, place(TR, s, j, phase, i), 0:width],
                               ACT.Copy).then_inc(tr_taken, 1)

            def deviation(n, tiles):
                act.wait_ge(var_ready, n + 1)
                act.activation(std[:, tiles], mv[:, tiles, 1], ACT.Sqrt, bias=eps[:, 0:1]).then_inc(std_ready, 1)

            def high_part(i):
                act.activation(w_hi[:, :, columns(i)], w_qkv[:, :, columns(i)], ACT.Copy).then_inc(w_hi_ready, 1)

            act.wait_ge(weights_in, weights_count)
            high_part(0)
            deviation(0, FIRST)

            def step(s, j):
                for what, i in ACT_ORDER:
                    t = tile(s, BACK[{"v": "q", "exp": "s"}.get(what, what)])
                    if t is None:
                        continue
                    if what == "v" and not v_on_dve:
                        after(act, q_full, t * nq + qk_slices + i + 1)
                        act.activation(vals[:, j % UNROLL, i * vh:(i + 1) * vh, 0:hd],
                                       q_ps[:, (qk_slices + i) % 2, 0:vw].rearrange("p (h d) -> p h d", d=hd),
                                       ACT.Copy).then_inc(v_taken, 1)
                    if what == "exp":
                        after(act, s_taken, t * nb + i + 1)
                        rows = probs[:, (j - 1) % 2, i * hb:(i + 1) * hb, :]
                        act.activation(rows, rows, ACT.Exp, scale=scale).then_inc(p_ready, 1)
                    if what == "qk":
                        flat = qkT[:].rearrange("p a c t -> p (a c t)")
                        copy_back(s, j, "qk", i, flat[:, i * BANK:(i + 1) * BANK], BANK)
                    if what == "probs":
                        copy_back(s, j, "probs", i, pT[:, i * hb:(i + 1) * hb, :].rearrange("p h t -> p (h t)"), BANK)
                    if what == "out":
                        w = min(4, no) * TOK
                        copy_back(s, j, "out", i, oT[:, 4 * i:4 * i + min(4, no), :].rearrange("p c t -> p (c t)"), w)
                    if what == "norm":
                        turned_x = tr_ps[:, place(TR, s, j, "norm", 0), 0:KD * TOK].rearrange("p (c t) -> p c t", c=KD)
                        after(act, tr_full, ring_count(TR, s, "norm", 0))
                        after(act, x_lo_ready, t)
                        act.activation(xT[:], turned_x, ACT.Copy)
                        act.activation(x_hi[:], turned_x, ACT.Copy).then_inc(tr_taken, 1)

            def settle():
                for i in range(1, nq):
                    high_part(i)
                deviation(1, OTHERS)

            run(act, step, settle)

        @block.vector
        def _(dve):

            def rotate(t, j, i):
                x = q_ps[:, i % 2, :].rearrange("p (h a d) -> p h a d", h=hps, a=2)
                out = qk_view(t, j, i * hps, hps).rearrange("p h (a d) -> p h a d", a=2)
                wide = lambda c: c[:].unsqueeze(1).to_broadcast([P, hps, half])
                both = cos[:].unsqueeze(1).unsqueeze(1).to_broadcast([P, hps, 2, half])
                after(dve, qk_ready, t * qk_slices + i + 1 - min(qk_slices, 2))
                dve.tensor_tensor(out, x, both, ALU.mult)
                dve.tensor_tensor(turned[:, i % 2, :, 0, :], x[:, :, 1, :], wide(nsin), ALU.mult)
                dve.tensor_tensor(turned[:, i % 2, :, 1, :], x[:, :, 0, :], wide(sin),
                                  ALU.mult).then_inc(qk_taken, 1)

            def statistics(tiles):
                dve.drain()
                for t in range(SEQS)[tiles]:
                    dve.bn_stats(stats[:, t, :], res[:, t, :])
                dve.drain()
                for t in range(SEQS)[tiles]:
                    last = dve.bn_aggr(mv[:, t, :], stats[:, t, :])
                last.then_inc(var_ready, 1)

            def inverse(n, tiles):
                dve.wait_ge(std_ready, n + 1)
                dve.reciprocal(rstd[:, tiles], std[:, tiles])

            def slice_qk(t, s, j, i):
                after(dve, q_full, t * nq + i + 1)
                if rope:
                    rotate(t, j, i)
                else:
                    dve.tensor_tensor(qk_view(t, j, i * hps, hps),
                                      q_ps[:, i % 2, :].rearrange("p (h d) -> p h d", d=hd),
                                      bias[:, i * BANK:(i + 1) * BANK].rearrange("p (h d) -> p h d", d=hd),
                                      ALU.add).then_inc(qk_taken, 1)

            def slice_v(t, s, j, i):
                if v_on_dve:
                    after(dve, q_full, t * nq + qk_slices + i + 1)
                    dve.tensor_tensor(
                        vals[:, j % UNROLL, i * vh:(i + 1) * vh, 0:hd],
                        q_ps[:, (qk_slices + i) % 2, 0:vw].rearrange("p (h d) -> p h d", d=hd),
                        bias[:, 2 * inner + i * vw:2 * inner + (i + 1) * vw].rearrange("p (h d) -> p h d", d=hd),
                        ALU.add).then_inc(v_taken, 1)

            def softmax_in(t, s, j, b):
                if isinstance(t, int) and t == 0:
                    dve.wait_ge(w_lo_ready, nq)
                after(dve, s_full, t * nb + b + 1)
                rows = probs[:, (j - 1) % 2, b * hb:(b + 1) * hb, :]
                sc = s_ps[:, b % 2, :].rearrange("p (h t) -> p h t", h=hb)
                dve.tensor_reduce(top[:], sc, AX_X, ALU.max)
                dve.drain()
                dve.tensor_tensor(rows, sc, top[:].unsqueeze(2).to_broadcast([P, hb, TOK]),
                                  ALU.subtract).then_inc(s_taken, 1)

            def heads_out(t, s, j, b):
                after(dve, av_full, ring_count(AV, s, "av", b))
                o = av_ps[:, place(AV, s, j, "av", b), 0:hav * (hd + 1)].rearrange("p (h e) -> p h e", h=hav)
                dve.reciprocal(rsum[:], o[:, :, hd])
                dve.drain()
                to, share = heads[:, (j - 2) % 2], rsum[:].unsqueeze(2).to_broadcast([P, hav, hd])
                if nav == nb:
                    dve.tensor_tensor(head_batch(to, b), o[:, :, 0:hd], share, ALU.mult).then_inc(av_taken, 1)
                else:
                    by_batch = lambda x: x.rearrange("p (b c) d -> p b c d", b=nb)
                    dve.tensor_tensor(to.rearrange("p (c b) d -> p b c d", b=nb), by_batch(o[:, :, 0:hd]),
                                      by_batch(share), ALU.mult).then_inc(av_taken, 1)

            def project_out(t, s, j, i):
                row = res[:, at(t), :].rearrange("p o d -> p (o d)")
                if onto is not None:
                    src = onto[:, at(t), :].rearrange("p o d -> p (o d)")
                    dve.tensor_scalar(src, row, mv[:, at(t), 0], rstd[:, at(t)], ALU.subtract, ALU.mult)
                    row = src
                o = av_ps[:, place(AV, s, j, "proj", 0), 0:D]
                after(dve, av_full, ring_count(AV, s, "proj", 0))
                if out_bias is not None:
                    dve.tensor_tensor(part[:], o, bias_o[:], ALU.add).then_inc(av_taken, 1)
                    dve.drain()
                    dve.tensor_tensor(row, row, part[:], ALU.add)
                else:
                    dve.tensor_tensor(row, row, o, ALU.add).then_inc(av_taken, 1)

            def norm_next(t, s, j, i):
                row = res[:, at(t), :].rearrange("p o d -> p (o d)")
                if not isinstance(s, int) or s >= 0:
                    after(dve, tr_full, ring_count(TR, s - 1, "norm", 0))
                dve.tensor_scalar(xs[:], row, mv[:, at(t), 0], rstd[:, at(t)],
                                  ALU.subtract, ALU.mult).then_inc(xs_ready, 1)

            WORK = {"q": (slice_qk, "q"), "v": (slice_v, "q"), "s": (softmax_in, "s"), "av": (heads_out, "av"),
                    "proj": (project_out, "proj"), "xs": (norm_next, "norm")}

            def step(s, j):
                for what, i in DVE_ORDER:
                    work, kind = WORK[what]
                    t = tile(s, BACK[kind])
                    if t is not None:
                        dve.drain()
                        work(t, s, j, i)

            def settle():
                statistics(OTHERS)
                dve.wait_ge(consts_in, 16 * n_consts)
                dve.wait_ge(set_up, 1)
                if mask_dram is not None:
                    dve.tensor_copy(mask_b[:], mask[:].unsqueeze(1).to_broadcast([P, hb, TOK]))
                    dve.tensor_copy(ident_b[:], ident[:]).then_inc(mask_set, 1)
                inverse(1, OTHERS)

            statistics(FIRST)
            inverse(0, FIRST)
            run(dve, step, settle)

        @block.tensor
        def _(pe):
            def settle():
                pe.wait_ge(set_up, 1)
                if mask_dram is not None:
                    pe.wait_ge(mask_set, 1)

            def turn(s, j, phase, i, blocks):
                at_ = ring_count(TR, s, phase, i)
                after(pe, tr_taken, at_ - 2)
                for n, blk in enumerate(blocks):
                    last = pe.transpose(tr_ps[:, place(TR, s, j, phase, i), n * TOK:(n + 1) * TOK],
                                        blk, ident[:])
                last.then_inc(tr_full, 1)

            def project(t, s, j, i):
                if i == 0:
                    after(pe, x_lo_ready, t + 1)
                if isinstance(t, int) and t == 0:
                    pe.wait_ge(w_lo_ready, i + 1)
                prev, owner = (i - 2, t) if i >= 2 else (i - 2 + nq, t - 1)
                if prev < qk_slices:
                    after(pe, qk_taken, owner * qk_slices + prev + 1)
                else:
                    after(pe, v_taken, owner * v_slices + prev - qk_slices + 1)
                width = BANK if i < qk_slices else vw
                for kc in range(KD):
                    for x, w in ((x_hi, w_hi), (x_hi, w_lo), (x_lo, w_hi)):
                        last = pe.matmul(q_ps[:, i % 2, 0:width], x[:, kc, :], w[:, kc, columns(i)],
                                         start=(kc == 0 and x is x_hi and w is w_hi), stop=(kc == KD - 1 and x is x_lo))
                last.then_inc(q_full, 1)

            def turn_qk(t, s, j, i):
                after(pe, qk_done, (t + 1) * qk_slices)
                flat = qk[:, (j - 1) % 2].rearrange("p h d -> p (h d)")
                turn(s, j, "qk", i, [flat[:, (4 * i + n) * P:(4 * i + n + 1) * P] for n in range(4)])

            def score(t, s, j, b):
                after(pe, tr_taken, ring_count(TR, s, "qk", 2 * nch // 4 - 1))
                after(pe, s_taken, t * nb + b - 1)
                masked = mask_dram is not None
                if masked:
                    pe.matmul(s_ps[:, b % 2, :], ident_b[:], mask_b[:].rearrange("p h t -> p (h t)"),
                              start=True, stop=False)
                for n, h in enumerate(heads_of(b)):
                    r = (h % hpc) * pad
                    last = pe.matmul(s_ps[:, b % 2, n * TOK:(n + 1) * TOK], qkT[r:r + hd, 0, h // hpc, :],
                                     qkT[r:r + hd, 1, h // hpc, :], start=not masked, stop=not masked or n == hb - 1)
                last.then_inc(s_full, 1)

            def turn_probs(t, s, j, b):
                after(pe, p_ready, t * nb + b + 1)
                turn(s, j, "probs", b, [probs[:, (j - 2) % 2, b * hb + n, :] for n in range(hb)])

            def weigh(t, s, j, i):
                weigh_batch(t, s, j, i if nav == nb else nb - 1, i).then_inc(av_full, 1)

            def weigh_part(t, s, j, b):
                weigh_batch(t, s, j, b, 0)

            def weigh_batch(t, s, j, b, i):
                after(pe, v_taken, (t + 1) * v_slices)
                after(pe, av_taken, ring_count(AV, s, "av", i) - 2)
                after(pe, tr_taken, ring_count(TR, s, "probs", b))
                for n, h in enumerate(heads_of(b)):
                    slot = n if nav == nb else b * hb + n
                    last = pe.matmul(av_ps[:, place(AV, s, j, "av", i), slot * (hd + 1):(slot + 1) * (hd + 1)],
                                     pT[:, b * hb + n, :], vals[:, (j - 2) % UNROLL, h, :], start=True, stop=True)
                return last

            def turn_heads(t, s, j, i):
                after(pe, av_taken, ring_count(AV, s - 1, "av", nav - 1))
                flat = heads[:, (j - 3) % 2].rearrange("p h d -> p (h d)")
                turn(s, j, "out", i, [flat[:, c * P:(c + 1) * P] for c in range(4 * i, min(4 * i + 4, no))])

            def project_out(t, s, j, i):
                after(pe, tr_taken, ring_count(TR, s, "out", -(-no // 4) - 1))
                after(pe, av_taken, ring_count(AV, s, "proj", 0) - 2)
                for c in range(no):
                    last = pe.matmul(av_ps[:, place(AV, s, j, "proj", 0), 0:D], oT[:, c, :], w_out[:, c, :],
                                     start=(c == 0), stop=(c == no - 1))
                last.then_inc(av_full, 1)

            def turn_norm(t, s, j, i):
                after(pe, xs_ready, t + 1)
                turn(s, j, "norm", 0, [xs[:, c * P:(c + 1) * P] for c in range(KD)])

            WORK = {"q": project, "qk": turn_qk, "s": score, "probs": turn_probs, "part": weigh_part, "av": weigh, "out": turn_heads,
                    "proj": project_out, "norm": turn_norm}

            def step(s, j):
                for what, i in PE_ORDER:
                    t = tile(s, BACK[what])
                    if t is not None:
                        WORK[what](t, s, j, i)

            run(pe, step, settle)


def load_expert(sp, io, name, store, e, par, biased):
    w_up, w_dn, b_up, w_in = store
    up, dn = io[name + "up"][at(e)], io[name + "dn"][at(e)]
    chunks = dn.shape[2]
    sp.dma_start(w_up[:, par], up.rearrange("e p k n -> (e p) k n")).then_inc(w_in[par], 16)
    sp.dma_start(w_dn[:, par, 0:chunks], dn.rearrange("e p k n -> (e p) k n")).then_inc(w_in[par], 16)
    if biased:
        b = io[name + "b_up"][at(e)]
        sp.dma_start(b_up[:, par], b.rearrange("e p c -> (e p) c")).then_inc(w_in[par], 16)


def experts_stage(nc, sems, io, res, ident, eps, name, n_exp, n_routed, chunks, gated, acc, store, out=None):
    k = Kit(nc, sems)
    E, R = n_exp, n_routed
    w_up, w_dn, b_up, w_in = store
    NUP = 4
    UNITS = E * GROUPS
    PEELED = 0 if gated else 1
    with k.mem:
        x_hi = k.sb(name + "x_hi", [P, KD, SEQS * TOK], F32R)
        x_lo = k.sb(name + "x_lo", [P, KD, SEQS * TOK], F32R)
        up_hi = k.sb(name + "up_hi", [P, 2, KD, NUP * P], F32R)
        up_lo = k.sb(name + "up_lo", [P, 2, KD, NUP * P], F32R)
        dn_hi = k.sb(name + "dn_hi", [P, 2, chunks, D], F32R)
        dn_lo = k.sb(name + "dn_lo", [P, 2, chunks, D], F32R)
        zero = k.sb(name + "zero", [P, 1])
        logits = k.sb(name + "logits", [R, GT])
        r_hi = k.sb(name + "r_hi", [P, KD, R], F32R)
        r_lo = k.sb(name + "r_lo", [P, KD, R], F32R)
        h = k.sb(name + "h", [P, chunks, GT])
        h_hi = k.sb(name + "h_hi", [P, 2, chunks, GT], F32R)
        h_lo = k.sb(name + "h_lo", [P, 2, chunks, GT], F32R)
        router = k.sb(name + "router", [P, KD, R])
        r_bias = k.sb(name + "r_bias", [P, R])
        stats = k.sb(name + "stats", [P, SEQS, 6])
        mv = k.sb(name + "mv", [P, SEQS, 2])
        std = k.sb(name + "std", [P, SEQS])
        rstd = k.sb(name + "rstd", [P, SEQS])
        score = k.sb(name + "score", [P, SEQS, R])
        choice = k.sb(name + "choice", [P, SEQS, R])
        rank = k.sb(name + "rank", [P, SEQS, R])
        lt = k.sb(name + "lt", [P, 4, 4] if gated else [P, R, R])
        greater = k.sb(name + "greater", [P, SEQS * 64])
        equal = k.sb(name + "equal", [P, SEQS * 64])
        total = k.sb(name + "total", [P, SEQS])
        weight = k.sb(name + "weight", [P, SEQS, E])
        if gated:
            xn = k.sb(name + "xn", [P, TPG, D])
            silu = k.sb(name + "silu", [P, chunks, GT])
            group = k.sb(name + "group", [P, SEQS, 4])
            best = k.sb(name + "best", [P, SEQS, 8])
            above = k.sb(name + "above", [P, SEQS, R])
            level = k.sb(name + "level", [P, SEQS, R])
            going = k.sb(name + "going", [P, SEQS, R])
            g_rank = k.sb(name + "g_rank", [P, SEQS, 4])
        else:
            b_dn = k.sb(name + "b_dn", [E, D])
            b_use = k.sb(name + "b_use", [P, 2, NUP])
            wT = k.sb(name + "wT", [E, SEQS * TOK])
            ln = k.sb(name + "ln", [P, 4, D])
        up_ps = k.ps(name + "up_ps", [P, 4, BANK])
        dn_ps = k.ps(name + "dn_ps", [P, 4, BANK])

        S = lambda n: k.sem(name + n)
        consts_in, first_hi_ready = S("consts_in"), S("first_hi_ready")
        var_ready, std_ready, xn_ready = S("var_ready"), S("std_ready"), S("xn_ready")
        t_full, xT_ready, x_lo_ready, r_full, r_split = (
            S("t_full"), S("xT_ready"), S("x_lo_ready"), S("r_full"), S("r_split"))
        logits_full, logits_ready = S("logits_full"), S("logits_ready")
        score_out, up_full, h_hi_ready, h_ready = S("score_out"), S("up_full"), S("h_hi_ready"), S("h_ready")
        dn_full, acc_done, w_split = S("dn_full"), S("acc_done"), [S("w_split_even"), S("w_split_odd")]
        if gated:
            silu_ready, prod_ready, stored = S("silu_ready"), S("prod_ready"), S("stored")
        else:
            x_ready, score_in, weights_ready = S("x_ready"), S("score_in"), S("weights_ready")
            wT_full, wT_ready, bias_full, bias_done = S("wT_full"), S("wT_ready"), S("bias_full"), S("bias_done")
            var2_ready, std2_ready, res_bias_added = S("var2_ready"), S("std2_ready"), S("res_bias_added")
        n_consts = 3 if gated else 8
        PER_EXPERT = 32 if gated else 48

        def run(eng, step):
            for e in range(2):
                for g in range(GROUPS):
                    step(e * GROUPS + g, e, e, g, 0)
            with eng.Fori(1, E // 2 - PEELED) as pair:
                for par in range(2):
                    for g in range(GROUPS):
                        step(pair * 2 * GROUPS + par * GROUPS + g, pair * 2 + par, par, g, pair)
            for e in range(E - 2 * PEELED, E):
                for g in range(GROUPS):
                    step(e * GROUPS + g, e, e % 2, g, e // 2)
            step(UNITS, None, 0, 0, None)

        def before(n, e, par, g):
            if isinstance(n, int) and n == 0:
                return None
            if e is None:
                return n - 1, E - 1, 1, GROUPS - 1
            return (n - 1, e, par, g - 1) if g else (n - 1, e - 1, 1 - par, GROUPS - 1)

        def biases_here(n):
            return not gated and isinstance(n, int) and n == 1

        def finished(n):
            return not gated and isinstance(n, int) and n > UNITS - GROUPS

        block = k.mem.enter_context(nc.Block())

        @block.sync
        def _(sp):
            sp.dma_start(router[:], io[name + "router"]).then_inc(consts_in, 16)
            sp.dma_start(r_bias[:], io[name + "r_bias"].to_broadcast([P, R])).then_inc(consts_in, 16)
            sp.dma_start(lt[:], io["lt%d" % lt.shape[1]]).then_inc(consts_in, 16)
            if not gated:
                sp.dma_start(b_dn[:], io[name + "b_dn"]).then_inc(consts_in, 16)
                for n, key in enumerate(("ln1_g", "ln1_b", "ln2_g", "ln2_b")):
                    sp.dma_start(ln[:, n, :], io[name + key].to_broadcast([P, D])).then_inc(consts_in, 16)
            with sp.Fori(1, E // 2) as i:
                for par in range(2):
                    sp.wait_ge(w_split[par], i)
                    load_expert(sp, io, name, store, i * 2 + par, par, not gated)
            if out is not None:
                for g in range(GROUPS):
                    sp.wait_ge(acc_done, 2 * (UNITS - GROUPS + g + 1))
                    sp.dma_start(out.rearrange("(t p) d -> p t d", p=P)[:, g * TPG:(g + 1) * TPG, :],
                                 acc[:, g * TPG:(g + 1) * TPG, :]).then_inc(stored, 16)
                sp.wait_ge(stored, 16 * GROUPS)

        def scaled(n):
            return ln[:, n:n + 1, :].to_broadcast([P, TPG, D])

        @block.gpsimd
        def _(pool):
            def split_low(par):
                pool.tensor_tensor(up_lo[:, par], w_up[:, par], up_hi[:, par].bitcast(F32), ALU.subtract)
                pool.tensor_tensor(dn_lo[:, par], w_dn[:, par, 0:chunks], dn_hi[:, par].bitcast(F32),
                                   ALU.subtract).then_inc(w_split[par], 1)

            def split(e, par):
                pair = 0 if isinstance(e, int) else e - par
                pool.drain()
                pool.wait_ge(w_in[par], pair * (PER_EXPERT // 2) + PER_EXPERT)
                after(pool, dn_full, (e - 1) * 2 * GROUPS)
                pool.tensor_tensor(up_hi[:, par], w_up[:, par], zero[:].unsqueeze(1).to_broadcast([P, KD, NUP * P]),
                                   ALU.add)
                pool.tensor_copy(dn_hi[:, par], w_dn[:, par, 0:chunks])
                if not gated:
                    pool.tensor_copy(b_use[:, par], b_up[:, par])
                pool.drain()
                split_low(par)

            pool.memset(zero[:], 0.0)
            pool.wait_ge(first_hi_ready, 1)
            if not gated:
                pool.tensor_copy(b_use[:, 0], b_up[:, 0])
            split_low(0)
            if not gated:
                pool.wait_ge(consts_in, 16 * n_consts)
                for g in range(GROUPS):
                    rows = acc[:, g * TPG:(g + 1) * TPG, :]
                    pool.wait_ge(xn_ready, g + 1)
                    pool.tensor_tensor(rows, rows, scaled(0), ALU.mult)
                    pool.drain()
                    pool.tensor_tensor(rows, rows, scaled(1), ALU.add).then_inc(x_ready, 1)
            split(1, 1)
            if not gated:
                for g in range(GROUPS):
                    rows = res[:, g * TPG:(g + 1) * TPG, :]
                    last = pool.tensor_tensor(rows, rows, scaled(3), ALU.add)
                last.then_inc(res_bias_added, 1)
            with pool.Fori(1, E // 2) as i:
                for par in range(2):
                    split(i * 2 + par, par)

        @block.scalar
        def _(act):
            act.wait_ge(w_in[0], PER_EXPERT)
            act.activation(up_hi[:, 0], w_up[:, 0], ACT.Copy)
            act.activation(dn_hi[:, 0], w_dn[:, 0, 0:chunks], ACT.Copy).then_inc(first_hi_ready, 1)

            def deviation(g, var, ready):
                tiles = slice(g * TPG, (g + 1) * TPG)
                act.wait_ge(var, g + 1)
                act.activation(std[:, tiles], mv[:, tiles, 1], ACT.Sqrt, bias=eps[:, 0:1]).then_inc(ready, 1)

            def copy_logits(g):
                act.wait_ge(logits_full, g + 1)
                act.activation(logits[:], up_ps[0:R, 2, :], ACT.Copy).then_inc(logits_ready, 1)

            deviation(0, var_ready, std_ready)
            for g in range(GROUPS):
                if g + 1 < GROUPS:
                    deviation(g + 1, var_ready, std_ready)
                for kc in range(KD):
                    act.wait_ge(t_full, g * KD + kc + 1)
                    act.activation(x_hi[:, kc, g * GT:(g + 1) * GT], up_ps[:, kc, :], ACT.Copy).then_inc(xT_ready, 1)
                if g:
                    copy_logits(g - 1)
            copy_logits(GROUPS - 1)
            if gated:
                act.wait_ge(r_full, 1)
                act.activation(score[:], up_ps[:, 3, 0:SEQS * R].rearrange("p (t r) -> p t r", r=R),
                               ACT.Sigmoid).then_inc(score_out, 1)
            else:
                act.wait_ge(score_in, 1)
                act.activation(score[:], score[:], ACT.Exp).then_inc(score_out, 1)

            def step(n, e, par, g, pair):
                if e is not None:
                    hidden(n, par, g)
                if finished(n):
                    deviation((n - UNITS - 1) % GROUPS, var2_ready, std2_ready)

            def hidden(n, par, g):
                for f in range(chunks):
                    if gated:
                        after(act, up_full, n * 4 + 2 * f + 1)
                        after(act, prod_ready, (n - 1) * chunks + f + 1)
                        act.activation(silu[:, f, :], up_ps[:, 2 * f, :], ACT.Silu).then_inc(silu_ready, 1)
                    else:
                        after(act, up_full, n * 4 + f + 1)
                        after(act, h_ready, (n - 1) * chunks + f + 1)
                        act.activation(h[:, f, :], up_ps[:, f, :], ACT.Relu, bias=b_use[:, par, f:f + 1])
                        act.activation(h_hi[:, g % 2, f, :], up_ps[:, f, :], ACT.Relu,
                                       bias=b_use[:, par, f:f + 1]).then_inc(h_hi_ready, 1)
                if gated:
                    for f in range(chunks):
                        after(act, prod_ready, n * chunks + f + 1)
                        act.activation(h_hi[:, g % 2, f, :], h[:, f, :], ACT.Copy).then_inc(h_hi_ready, 1)
                if biases_here(n):
                    for b in range(GROUPS):
                        act.wait_ge(wT_full, b + 1)
                        act.activation(wT[:, b * GT:(b + 1) * GT], dn_ps[0:E, b, :], ACT.Copy).then_inc(wT_ready, 1)

            run(act, step)

        @block.vector
        def _(dve):
            def statistics(tiles, ready):
                dve.drain()
                for t in tiles:
                    dve.bn_stats(stats[:, t, :], acc[:, t, :])
                dve.drain()
                for t in tiles:
                    last = dve.bn_aggr(mv[:, t, :], stats[:, t, :])
                last.then_inc(ready, 1)

            def group_tiles(g):
                return range(g * TPG, (g + 1) * TPG)

            def norm(g):
                of = slice(g * TPG, (g + 1) * TPG)
                dve.wait_ge(std_ready, g + 1)
                dve.reciprocal(rstd[:, of], std[:, of])
                dve.drain()
                if gated:
                    after(dve, t_full, g * KD)
                for t in group_tiles(g):
                    last = dve.tensor_scalar(xn[:, t % TPG, :] if gated else acc[:, t, :], acc[:, t, :], mv[:, t, 0:1],
                                             rstd[:, t:t + 1], ALU.subtract, ALU.mult)
                last.then_inc(xn_ready, 1)

            def ranks(values, out_rank, tri, groups, n):
                shape = [P, groups, n, n]
                g4 = greater[:, 0:groups * n * n].rearrange("p (g e j) -> p g e j", e=n, j=n)
                e4 = equal[:, 0:groups * n * n].rearrange("p (g e j) -> p g e j", e=n, j=n)
                other = values.unsqueeze(2).to_broadcast(shape)
                own = values.unsqueeze(3).to_broadcast(shape)
                dve.drain()
                dve.tensor_tensor(g4, other, own, ALU.is_gt)
                dve.tensor_tensor(e4, other, own, ALU.is_equal)
                dve.drain()
                dve.tensor_tensor(e4, e4, tri[:].unsqueeze(1).to_broadcast(shape), ALU.mult)
                dve.drain()
                dve.tensor_tensor(g4, g4, e4, ALU.add)
                dve.drain()
                dve.tensor_reduce(out_rank, g4, AX_X, ALU.add)
                dve.drain()

            def wide(t, n):
                return t.unsqueeze(2).to_broadcast([P, SEQS, n])

            def low_part(g):
                for kc in range(KD):
                    there = slice(g * GT, (g + 1) * GT)
                    dve.wait_ge(xT_ready, g * KD + kc + 1)
                    dve.tensor_tensor(x_lo[:, kc, there], up_ps[:, kc, :], x_hi[:, kc, there].bitcast(F32),
                                      ALU.subtract).then_inc(x_lo_ready, 1)

            def hidden(n, g):
                if gated:
                    dve.drain()
                    for f in range(chunks):
                        after(dve, up_full, n * 4 + 2 * f + 2)
                        after(dve, silu_ready, n * chunks + f + 1)
                        dve.tensor_tensor(h[:, f, :], silu[:, f, :], up_ps[:, 2 * f + 1, :],
                                          ALU.mult).then_inc(prod_ready, 1)
                for f in range(chunks):
                    after(dve, h_hi_ready, n * chunks + f + 1)
                    dve.tensor_tensor(h_lo[:, g % 2, f, :], h[:, f, :], h_hi[:, g % 2, f, :].bitcast(F32),
                                      ALU.subtract).then_inc(h_ready, 1)

            statistics(group_tiles(0), var_ready)
            for g in range(GROUPS):
                if g + 1 < GROUPS:
                    statistics(group_tiles(g + 1), var_ready)
                norm(g)
                if g == 0:
                    dve.wait_ge(consts_in, 16 * n_consts)
                    dve.tensor_copy(r_hi[:], router[:])
                    dve.drain()
                    dve.tensor_tensor(r_lo[:], router[:], r_hi[:].bitcast(F32), ALU.subtract).then_inc(r_split, 1)
                else:
                    low_part(g - 1)
            low_part(GROUPS - 1)
            dve.drain()
            if gated:
                dve.memset(weight[:, :, R:E], 1.0)
                dve.memset(going[:], 1.0)
                dve.drain()
                dve.memset(going[:, :, 0:1], 0.0)
                dve.wait_ge(score_out, 1)
                dve.tensor_tensor(choice[:], score[:], r_bias[:].unsqueeze(1).to_broadcast([P, SEQS, R]), ALU.add)
                quads = choice[:].rearrange("p t (g e) -> p (t g) e", e=4)
                q_rank = rank[:].rearrange("p t (g e) -> p (t g) e", e=4)
                ranks(quads, q_rank, lt, SEQS * 4, 4)
                hidden(0, 0)
                dve.scalar_tensor_tensor(rank[:], rank[:], 2.0, choice[:], ALU.is_lt, ALU.mult)
                dve.drain()
                dve.tensor_reduce(group[:].rearrange("p t g -> p (t g)"), q_rank, AX_X, ALU.add)
                ranks(group[:], g_rank[:], lt, SEQS, 4)
                dve.tensor_scalar(group[:], g_rank[:], 2.0, None, ALU.is_lt)
                dve.drain()
                dve.tensor_scalar(g_rank[:], group[:], -1.0, None, ALU.add)
                keep = lambda t: t[:].rearrange("p t g -> p (t g)").unsqueeze(2).to_broadcast([P, SEQS * 4, 4])
                dve.tensor_tensor(quads, quads, keep(group), ALU.mult)
                dve.drain()
                dve.tensor_tensor(quads, quads, keep(g_rank), ALU.add)
                dve.drain()
                for t in range(SEQS):
                    dve.max(best[:, t, :], choice[:, t, :])
                dve.drain()
                fourth = best[:, :, 3].unsqueeze(2).to_broadcast([P, SEQS, R])
                hidden(1, 1)
                dve.tensor_tensor(above[:], choice[:], fourth, ALU.is_gt)
                dve.tensor_tensor(level[:], choice[:], fourth, ALU.is_equal)
                dve.drain()
                dve.tensor_reduce(total[:], above[:], AX_X, ALU.add)
                flat = lambda x: x[:].rearrange("p t r -> p (t r)")
                dve.tensor_tensor_scan(flat(rank), flat(going), flat(level), 0.0, ALU.mult, ALU.add)
                dve.drain()
                dve.tensor_tensor(rank[:], rank[:], wide(total[:], R), ALU.add)
                dve.drain()
                dve.scalar_tensor_tensor(level[:], rank[:], 4.5, level[:], ALU.is_lt, ALU.mult)
                dve.drain()
                dve.tensor_tensor(above[:], above[:], level[:], ALU.add)
                dve.drain()
                dve.tensor_tensor(choice[:], above[:], score[:], ALU.mult)
                dve.drain()
                dve.tensor_reduce(total[:], choice[:], AX_X, ALU.add)
                dve.drain()
                dve.tensor_scalar(total[:], total[:], 1e-20, None, ALU.add)
                dve.drain()
                dve.reciprocal(total[:], total[:])
                dve.drain()
                dve.scalar_tensor_tensor(weight[:, :, 0:R], choice[:], 2.5, wide(total[:], R), ALU.mult, ALU.mult)
            else:
                dve.wait_ge(r_full, 1)
                dve.tensor_tensor(score[:], up_ps[:, 3, 0:SEQS * R].rearrange("p (t r) -> p t r", r=R),
                                  r_bias[:].unsqueeze(1).to_broadcast([P, SEQS, R]), ALU.add)
                dve.drain()
                dve.tensor_reduce(total[:], score[:], AX_X, ALU.max)
                dve.drain()
                dve.tensor_tensor(score[:], score[:], wide(total[:], R), ALU.subtract).then_inc(score_in, 1)
                dve.wait_ge(score_out, 1)
                dve.tensor_reduce(total[:], score[:], AX_X, ALU.add)
                dve.drain()
                dve.reciprocal(total[:], total[:])
                dve.drain()
                dve.tensor_tensor(score[:], score[:], wide(total[:], R), ALU.mult)
                ranks(score[:], rank[:], lt, SEQS, R)
                dve.scalar_tensor_tensor(weight[:], rank[:], 2.0, score[:], ALU.is_lt,
                                         ALU.mult).then_inc(weights_ready, 1)

            def last_norm(g):
                of = slice(g * TPG, (g + 1) * TPG)
                dve.drain()
                for t in group_tiles(g):
                    dve.scalar_tensor_tensor(acc[:, t, :], acc[:, t, :], mv[:, t, 0:1], ln[:, 2, :],
                                             ALU.subtract, ALU.mult)
                dve.wait_ge(std2_ready, g + 1)
                dve.reciprocal(rstd[:, of], std[:, of])
                dve.drain()
                dve.wait_ge(res_bias_added, 1)
                for t in group_tiles(g):
                    dve.scalar_tensor_tensor(res[:, t, :], acc[:, t, :], rstd[:, t:t + 1], res[:, t, :],
                                             ALU.mult, ALU.add)

            def step(n, e, par, g, pair):
                if e is not None and not (gated and isinstance(n, int) and n < 2):
                    hidden(n, g)
                if biases_here(n):
                    for b in range(SEQS // 2):
                        dve.wait_ge(bias_full, b + 1)
                        rows = acc[:, 2 * b:2 * b + 2, :]
                        dve.tensor_tensor(rows, rows, dn_ps[:, b % 4, :].rearrange("p (j d) -> p j d", j=2),
                                          ALU.add).then_inc(bias_done, 1)
                prev = before(n, e, par, g)
                if prev:
                    m, pe_, ppar, pg = prev
                    dve.drain()
                    for b in range(2):
                        after(dve, dn_full, m * 2 + b + 1)
                        for j in range(2):
                            t = pg * TPG + 2 * b + j
                            last = dve.scalar_tensor_tensor(
                                acc[:, t, :], dn_ps[:, 2 * (pg % 2) + b, j * D:(j + 1) * D], weight[:, t, at(pe_)],
                                acc[:, t, :], ALU.mult, ALU.add)
                        last.then_inc(acc_done, 1)
                    if finished(n):
                        statistics(group_tiles(pg), var2_ready)
                        if n > UNITS - GROUPS + 1:
                            last_norm(pg - 1)
                    if isinstance(n, int) and n == UNITS and not gated:
                        last_norm(pg)

            run(dve, step)

        @block.tensor
        def _(pe):
            def product(out, n, still, moving):
                for c in range(n):
                    for a, b in ((0, 0), (0, 1), (1, 0)):
                        last = pe.matmul(out, still(c, a), moving(c, b), start=(c == 0 and a + b == 0),
                                         stop=(c == n - 1 and a == 1))
                return last

            def route(g):
                pe.wait_ge(x_lo_ready, (g + 1) * KD)
                pe.wait_ge(r_split, 1)
                if g:
                    turn_logits(g - 1)
                there = slice(g * GT, (g + 1) * GT)
                product(up_ps[0:R, 2, :], KD, lambda kc, r: (r_hi, r_lo)[r][:, kc, :],
                        lambda kc, x: (x_hi, x_lo)[x][:, kc, there]).then_inc(logits_full, 1)

            def turn_logits(g):
                pe.wait_ge(logits_ready, g + 1)
                for t in range(g * TPG, (g + 1) * TPG):
                    last = pe.transpose(up_ps[:, 3, t * R:(t + 1) * R], logits[:, t % TPG * TOK:(t % TPG + 1) * TOK],
                                        ident[0:R, 0:R])
                return last

            for g in range(GROUPS):
                pe.wait_ge(xn_ready if gated else x_ready, g + 1)
                for kc in range(KD):
                    after(pe, x_lo_ready, (g - 1) * KD + kc + 1)
                    for j in range(TPG):
                        src = xn[:, j, kc * P:(kc + 1) * P] if gated else acc[:, g * TPG + j, kc * P:(kc + 1) * P]
                        last = pe.transpose(up_ps[:, kc, j * TOK:(j + 1) * TOK], src, ident[:])
                    last.then_inc(t_full, 1)
                if g:
                    route(g - 1)
            route(GROUPS - 1)
            last = turn_logits(GROUPS - 1)
            last.then_inc(r_full, 1)

            def step(n, e, par, g, pair):
                if e is not None:
                    pe.wait_ge(w_split[par], pair + 1)
                    for c in range(NUP):
                        if c == 3 and isinstance(n, int) and n == 0:
                            pe.wait_ge(score_out if gated else score_in, 1)
                        if gated:
                            after(pe, prod_ready if c % 2 else silu_ready, (n - 1) * chunks + c // 2 + 1)
                        else:
                            after(pe, h_hi_ready, (n - 1) * chunks + c + 1)
                        product(up_ps[:, c, :], KD, lambda kc, w: (up_hi, up_lo)[w][:, par, kc, c * P:(c + 1) * P],
                                lambda kc, x: (x_hi, x_lo)[x][:, kc, g * GT:(g + 1) * GT]).then_inc(up_full, 1)
                if biases_here(n):
                    pe.wait_ge(weights_ready, 1)
                    for t in range(SEQS):
                        last = pe.transpose(dn_ps[0:E, t // TPG, t % TPG * TOK:(t % TPG + 1) * TOK], weight[:, t, :],
                                            ident[:])
                        if t % TPG == TPG - 1:
                            last.then_inc(wT_full, 1)
                    pe.wait_ge(consts_in, 16 * n_consts)
                    pe.wait_ge(wT_ready, GROUPS)
                    for b in range(SEQS // 2):
                        after(pe, bias_done, b - 3)
                        for t in (2 * b, 2 * b + 1):
                            last = pe.matmul(dn_ps[:, b % 4, t % 2 * D:(t % 2 + 1) * D], wT[:, t * TOK:(t + 1) * TOK],
                                             b_dn[:], start=True, stop=True)
                        last.then_inc(bias_full, 1)
                    pe.wait_ge(bias_done, SEQS // 2)
                prev = before(n, e, par, g)
                if prev:
                    m, pe_, ppar, pg = prev
                    after(pe, h_ready, m * chunks + chunks)
                    for b in range(2):
                        after(pe, acc_done, (m - 2) * 2 + b + 1)
                        for j in range(2):
                            t = 2 * b + j
                            last = product(dn_ps[:, 2 * (pg % 2) + b, j * D:(j + 1) * D], chunks,
                                           lambda f, x: (h_hi, h_lo)[x][:, pg % 2, f, t * TOK:(t + 1) * TOK],
                                           lambda f, w: (dn_hi, dn_lo)[w][:, ppar, f, :])
                        last.then_inc(dn_full, 1)

            run(pe, step)


def build(nc, io, out):
    with ExitStack() as sems:
        res = sems.enter_context(nc.sbuf_tensor("res", [P, SEQS, D], F32))
        ident = sems.enter_context(nc.sbuf_tensor("ident", [P, P], F32))
        eps = sems.enter_context(nc.sbuf_tensor("eps", [P, 1], F32))
        ident_in = sems.enter_context(nc.semaphore("ident_in"))
        eps_set = sems.enter_context(nc.semaphore("eps_set"))
        with nc.Block() as block:
            @block.sync
            def _(sp):
                sp.dma_start(ident[:], io["ident"]).then_inc(ident_in, 16)
                sp.wait_ge(ident_in, 16)

            @block.vector
            def _(dve):
                dve.memset(eps[:], EPS).then_inc(eps_set, 1)
                dve.wait_ge(eps_set, 1)

        heads_dim = {"f0_": 16, "a1_": 16, "a0_": 64}
        w, first = {}, ExitStack()
        for name, hd in heads_dim.items():
            keep = first if name == "a0_" else sems
            w[name] = (keep.enter_context(nc.sbuf_tensor(name + "w_qkv", [P, KD, 3 * HEADS * hd], F32)),
                       keep.enter_context(nc.sbuf_tensor(name + "w_out", [P, HEADS * hd // P, D], F32)),
                       sems.enter_context(nc.semaphore(name + "weights_in")), 32)

        def load_attention(sp):
            for name in heads_dim:
                sp.dma_start(w[name][0][:], io[name + "w_qkv"]).then_inc(w[name][2], 16)
                sp.dma_start(w[name][1][:], io[name + "w_out"]).then_inc(w[name][2], 16)

        def first_experts(name, biased):
            def load(sp):
                for e in range(2):
                    load_expert(sp, io, name, store[name], e, e, biased)
            return load

        token_stage(nc, sems, io, res, ident, eps, load_attention)
        attention_stage(nc, sems, io, res, ident, eps, "a0_", 64, *w["a0_"],
                        rope=(io["cos64"], io["sin64"], io["nsin64"]), out_bias=io["a0_b_out"])
        first.close()
        w_up = sems.enter_context(nc.sbuf_tensor("w_up", [P, 2, KD, 4 * P], F32))
        w_dn = sems.enter_context(nc.sbuf_tensor("w_dn", [P, 2, 4, D], F32))
        b_up = sems.enter_context(nc.sbuf_tensor("b_up", [P, 2, 4], F32))
        store = {n: (w_up, w_dn, b_up, [sems.enter_context(nc.semaphore(n + "w_in_even")),
                                        sems.enter_context(nc.semaphore(n + "w_in_odd"))]) for n in ("m0_", "m1_")}
        with nc.sbuf_tensor("mixed", [P, SEQS, D], F32) as mixed:
            attention_stage(nc, sems, io, res, ident, eps, "f0_", 16, *w["f0_"],
                            qkv_bias=io["f0_b_qkv"], out_bias=io["f0_b_out"], onto=mixed,
                            prefetch=first_experts("m0_", True))
            experts_stage(nc, sems, io, res, ident, eps, "m0_", 8, 8, 4, False, mixed, store["m0_"])
        attention_stage(nc, sems, io, res, ident, eps, "a1_", 16, *w["a1_"],
                        rope=(io["cos16"], io["sin16"], io["nsin16"]), mask_dram=io["mask"],
                        prefetch=first_experts("m1_", False))
        experts_stage(nc, sems, io, res, ident, eps, "m1_", 18, 16, 2, True, res, store["m1_"], out=out)


def kernel(**inputs):
    import numpy as np
    import concourse.bacc as bacc
    from concourse.bass_utils import run_bass_kernel_spmd

    a = {n: np.asarray(v) for n, v in inputs.items()}

    def rows(w):
        *lead, kk, n = w.shape
        return np.moveaxis(w.reshape(*lead, kk // P, P, n), -3, -2)

    def cols(v):
        *lead, kk = v.shape
        return np.moveaxis(v.reshape(*lead, kk // P, P), -1, 0)

    def rope(n, half):
        theta = (np.float32(1.0) / np.float32(10000.0) ** (np.arange(half, dtype=np.float32) / np.float32(half)))
        angle = np.arange(n, dtype=np.float32)[:, None] * theta.astype(np.float32)[None, :]
        return np.cos(angle).astype(np.float32), np.sin(angle).astype(np.float32)

    def lower(n):
        return np.broadcast_to(np.tril(np.ones((n, n), np.float32), -1), (P, n, n))

    t = {"ids": a["x"].T, "emb": a["L0_tok_tok_emb"], "pos": a["L0_tok_pos_emb"][:TOK]}
    t["w_in"] = rows(a["L0_tok_W_in"].transpose(0, 2, 1))
    t["w_b"] = rows(a["L0_tok_W_B"].transpose(0, 2, 1))
    t["w_c"] = a["L0_tok_W_C"].transpose(0, 2, 1)
    t["w_o"] = rows(a["L0_tok_W_out"].transpose(0, 2, 1))
    t["conv_w"] = np.moveaxis(a["L0_tok_conv_w"][:, :, 0, :].reshape(LAYERS, KI, P, TAPS), 2, 0)
    t["conv_b"] = cols(a["L0_tok_conv_b"])
    t["d_vec"] = cols(a["L0_tok_D_vec"])
    t["tok_ln_g"], t["tok_ln_b"] = a["L0_tok_ln_g"], a["L0_tok_ln_b"]
    decay = np.full((STATE, GT), DECAY, np.float32)
    decay[:, ::TOK] = 0.0
    t["decay"] = decay
    t["ident"] = np.eye(P, dtype=np.float32)
    t["cos64"], t["sin64"] = rope(TOK, 32)
    t["cos16"], t["sin16"] = rope(TOK, 8)
    t["nsin64"], t["nsin16"] = -t["sin64"], -t["sin16"]
    i = np.arange(TOK)
    seen = (i[:, None] // 64 == i[None, :] // 64) & (i[None, :] <= i[:, None])
    t["mask"] = np.where(seen, np.float32(0), np.float32(-3e38)).astype(np.float32)
    for n in (4, 8):
        t["lt%d" % n] = lower(n)
    t["a0_w_qkv"] = rows(a["L0_attn_w_qkv"])
    t["a0_w_out"] = rows(a["L0_attn_w_out"])
    t["a0_b_out"] = a["L0_attn_b_out"][None]
    t["f0_w_qkv"] = rows(np.concatenate([a["L0_ffn_Wq"], a["L0_ffn_Wk"], a["L0_ffn_Wv"]], 1))
    t["f0_b_qkv"] = np.concatenate([a["L0_ffn_bq"], a["L0_ffn_bk"], a["L0_ffn_bv"]])[None]
    t["f0_w_out"] = rows(a["L0_ffn_Wo"])
    t["f0_b_out"] = a["L0_ffn_bo"][None]
    t["m0_router"] = rows(a["L0_ffn_gW"])
    t["m0_r_bias"] = a["L0_ffn_gb"][None]
    t["m0_up"] = rows(a["L0_ffn_W1"])
    t["m0_b_up"] = a["L0_ffn_b1"].reshape(8, 4, P).transpose(0, 2, 1)
    t["m0_dn"] = rows(a["L0_ffn_W2"])
    t["m0_b_dn"] = a["L0_ffn_b2"]
    for n in ("ln1_g", "ln1_b", "ln2_g", "ln2_b"):
        t["m0_" + n] = a["L0_ffn_" + n][None]
    w = a["L1_attn_Wqkv"].reshape(3, HEADS, 8, 2, D)
    q_k = w[:2].transpose(0, 1, 3, 2, 4).reshape(2 * D, D)
    t["a1_w_qkv"] = rows(np.concatenate([q_k, a["L1_attn_Wqkv"][2 * D:]]).T)
    t["a1_w_out"] = rows(a["L1_attn_Wout"].T)
    t["m1_router"] = rows(a["L1_ffn_router_w"].T)
    t["m1_r_bias"] = a["L1_ffn_bias"][None]

    def experts(routed, shared):
        return np.concatenate([routed, shared.reshape(D, 2, D).transpose(1, 0, 2)])

    gate = experts(a["L1_ffn_gate_w"], a["L1_ffn_sh_gate_w"]).reshape(18, D, 2, P)
    up = experts(a["L1_ffn_up_w"], a["L1_ffn_sh_up_w"]).reshape(18, D, 2, P)
    t["m1_up"] = rows(np.stack([gate, up], 3).reshape(18, D, 4 * P))
    t["m1_dn"] = rows(np.concatenate([a["L1_ffn_down_w"], a["L1_ffn_sh_down_w"].reshape(2, D, D)]))

    nc = bacc.Bacc("TRN2", target_bir_lowering=False, num_devices=1)
    arrays, io = {}, {}
    for n, v in t.items():
        arrays["in_" + n] = np.ascontiguousarray(v)
        io[n] = nc.dram_tensor("in_" + n, v.shape, mybir.dt.from_np(v.dtype), kind="ExternalInput").ap()
    out = nc.dram_tensor("out_0", (SEQS * TOK, D), F32, kind="ExternalOutput").ap()
    build(nc, io, out)
    r = run_bass_kernel_spmd(nc, [arrays], core_ids=[0])
    return r.results[0]["out_0"].reshape(SEQS, TOK, D)
```
